# Optimizing a Trainium2 kernel written in Bass

```python
import numpy as np
import jax
import jax.numpy as jnp

def _softmax(x, axis=-1):
    return jax.nn.softmax(x, axis=axis)

def _gelu(x):
    return jax.nn.gelu(x, approximate=True)

def _silu(x):
    return jax.nn.silu(x)

def _sigmoid(x):
    return jax.nn.sigmoid(x)

def _layernorm(x, axis=-1, eps=1e-05):
    m = jnp.mean(x, axis=axis, keepdims=True)
    v = jnp.var(x, axis=axis, keepdims=True)
    return (x - m) / jnp.sqrt(v + eps)

def _scatter_add(tgt, idx, src, axis=0):
    return tgt.at[idx].add(src)

def _segment_sum(src, seg, n):
    return jax.ops.segment_sum(src, seg, n)
kernel_name = 'mk_xattn_ffn_d1_seqx_r8_9e0a65'

def setup_inputs(seed: int=0):
    np.random.seed(seed)
    _w = jnp.asarray

    def _rec_inputs():
        import jax
        import jax.numpy as jnp
        _rk = jax.random.key(seed)
        x = 7.22e-05 + 1 * jax.random.normal(jax.random.fold_in(_rk, 1), (32, 56, 256), jnp.float32)
        _lenS = 56 - jax.random.randint(jax.random.fold_in(_rk, 7), (32,), 0, max(1, 56 // 4) + 1, jnp.int32)
        _lenS2 = 1500 - jax.random.randint(jax.random.fold_in(_rk, 8), (32,), 0, max(1, 1500 // 4) + 1, jnp.int32)
        _ctx_1024P = jax.random.normal(jax.random.fold_in(_rk, 11), (32, 16, 128), jnp.float32)
        _ctx_1024c = jax.random.dirichlet(jax.random.fold_in(_rk, 511), 0.3 * jnp.ones((16,), jnp.float32), (32, 1500))
        _ctx_1024t = jnp.einsum('bsk,bkd->bsd', _ctx_1024c, _ctx_1024P)
        _ctx_1024t = _ctx_1024t * jax.lax.rsqrt(jnp.mean(jnp.square(_ctx_1024t)) + 1e-12) * 0.953939
        ctx_1024 = -0.000673644 + 1.00013 * (_ctx_1024t + 0.3 * jax.random.normal(jax.random.fold_in(_rk, 611), (32, 1500, 128), jnp.float32))
        return (x, ctx_1024)
    x, ctx_1024 = _rec_inputs()

    def _L0_xattn_setup():
        import jax, jax.numpy as jnp
        import numpy as np
        B, S1, S2, DCA = (2, 256, 128, 16)
        QDIM, KDIM, H = (256, 128, 16)
        HD = QDIM // H
        SCALE = HD ** (-0.5)
        EPS = 1e-06
        DCA_WEIGHT = 1.0

        def _ln(t, w, b):
            m = jnp.mean(t, axis=-1, keepdims=True)
            v = jnp.var(t, axis=-1, keepdims=True)
            return (t - m) * jax.lax.rsqrt(v + EPS) * w + b

        def _attn(q, k, v):
            s = jnp.einsum('bhqd,bhkd->bhqk', q, k) * SCALE
            p = jax.nn.softmax(s, axis=-1)
            return jnp.einsum('bhqk,bhkd->bhqd', p, v)
        key = jax.random.key(seed)
        ks = jax.random.split(key, 8)
        w = lambda k, shape: jax.random.normal(k, shape, jnp.float32) * 0.02
        return {'x': jax.random.normal(ks[0], (B, S1, QDIM), jnp.float32), 'y': jax.random.normal(ks[1], (B, S2 + DCA, KDIM), jnp.float32), 'Wq': w(ks[2], (QDIM, QDIM)), 'bq': jnp.zeros((QDIM,), jnp.float32), 'Wk': w(ks[3], (KDIM, QDIM)), 'bk': jnp.zeros((QDIM,), jnp.float32), 'Wv': w(ks[4], (KDIM, QDIM)), 'bv': jnp.zeros((QDIM,), jnp.float32), 'Wkv_dca': w(ks[5], (KDIM, 2 * QDIM)), 'bkv_dca': jnp.zeros((2 * QDIM,), jnp.float32), 'qn_w': jnp.ones((HD,), jnp.float32), 'qn_b': jnp.zeros((HD,), jnp.float32), 'kn_w': jnp.ones((HD,), jnp.float32), 'kn_b': jnp.zeros((HD,), jnp.float32), 'kn_dca_w': jnp.ones((HD,), jnp.float32), 'kn_dca_b': jnp.zeros((HD,), jnp.float32), 'Wo': w(ks[6], (QDIM, QDIM)), 'bo': jnp.zeros((QDIM,), jnp.float32)}
    _L0_xattn_all = _L0_xattn_setup()
    _L0_xattn_in = {k: v for k, v in _L0_xattn_all.items() if k in ('Wq', 'bq', 'Wk', 'bk', 'Wv', 'bv', 'Wkv_dca', 'bkv_dca', 'qn_w', 'qn_b', 'kn_w', 'kn_b', 'kn_dca_w', 'kn_dca_b', 'Wo', 'bo')}
    del _L0_xattn_all

    def _L0_ffn_setup():
        import jax, jax.numpy as jnp
        import numpy as np
        B, S, H = (1, 128, 256)
        E, K = (32, 4)
        F, FS = (176, 704)
        CAP = 32

        def silu(x):
            return x * jax.nn.sigmoid(x)
        key = jax.random.key(seed)
        ks = jax.random.split(key, 9)
        sc = 0.02
        return {'hidden_states': jax.random.normal(ks[0], (B, S, H), jnp.float32), 'Wr': jax.random.normal(ks[1], (H, E), jnp.float32) * sc, 'Wg': jax.random.normal(ks[2], (E, H, F), jnp.float32) * sc, 'Wu': jax.random.normal(ks[3], (E, H, F), jnp.float32) * sc, 'Wd': jax.random.normal(ks[4], (E, F, H), jnp.float32) * sc, 'Wsg': jax.random.normal(ks[5], (H, FS), jnp.float32) * sc, 'Wsu': jax.random.normal(ks[6], (H, FS), jnp.float32) * sc, 'Wsd': jax.random.normal(ks[7], (FS, H), jnp.float32) * sc, 'Wse': jax.random.normal(ks[8], (H, 1), jnp.float32) * sc}
    _L0_ffn_all = _L0_ffn_setup()
    _L0_ffn_in = {k: v for k, v in _L0_ffn_all.items() if k in ('Wr', 'Wg', 'Wu', 'Wd', 'Wsg', 'Wsu', 'Wsd', 'Wse')}
    del _L0_ffn_all
    return {'x': x, 'ctx_1024': ctx_1024, 'L0_xattn_Wq': _L0_xattn_in['Wq'], 'L0_xattn_bq': _L0_xattn_in['bq'], 'L0_xattn_Wk': _L0_xattn_in['Wk'], 'L0_xattn_bk': _L0_xattn_in['bk'], 'L0_xattn_Wv': _L0_xattn_in['Wv'], 'L0_xattn_bv': _L0_xattn_in['bv'], 'L0_xattn_Wkv_dca': _L0_xattn_in['Wkv_dca'], 'L0_xattn_bkv_dca': _L0_xattn_in['bkv_dca'], 'L0_xattn_qn_w': _L0_xattn_in['qn_w'], 'L0_xattn_qn_b': _L0_xattn_in['qn_b'], 'L0_xattn_kn_w': _L0_xattn_in['kn_w'], 'L0_xattn_kn_b': _L0_xattn_in['kn_b'], 'L0_xattn_kn_dca_w': _L0_xattn_in['kn_dca_w'], 'L0_xattn_kn_dca_b': _L0_xattn_in['kn_dca_b'], 'L0_xattn_Wo': _L0_xattn_in['Wo'], 'L0_xattn_bo': _L0_xattn_in['bo'], 'L0_ffn_Wr': _L0_ffn_in['Wr'], 'L0_ffn_Wg': _L0_ffn_in['Wg'], 'L0_ffn_Wu': _L0_ffn_in['Wu'], 'L0_ffn_Wd': _L0_ffn_in['Wd'], 'L0_ffn_Wsg': _L0_ffn_in['Wsg'], 'L0_ffn_Wsu': _L0_ffn_in['Wsu'], 'L0_ffn_Wsd': _L0_ffn_in['Wsd'], 'L0_ffn_Wse': _L0_ffn_in['Wse']}

def reference(x, ctx_1024, L0_xattn_Wq, L0_xattn_bq, L0_xattn_Wk, L0_xattn_bk, L0_xattn_Wv, L0_xattn_bv, L0_xattn_Wkv_dca, L0_xattn_bkv_dca, L0_xattn_qn_w, L0_xattn_qn_b, L0_xattn_kn_w, L0_xattn_kn_b, L0_xattn_kn_dca_w, L0_xattn_kn_dca_b, L0_xattn_Wo, L0_xattn_bo, L0_ffn_Wr, L0_ffn_Wg, L0_ffn_Wu, L0_ffn_Wd, L0_ffn_Wsg, L0_ffn_Wsu, L0_ffn_Wsd, L0_ffn_Wse):
    import jax
    import jax.numpy as jnp

    def _L0_xattn_ref(x, y, Wq, bq, Wk, bk, Wv, bv, Wkv_dca, bkv_dca, qn_w, qn_b, kn_w, kn_b, kn_dca_w, kn_dca_b, Wo, bo):
        import jax, jax.numpy as jnp
        import numpy as np
        B, S1, S2, DCA = (2, 256, 128, 16)
        QDIM, KDIM, H = (256, 128, 16)
        HD = QDIM // H
        SCALE = HD ** (-0.5)
        EPS = 1e-06
        DCA_WEIGHT = 1.0

        def _ln(t, w, b):
            m = jnp.mean(t, axis=-1, keepdims=True)
            v = jnp.var(t, axis=-1, keepdims=True)
            return (t - m) * jax.lax.rsqrt(v + EPS) * w + b

        def _attn(q, k, v):
            s = jnp.einsum('bhqd,bhkd->bhqk', q, k) * SCALE
            p = jax.nn.softmax(s, axis=-1)
            return jnp.einsum('bhqk,bhkd->bhqd', p, v)
        b, s1, _ = x.shape
        y_dca = y[:, -DCA:, :]
        y_main = y[:, :-DCA, :]
        kv_dca = (y_dca @ Wkv_dca + bkv_dca).reshape(b, DCA, 2, H, HD)
        k_dca = _ln(kv_dca[:, :, 0], kn_dca_w, kn_dca_b)
        v_dca = kv_dca[:, :, 1]
        s2 = y_main.shape[1]
        q = _ln((x @ Wq + bq).reshape(b, s1, H, HD), qn_w, qn_b)
        kv = jnp.concatenate([y_main @ Wk + bk, y_main @ Wv + bv], axis=-1)
        kv = kv.reshape(b, s2, H, 2 * HD)
        k = _ln(kv[..., :HD], kn_w, kn_b)
        v = kv[..., HD:]
        qT = q.transpose(0, 2, 1, 3)
        ctx = _attn(qT, k.transpose(0, 2, 1, 3), v.transpose(0, 2, 1, 3))
        ctx = ctx.transpose(0, 2, 1, 3).reshape(b, s1, QDIM)
        ctx_dca = _attn(qT, k_dca.transpose(0, 2, 1, 3), v_dca.transpose(0, 2, 1, 3))
        ctx_dca = ctx_dca.transpose(0, 2, 1, 3).reshape(b, s1, QDIM)
        ctx = ctx + DCA_WEIGHT * ctx_dca
        return ctx @ Wo + bo

    def _L0_ffn_ref(hidden_states, Wr, Wg, Wu, Wd, Wsg, Wsu, Wsd, Wse):
        import jax, jax.numpy as jnp
        import numpy as np
        B, S, H = (1, 128, 256)
        E, K = (32, 4)
        F, FS = (176, 704)
        CAP = 32

        def silu(x):
            return x * jax.nn.sigmoid(x)
        b, s_len, h = hidden_states.shape
        x = hidden_states.reshape(-1, h)
        T = x.shape[0]
        probs = jax.nn.softmax(x @ Wr, axis=-1)
        topw, topi = jax.lax.top_k(probs, K)
        topw = topw / jnp.sum(topw, axis=-1, keepdims=True)
        shared = silu(x @ Wsg) * (x @ Wsu) @ Wsd
        shared = shared * jax.nn.sigmoid(x @ Wse)
        sel = topi.reshape(-1)
        w = topw.reshape(-1)
        tok = jnp.repeat(jnp.arange(T), K)
        oh = jax.nn.one_hot(sel, E, dtype=jnp.int32)
        pos = (jnp.cumsum(oh, axis=0) * oh).sum(-1) - 1
        valid = (pos < CAP).astype(x.dtype)
        posc = jnp.clip(pos, 0, CAP - 1)
        xe = jnp.zeros((E, CAP, h), x.dtype).at[sel, posc].add(x[tok] * valid[:, None])
        g = silu(jnp.einsum('ech,ehf->ecf', xe, Wg))
        u = jnp.einsum('ech,ehf->ecf', xe, Wu)
        ye = jnp.einsum('ecf,efh->ech', g * u, Wd)
        y_pair = ye[sel, posc] * (w * valid)[:, None]
        out = shared.at[tok].add(y_pair)
        return out.reshape(b, s_len, h)
    x = x + _L0_xattn_ref(_layernorm(x, axis=-1), ctx_1024, L0_xattn_Wq, L0_xattn_bq, L0_xattn_Wk, L0_xattn_bk, L0_xattn_Wv, L0_xattn_bv, L0_xattn_Wkv_dca, L0_xattn_bkv_dca, L0_xattn_qn_w, L0_xattn_qn_b, L0_xattn_kn_w, L0_xattn_kn_b, L0_xattn_kn_dca_w, L0_xattn_kn_dca_b, L0_xattn_Wo, L0_xattn_bo)
    x = x + _L0_ffn_ref(_layernorm(x, axis=-1), L0_ffn_Wr, L0_ffn_Wg, L0_ffn_Wu, L0_ffn_Wd, L0_ffn_Wsg, L0_ffn_Wsu, L0_ffn_Wsd, L0_ffn_Wse)
    return x

_drawn_inputs = setup_inputs


def setup_inputs(seed=0):
    import zlib

    import numpy as np

    out = dict(_drawn_inputs(seed))
    spreads = {'L0_xattn_bq': (0.0, 0.8),
     'L0_xattn_bk': (0.0, 0.401),
     'L0_xattn_bv': (0.0, 0.331),
     'L0_xattn_bkv_dca': (0.0, 0.1),
     'L0_xattn_qn_w': (1.0, 0.6),
     'L0_xattn_qn_b': (0.0, 0.8),
     'L0_xattn_kn_w': (1.0, 0.6),
     'L0_xattn_kn_b': (0.0, 0.8),
     'L0_xattn_kn_dca_w': (1.0, 0.6),
     'L0_xattn_kn_dca_b': (0.0, 0.8),
     'L0_xattn_bo': (0.0, 0.1)}
    factors = {'L0_ffn_Wr': 8.0,
     'L0_ffn_Wg': 8.0,
     'L0_ffn_Wu': 8.0,
     'L0_ffn_Wd': 8.0,
     'L0_ffn_Wsg': 4.049,
     'L0_ffn_Wsu': 4.014,
     'L0_ffn_Wsd': 4.011,
     'L0_ffn_Wse': 8.0}
    for name, (base, spread) in spreads.items():
        noise = np.random.default_rng([zlib.crc32(name.encode()), seed]).standard_normal(out[name].shape)
        drawn = base * np.exp(spread * noise) if base else spread * noise
        out[name] = jnp.asarray(drawn.astype(out[name].dtype))
    for name, factor in factors.items():
        out[name] = (out[name] * factor).astype(out[name].dtype)
    return out
```

```python
from contextlib import ExitStack

import numpy as np
import concourse.bass as bass
from concourse import mybir

F32 = mybir.dt.float32
BF16 = mybir.dt.bfloat16
U32 = mybir.dt.uint32
ALU = mybir.AluOpType
ACT = mybir.ActivationFunctionType
AX = mybir.AxisListType

B, S1, D = 32, 56, 256
SK, DY = 1500, 128
DCA = 16
H, HD = 16, 16
G = 2
T = B * S1
NT = T // 128
MAIN = SK - DCA
KT = 12
REST = MAIN - (KT - 1) * 128
DROW = 96
DCOL = (KT - 1) * 128 + DROW
KW = DCOL + DCA
PAIRS = H // 2
PR = 2 * S1
SLOT = 1536
E, CAP = 32, 32
F, FH = 176, 88
FS, FC = 704, 6
EPS_ATTN, EPS_LN = 1e-6, 1e-5
SCALE = HD ** -0.5


class Slots:
    PREP = {"Y": 0, "KV0": 1, "KV1": 0, "KV2": 1, "KV3": 0, "KT0": 0, "KT1": 1}
    BODY = [["P0", "Y", "P2", "KV1", "P4", "KV3", "P6", "KT0"], ["P1", "KV0", "P3", "KV2", "P5", "P7", "KT1"]]
    LAST = [["P0", "P2", "P4", "P6"], ["P1", "P3", "P5", "P7"]]
    AFTER_PROLOGUE = [4, 3]

    @classmethod
    def prologue(cls, unit):
        s = cls.PREP[unit]
        return s, [u for u in cls.PREP if cls.PREP[u] == s].index(unit)

    @classmethod
    def body(cls, unit, b):
        s = 0 if unit in cls.BODY[0] else 1
        return s, cls.AFTER_PROLOGUE[s] + len(cls.BODY[s]) * b + cls.BODY[s].index(unit)

    @classmethod
    def p7_before(cls, b):
        return cls.body("P7", b - 1)[1]

    @classmethod
    def last(cls, unit):
        s = 0 if unit in cls.LAST[0] else 1
        return s, cls.AFTER_PROLOGUE[s] + len(cls.BODY[s]) * (B - 1) + cls.LAST[s].index(unit)


def program(nc, a, out, stage="all"):
    with ExitStack() as ctx:
        env = Env(nc, a, out, ctx)
        with ExitStack() as part:
            shared = AttentionShared(env, part)
            project_queries(env, shared)
            attention(env, shared)
        if stage == "attn":
            dump_x1(env)
        else:
            feed_forward(env)


class Env:

    def __init__(self, nc, a, out, ctx):
        self.nc, self.a, self.out = nc, a, out
        self.sb = lambda name, shape, dt=F32: ctx.enter_context(nc.sbuf_tensor(name, shape, dt))
        self.x = self.sb("x_tokens", [128, NT, D])
        self.ctxT = self.sb("ctxT", [128, G, T])
        self.wo = self.sb("wo", [128, G, D])
        self.bo = self.sb("bo", [128, D])
        self.ident = self.sb("ident", [128, 128])


class AttentionShared:

    def __init__(self, env, ctx):
        def sb(name, shape, dt=F32):
            return ctx.enter_context(env.nc.sbuf_tensor(name, shape, dt))
        self.wkv = [sb("wkv", [128, 2, H, HD]), sb("wkv_dca", [128, 2, H, HD])]
        self.bkv = [sb("bkv", [128, 2, H, HD]), sb("bkv_dca", [128, 2, H, HD])]
        self.bias_last = sb("bias_last", [128, 2, H, HD])
        self.ln_cols = sb("ln_cols", [128, 8])
        self.pair_row = sb("pair_row", [128, 2])
        self.pair_out = sb("pair_out", [128, 2])
        self.fold = sb("fold", [128, S1])
        self.qT = sb("qT", [128, G, T])


def project_queries(env, sh):
    nc, a = env.nc, env.a
    with ExitStack() as ctx:
        def sb(name, shape, dt=F32):
            return ctx.enter_context(nc.sbuf_tensor("q_" + name, shape, dt))

        def sem(name):
            return ctx.enter_context(nc.semaphore("q_" + name))

        x, ident = env.x, env.ident
        wkv, bkv, ln_cols = sh.wkv, sh.bkv, sh.ln_cols
        wq = sb("wq", [128, 2, H, HD])
        bq = sb("bq", [128, H, HD])
        means = sb("means", [128, 7, H])
        xn = sb("xn", [128, NT, D])
        sqx = sb("sqx", [128, NT, D])
        xnT = sb("xnT", [128, G * T])
        q = sb("q", [128, NT, H, HD])
        mean_x = sb("mean_x", [128, NT])
        var = [sb("var_x", [128, NT]), sb("var_q", [128, NT * H])]
        lnv = [sb("lnv_x", [128, NT]), sb("lnv_q", [128, NT * H])]
        rstd = [sb("rstd_x", [128, NT]), sb("rstd_q", [128, NT * H])]
        tmp = [sb("tmp_x", [128, NT]), sb("tmp_q", [128, NT * H])]
        slot = [ctx.enter_context(nc.psum_tensor(f"qslot{i}", [128, SLOT], F32)) for i in range(2)]

        x_loaded, consts_loaded = sem("x_loaded"), sem("consts_loaded")
        chain_done = sem("chain_done")
        centred = sem("centred")
        squared = sem("squared")
        var_done = sem("var_done")
        ln_done = sem("ln_done")
        r0_done = sem("r0_done")
        normed = sem("normed")
        w_ready = sem("w_ready")
        full = sem("full")
        free = sem("free")

        block = ctx.enter_context(nc.Block())
        N_CONSTS = 15

        def cols(i):
            return min(12, G * NT - 12 * i) * 128

        @block.sync
        def _(sp):
            sp.dma_start(x[:], a["x"].rearrange("b s d -> (b s) d").rearrange("(n p) d -> p n d", p=128)).then_inc(x_loaded, 16)

            def const(dst, src):
                sp.dma_start(dst, src).then_inc(consts_loaded, 16)
            for half, name in enumerate(("Wk", "Wv")):
                hs = slice(half * H // 2, (half + 1) * H // 2)
                src = a[name].rearrange("k (h a d) -> k a h d", a=2, d=HD)
                for part in range(2):
                    const(wkv[0][:, part, hs, :], src[:, part])
            const(wkv[1][:], a["Wkv_dca"].rearrange("k (a h d) -> k a h d", a=2, d=HD))
            const(wq[:], a["Wq"].rearrange("(c k) (h d) -> k c h d", k=128, d=HD))
            const(env.wo[:], a["Wo"].rearrange("(c k) n -> k c n", k=128))
            const(env.bo[:], a["bo_rows"])
            const(bkv[0][:].rearrange("p a h d -> p (a h d)"), a["bkv_rows"])
            const(bkv[1][:].rearrange("p a h d -> p (a h d)"), a["bkv_dca_rows"])
            const(bq[:].rearrange("p h d -> p (h d)"), a["bq_rows"])
            const(ln_cols[:, 0:6], a["ln_cols"])
            const(ident[:], a["ident"])
            const(sh.pair_row[:], a["pair_masks"][:, 0:2])
            const(sh.pair_out[:], a["pair_masks"][:, 2:4])
            const(sh.fold[0:PR, :], a["fold"])

        N_CONSTS = 16

        @block.tensor
        def _(pe):
            pe.wait_ge(consts_loaded, 16 * N_CONSTS)

            def turn(unit, src):
                if unit >= 2:
                    pe.wait_ge(free, unit - 1)
                for k in range(12 * (unit % 3), min(12 * (unit % 3) + 12, G * NT)):
                    g, n = k // NT, k % NT
                    m = pe.transpose(slot[unit % 2][:, (k % 12) * 128:(k % 12) * 128 + 128], src(n, g), ident[:])
                m.then_inc(full, 1)

            pe.wait_ge(normed, 1)
            for unit in range(3):
                turn(unit, lambda n, g: xn[:, n, g * 128:(g + 1) * 128])
            pe.wait_ge(w_ready, 1)
            for unit in range(3, 6):
                pe.wait_ge(free, 3 if unit == 3 else unit - 1)
                for n in range(6 * (unit - 3), min(6 * (unit - 3) + 6, NT)):
                    for c in range(G):
                        m = pe.matmul(slot[unit % 2][:, (n % 6) * D:(n % 6 + 1) * D],
                                      xnT[:, c * T + n * 128:c * T + (n + 1) * 128],
                                      wq[:, c].rearrange("p h d -> p (h d)"), start=(c == 0), stop=(c == 1))
                m.then_inc(full, 1)
            pe.wait_ge(normed, 2)
            for unit in range(6, 9):
                turn(unit, lambda n, g: q[:, n, g * 8:(g + 1) * 8, :].rearrange("p h d -> p (h d)"))

        @block.scalar
        def _(act):
            act.preload_act_table_set("natural_log_exp_and_others")

            def rstd_start(k, src, dst):
                act.wait_ge(centred, k + 1)
                act.activation(dst, src, ACT.Square).then_inc(squared, 1)
                act.wait_ge(var_done, k + 1)
                act.activation(lnv[k][:], var[k][:], ACT.Ln).then_inc(ln_done, 1)
                act.wait_ge(ln_done, k + 1)
                act.activation(rstd[k][:], lnv[k][:], ACT.Exp, scale=-0.5).then_inc(r0_done, 1)

            rstd_start(0, xn[:], sqx[:])
            for unit in range(3):
                act.wait_ge(full, unit + 1)
                act.activation(xnT[:, unit * SLOT:unit * SLOT + cols(unit)], slot[unit % 2][:, 0:cols(unit)],
                               ACT.Copy).then_inc(free, 1)
            rstd_start(1, q[:].rearrange("p n h d -> p n (h d)"), sqx[:])
            act.wait_ge(w_ready, 1)
            for unit in range(6, 9):
                c0, n = (unit - 6) * SLOT, cols(unit - 6)
                act.wait_ge(full, unit + 1)
                act.activation(sh.qT[:].rearrange("p c t -> p (c t)")[:, c0:c0 + n], slot[unit % 2][:, 0:n],
                               ACT.Identity, scale=ln_cols[:, 6:7], bias=ln_cols[:, 7:8]).then_inc(free, 1)

        @block.vector
        def _(dve):
            step = [0]

            def chain(ins):
                step[0] += 1
                ins.then_inc(chain_done, 1)
                dve.wait_ge(chain_done, step[0])

            def normalise(k, sq, n, eps, values):
                dve.wait_ge(squared, k + 1)
                chain(dve.tensor_reduce(tmp[k][:], sq, AX.X, ALU.add))
                dve.tensor_scalar(var[k][:], tmp[k][:], 1.0 / n, eps, ALU.mult, ALU.add).then_inc(var_done, 1)
                r, t = rstd[k][:], tmp[k][:]
                dve.wait_ge(r0_done, k + 1)
                chain(dve.tensor_tensor(t, r, r, ALU.mult))
                chain(dve.scalar_tensor_tensor(out=t, in0=t, scalar=-0.5, in1=var[k][:], op0=ALU.mult, op1=ALU.mult))
                chain(dve.scalar_tensor_tensor(out=r, in0=t, scalar=1.5, in1=r, op0=ALU.add, op1=ALU.mult))
                dve.tensor_tensor(values, values, r.unsqueeze(2).broadcast_to([128, r.shape[1], n]),
                                  ALU.mult).then_inc(normed, 1)

            dve.wait_ge(x_loaded, 16)
            chain(dve.tensor_reduce(mean_x[:], x[:], AX.X, ALU.add))
            dve.scalar_tensor_tensor(out=xn[:], in0=mean_x[:].unsqueeze(2).broadcast_to([128, NT, D]), scalar=-1.0 / D,
                                     in1=x[:], op0=ALU.mult, op1=ALU.add).then_inc(centred, 1)
            dve.wait_ge(consts_loaded, 16 * N_CONSTS)
            mats = [wkv[0][:, 0], wkv[1][:, 0], bkv[0][:, 0], bkv[1][:, 0], wq[:, 0], wq[:, 1], bq[:]]
            for k, w in enumerate(mats):
                last = dve.tensor_reduce(means[:, k, :], w, AX.X, ALU.add)
            chain(last)
            for k, w in enumerate(mats):
                last = dve.scalar_tensor_tensor(out=w, in0=means[:, k, :].unsqueeze(2).broadcast_to([128, H, HD]),
                                                scalar=-1.0 / HD, in1=w, op0=ALU.mult, op1=ALU.add)
            chain(last)
            dve.tensor_copy(sh.bias_last[0:DROW], bkv[0][0:DROW])
            dve.tensor_copy(sh.bias_last[DROW:], bkv[1][DROW:])
            dve.tensor_scalar(ln_cols[:, 6:8], ln_cols[:, 0:2], SCALE, None, ALU.mult).then_inc(w_ready, 1)

            dve.wait_ge(centred, 1)
            normalise(0, sqx[:], D, EPS_LN, xn[:])
            for unit in range(3, 6):
                n0, n1 = 6 * (unit - 3), min(6 * (unit - 3) + 6, NT)
                dve.wait_ge(full, unit + 1)
                ins = dve.tensor_tensor(q[:, n0:n1].rearrange("p n h d -> p n (h d)"),
                                        slot[unit % 2][:, 0:(n1 - n0) * D].rearrange("p (n f) -> p n f", f=D),
                                        bq[:].rearrange("p h d -> p (h d)").unsqueeze(1).broadcast_to([128, n1 - n0, D]),
                                        ALU.add)
                ins.then_inc(free, 1)
            dve.wait_ge(free, 6)
            dve.memset(mean_x[:], 0.0).then_inc(centred, 1)
            normalise(1, sqx[:].rearrange("p n (h d) -> p (n h) d", d=HD), HD, EPS_ATTN,
                      q[:].rearrange("p n h d -> p (n h) d"))



def attention(env, sh):
    nc, a = env.nc, env.a
    with ExitStack() as ctx:
        def sb(name, shape, dt=F32):
            return ctx.enter_context(nc.sbuf_tensor("a_" + name, shape, dt))

        def sem(name):
            return ctx.enter_context(nc.semaphore("a_" + name))

        ident = env.ident
        wkv, bkv, bias_last, ln_cols = sh.wkv, sh.bkv, sh.bias_last, sh.ln_cols
        pair_row, pair_out, fold, qT = sh.pair_row, sh.pair_out, sh.fold, sh.qT
        qpair = [sb(f"qpair{i}", [128, G, 2, S1]) for i in range(2)]
        y = [sb(f"y{i}", [128, KT, DY]) for i in range(2)]
        yT = sb("yT", [128, SLOT])
        kv = sb("kv", [128, KT, 2 * D])
        sq = [sb(f"sq{i}", [128, 3, D]) for i in range(2)]
        var = sb("var", [128, KT * H])
        lnv = sb("lnv", [128, KT * H])
        rstd = sb("rstd", [128, KT * H])
        newt = sb("newt", [128, KT * H])
        kn = sb("kn", [128, KT, D])
        keys = [sb(f"keys{i}", [128, G, KW]) for i in range(2)]
        vals = [sb(f"vals{i}", [128, KT, PAIRS, 64], BF16) for i in range(2)]
        P = [sb(f"P{i}", [128, SLOT]) for i in range(2)]
        pt = [sb(f"pt{i}", [128, KT * PR + 16]) for i in range(2)]
        pt_lo = [sb(f"pt_lo{i}", [128, KT * PR + 16], BF16) for i in range(2)]
        negmax = sb("negmax", [128, PAIRS])
        negmax_dca = sb("negmax_dca", [128, PAIRS])
        total = [sb(f"total{i}", [128, PAIRS]) for i in range(2)]
        total_dca = sb("total_dca", [128, PAIRS])
        rtotal_dca = sb("rtotal_dca", [128, PAIRS])
        rtotal = sb("rtotal", [128, PAIRS])
        coef = sb("coef", [128, PAIRS, 2])
        o_hi = sb("o_hi", [128, D])
        o_lo = sb("o_lo", [128, D])
        o_sum = sb("o_sum", [128, D])

        slot = [ctx.enter_context(nc.psum_tensor(f"slot{i}", [128, SLOT], F32)) for i in range(2)]
        pt_ps = ctx.enter_context(nc.psum_tensor("pt_ps", [128, 512], F32))
        acc = ctx.enter_context(nc.psum_tensor("acc", [128, PAIRS, 64], F32))

        slot_full = [sem("slot_full0"), sem("slot_full1")]
        slot_free = [sem("slot_free0"), sem("slot_free1")]
        y_loaded = [sem("y_loaded0"), sem("y_loaded1")]
        zeroed = sem("zeroed")
        qpair_ready = sem("qpair_ready")
        max_ready = sem("max_ready")
        kv_chain = sem("kv_chain")
        dca_ready = sem("dca_ready")
        dca_chain = sem("dca_chain")
        pt_full = sem("pt_full")
        pt_free = sem("pt_free")
        lo_done = sem("lo_done")
        pv_done = sem("pv_done")
        sq_done = sem("sq_done")
        ss_done = sem("ss_done")
        vhi_done = sem("vhi_done")
        vlo_done = sem("vlo_done")
        var_ready = sem("var_ready")
        ln_done = sem("ln_done")
        r0_ready = sem("r0_ready")
        newton = sem("newton")
        kn_ready = sem("kn_ready")
        o_chain = sem("o_chain")

        block = ctx.enter_context(nc.Block())
        PT_USES = 3 * PAIRS + 1
        PTW = 4 * PR

        def bcast_bias(ap, n):
            return ap[:].rearrange("p a h d -> p (a h d)").unsqueeze(1).broadcast_to([128, n, 2 * D])

        @block.sync
        def _(sp):
            def load_y(b, par):
                sp.dma_start(y[par][:, 0:KT - 1, :], a["ctx"][b, 0:(KT - 1) * 128, :].rearrange("(p t) d -> p t d", p=128)).then_inc(y_loaded[par], 16)
                sp.dma_start(y[par][0:REST, KT - 1, :], a["ctx"][b, (KT - 1) * 128:MAIN, :]).then_inc(y_loaded[par], 16)
                sp.dma_start(y[par][DROW:DROW + DCA, KT - 1, :], a["ctx"][b, MAIN:SK, :]).then_inc(y_loaded[par], 16)

            sp.wait_ge(zeroed, 1)
            load_y(0, 0)
            load_y(1, 1)
            sl, n = Slots.prologue("Y")
            sp.wait_ge(slot_full[sl], n + 1)
            load_y(2, 0)

            def ahead(b, par):
                sl, n = Slots.body("Y", b)
                sp.wait_ge(slot_full[sl], n + 1)
                load_y(b + 3, 1 - par)
            with sp.Fori(0, (B - 4) // 2) as i:
                for par in range(2):
                    ahead(2 * i + par, par)
            ahead(B - 4, 0)

        @block.tensor
        def _(pe):
            def put(use):
                sl, n = use
                if not (isinstance(n, int) and n == 0):
                    pe.wait_ge(slot_free[sl], n)
                return slot[sl]

            def unit_y(use, n_loaded, par):
                ps = put(use)
                pe.wait_ge(y_loaded[par], n_loaded)
                for t in range(KT):
                    m = pe.transpose(ps[:, t * 128:t * 128 + 128], y[par][:, t, :], ident[:])
                m.then_inc(slot_full[use[0]], 1)

            def unit_kv(use, u, y_use):
                ps = put(use)
                if u == 0:
                    pe.wait_ge(slot_free[y_use[0]], y_use[1] + 1)
                w = [wkv[k][:].rearrange("p a h d -> p (a h d)") for k in range(2)]
                for k in range(3):
                    t = 3 * u + k
                    o = ps[:, k * 512:(k + 1) * 512]
                    if t < KT - 1:
                        m = pe.matmul(o, yT[:, t * 128:(t + 1) * 128], w[0], start=True, stop=True)
                    else:
                        pe.matmul(o[0:DROW], yT[:, t * 128:t * 128 + DROW], w[0], start=True, stop=True)
                        m = pe.matmul(o[DROW:DROW + DCA], yT[:, DCOL:DCOL + DCA], w[1], start=True, stop=True)
                m.then_inc(slot_full[use[0]], 1)

            def unit_kt(use, g, n_kn):
                ps = put(use)
                pe.wait_ge(kn_ready, n_kn)
                for t in range(KT):
                    m = pe.transpose(ps[:, t * 128:t * 128 + 128], kn[:, t, g * 128:(g + 1) * 128], ident[:])
                m.then_inc(slot_full[use[0]], 1)

            def unit_p(use, j, par):
                ps = put(use)
                g, r = j // 4, 32 * (j % 4)
                for c0 in range(0, KW, 512):
                    c1 = min(c0 + 512, KW)
                    m = pe.matmul(ps[0:PR, c0:c1], qpair[par][r:r + 32, g].rearrange("p i q -> p (i q)"),
                                  keys[par][r:r + 32, g, c0:c1], start=True, stop=True)
                m.then_inc(slot_full[use[0]], 1)

            def pt_put(n):
                if not isinstance(n, int) or n >= 1:
                    pe.wait_ge(pt_free, n)

            def turn(b, j, h):
                pt_put(PT_USES * b + 3 * j + h)
                for k in range(4):
                    t = 4 * h + k
                    m = pe.transpose(pt_ps[:, k * PR:(k + 1) * PR], P[j % 2][0:PR, t * 128:(t + 1) * 128],
                                     ident[0:PR, 0:PR])
                m.then_inc(pt_full, 1)

            def pv(b, j, h, par):
                if h == 0:
                    pe.wait_ge(pt_free, PT_USES * b + 3 * j + 3)
                    if j == 0:
                        if not isinstance(b, int) or b > 0:
                            pe.wait_ge(o_chain, 5 * b)
                        pe.wait_ge(vhi_done, 4 * b + 4)
                        pe.wait_ge(vlo_done, 4 * b + 4)
                pe.wait_ge(lo_done, 3 * PAIRS * b + 3 * j + min(h + 2, 3))
                hi = pt[j % 2][:].bitcast(BF16)[:, 1::2]
                for k in range(4):
                    t = 4 * h + k
                    rows = 128 if t < KT - 1 else DROW + DCA
                    for part, w in enumerate((hi, pt_lo[j % 2][:])):
                        m = pe.matmul(acc[:, j, :], w[0:rows, t * PR:t * PR + 128], vals[par][0:rows, t, j, :],
                                      start=(j == 0 and t == 0 and part == 0), stop=(t == KT - 1 and part == 1),
                                      skip_group_check=True)
                if h == 2:
                    m.then_inc(pv_done, 1)

            def turns(b, j, par, p_use):
                pe.wait_ge(slot_free[p_use[0]], p_use[1] + 1)
                for h in range(3):
                    if h == 2:
                        pe.wait_ge(dca_ready, PAIRS * b + j + 1)
                    turn(b, j, h)
                    if j > 0:
                        pv(b, j - 1, h, par)

            def output(b):
                pe.wait_ge(o_chain, 5 * b + 5)
                pt_put(PT_USES * b + 3 * PAIRS)
                for g in range(G):
                    m = pe.matmul(pt_ps[:, g * S1:(g + 1) * S1], o_sum[0:PR, g * 128:(g + 1) * 128], fold[0:PR, :],
                                  start=True, stop=True)
                m.then_inc(pt_full, 1)

            unit_y(Slots.prologue("Y"), 48, 0)
            for u in range(4):
                unit_kv(Slots.prologue(f"KV{u}"), u, Slots.prologue("Y"))
            for g in range(G):
                unit_kt(Slots.prologue(f"KT{g}"), g, 1)

            def batch(b, par, prep, n_loaded=None):
                use = (lambda u: Slots.body(u, b)) if prep else Slots.last
                pe.wait_ge(qpair_ready, b + 1)
                for g in range(G):
                    sl, n = (Slots.prologue(f"KT{g}") if isinstance(b, int) and b == 0 else Slots.body(f"KT{g}", b - 1))
                    pe.wait_ge(slot_free[sl], n + 1)
                unit_p(use("P0"), 0, par)
                unit_p(use("P1"), 1, par)
                if prep:
                    unit_y(use("Y"), n_loaded, 1 - par)
                    unit_kv(use("KV0"), 0, use("Y"))
                turns(b, 0, par, use("P0"))
                unit_p(use("P2"), 2, par)
                turns(b, 1, par, use("P1"))
                unit_p(use("P3"), 3, par)
                if prep:
                    unit_kv(use("KV1"), 1, None)
                    unit_kv(use("KV2"), 2, None)
                turns(b, 2, par, use("P2"))
                unit_p(use("P4"), 4, par)
                turns(b, 3, par, use("P3"))
                unit_p(use("P5"), 5, par)
                if prep:
                    unit_kv(use("KV3"), 3, None)
                turns(b, 4, par, use("P4"))
                unit_p(use("P6"), 6, par)
                turns(b, 5, par, use("P5"))
                unit_p(use("P7"), 7, par)
                turns(b, 6, par, use("P6"))
                if prep:
                    unit_kt(use("KT0"), 0, b + 2)
                turns(b, 7, par, use("P7"))
                if prep:
                    unit_kt(use("KT1"), 1, b + 2)
                for h in range(3):
                    pv(b, 7, h, par)
                output(b)

            batch(0, 0, True, 48)
            with pe.Fori(0, B // 2 - 1) as i:
                batch(2 * i + 1, 1, True, 48 * i + 96)
                batch(2 * i + 2, 0, True, 48 * i + 96)
            batch(B - 1, 1, False)

        @block.scalar
        def _(act):
            act.preload_act_table_set("natural_log_exp_and_others")
            def take(use):
                sl, n = use
                act.wait_ge(slot_full[sl], n + 1)
                return slot[sl]

            def free(ins, use):
                ins.then_inc(slot_free[use[0]], 1)

            def ev_y(use):
                free(act.activation(yT[:], take(use)[:], ACT.Copy), use)

            def squares(n, u, kv_use):
                act.wait_ge(slot_free[kv_use[0]], kv_use[1] + 1)
                if not isinstance(n, int) or n >= 2:
                    act.wait_ge(ss_done, n - 1)
                act.activation(sq[u % 2][:], kv[:, 3 * u:3 * u + 3, 0:D], ACT.Square).then_inc(sq_done, 1)

            def rstd_start(n):
                act.wait_ge(var_ready, n + 1)
                act.activation(lnv[:], var[:], ACT.Ln).then_inc(ln_done, 1)
                act.wait_ge(ln_done, n + 1)
                act.activation(rstd[:], lnv[:], ACT.Exp, scale=-0.5).then_inc(r0_ready, 1)

            def ev_kt(use, g, par):
                ps = take(use)
                act.activation(keys[par][:, g, 0:DCOL], ps[:, 0:DCOL], ACT.Identity, scale=ln_cols[:, 2:3], bias=ln_cols[:, 3:4])
                free(act.activation(keys[par][:, g, DCOL:KW], ps[:, DCOL:KW], ACT.Identity, scale=ln_cols[:, 4:5],
                                    bias=ln_cols[:, 5:6]), use)

            def probs(b, j, par, use):
                ps = slot[use[0]]
                act.wait_ge(max_ready, 2 * (PAIRS * b + j + 1))
                if j >= 2:
                    act.wait_ge(pt_full, PT_USES * b + 3 * (j - 1))
                elif not isinstance(b, int) or b > 0:
                    act.wait_ge(pt_full, PT_USES * (b - 1) + 3 * (PAIRS - 1 + j))
                act.activation(P[j % 2][0:PR, 0:MAIN], ps[0:PR, 0:MAIN], ACT.Exp, bias=negmax[0:PR, j:j + 1],
                               accum_out=total[par][0:PR, j:j + 1])
                free(act.activation(P[j % 2][0:PR, DCOL:KW], ps[0:PR, DCOL:KW], ACT.Exp, bias=negmax_dca[0:PR, j:j + 1],
                                    accum_out=total_dca[0:PR, j:j + 1]), use)

            def turned(b, j):
                for h in range(3):
                    act.wait_ge(pt_full, PT_USES * b + 3 * j + h + 1)
                    if h == 0 and (j >= 2 or not isinstance(b, int) or b > 0):
                        act.wait_ge(pv_done, PAIRS * b + j - 1)
                    act.activation(pt[j % 2][:, h * PTW:(h + 1) * PTW], pt_ps[:, 0:PTW], ACT.Copy).then_inc(pt_free, 1)

            use = Slots.prologue
            ev_y(use("Y"))
            for u in range(4):
                squares(u, u, use(f"KV{u}"))
            rstd_start(0)
            for g in range(G):
                ev_kt(use(f"KT{g}"), g, 0)

            def batch(b, par, prep):
                use = (lambda u: Slots.body(u, b)) if prep else Slots.last
                probs(b, 0, par, use("P0"))
                probs(b, 1, par, use("P1"))
                if prep:
                    ev_y(use("Y"))
                turned(b, 0)
                probs(b, 2, par, use("P2"))
                if prep:
                    squares(4 * b + 4, 0, use("KV0"))
                turned(b, 1)
                probs(b, 3, par, use("P3"))
                turned(b, 2)
                probs(b, 4, par, use("P4"))
                if prep:
                    squares(4 * b + 5, 1, use("KV1"))
                    squares(4 * b + 6, 2, use("KV2"))
                turned(b, 3)
                probs(b, 5, par, use("P5"))
                turned(b, 4)
                if prep:
                    squares(4 * b + 7, 3, use("KV3"))
                probs(b, 6, par, use("P6"))
                turned(b, 5)
                if prep:
                    rstd_start(b + 1)
                probs(b, 7, par, use("P7"))
                turned(b, 6)
                if prep:
                    ev_kt(use("KT0"), 0, 1 - par)
                turned(b, 7)
                if prep:
                    ev_kt(use("KT1"), 1, 1 - par)

            batch(0, 0, True)
            with act.Fori(0, B // 2 - 1) as i:
                batch(2 * i + 1, 1, True)
                batch(2 * i + 2, 0, True)
            batch(B - 1, 1, False)

        @block.gpsimd
        def _(pool):
            def queries(b, par):
                if isinstance(b, int):
                    src = qT[:, :, b * S1:b * S1 + S1]
                else:
                    src = qT[:, :, bass.ds(b * S1, S1)]
                pool.tensor_tensor(qpair[par][:], src.unsqueeze(2).broadcast_to([128, G, 2, S1]),
                                   pair_row[:].unsqueeze(1).unsqueeze(3).broadcast_to([128, G, 2, S1]),
                                   ALU.mult).then_inc(qpair_ready, 1)

            def low_vals(n, u, par):
                pool.wait_ge(vhi_done, n + 1)
                v = vals[par][:, 3 * u:3 * u + 3]
                pool.tensor_tensor(v[:, :, :, 32:64], kv[:, 3 * u:3 * u + 3, D:2 * D].rearrange("p t (j c) -> p t j c", c=32),
                                   v[:, :, :, 0:32], ALU.subtract).then_inc(vlo_done, 1)

            def norm_keys(n):
                pool.wait_ge(newton, 3 * n + 3)
                pool.tensor_tensor(kn[:].rearrange("p t (h d) -> p t h d", d=HD),
                                   kv[:, :, 0:D].rearrange("p t (h d) -> p t h d", d=HD),
                                   rstd[:].rearrange("p (t h) -> p t h", h=H).unsqueeze(3).broadcast_to([128, KT, H, HD]),
                                   ALU.mult).then_inc(kn_ready, 1)

            queries(0, 0)
            for u in range(4):
                low_vals(u, u, 0)
            norm_keys(0)

            def batch(b, par):
                for u in range(4):
                    low_vals(4 * b + 4 + u, u, 1 - par)
                queries(b + 1, 1 - par)
                norm_keys(b + 1)

            batch(0, 0)
            with pool.Fori(0, B // 2 - 1) as i:
                batch(2 * i + 1, 1)
                batch(2 * i + 2, 0)

        @block.vector
        def _(dve):
            dve.memset(y[0][:, KT - 1, :], 0.0)
            dve.memset(y[1][:, KT - 1, :], 0.0).then_inc(zeroed, 1)
            for t in (P[0], P[1]):
                dve.memset(t[:], 0.0).then_inc(zeroed, 1)
            for t in (*pt, *pt_lo):
                dve.memset(t[:, KT * PR:], 0.0).then_inc(zeroed, 1)
            dve.memset(kv[:, KT - 1, :], 0.0).then_inc(zeroed, 1)
            dve.wait_ge(zeroed, 8)

            def ev_kv(n, u, kv_use, par):
                ps = slot[kv_use[0]]
                dve.wait_ge(slot_full[kv_use[0]], kv_use[1] + 1)
                if not isinstance(n, int) or n >= 4:
                    dve.wait_ge(vlo_done, n - 3)
                    if u == 0:
                        dve.wait_ge(kn_ready, kn_uses[0])
                bias = bkv[0][:].rearrange("p a h d -> p (a h d)")
                whole = 3 if u < 3 else 2
                ins = dve.tensor_tensor(kv[:, 3 * u:3 * u + whole, :],
                                        ps[:, 0:whole * 512].rearrange("p (t f) -> p t f", f=512),
                                        bias.unsqueeze(1).broadcast_to([128, whole, 512]), ALU.add)
                if u == 3:
                    rows = DROW + DCA
                    ins.then_inc(kv_chain, 1)
                    ins = dve.tensor_tensor(kv[0:rows, KT - 1, :], ps[0:rows, 1024:1536],
                                            bias_last[0:rows].rearrange("p a h d -> p (a h d)"), ALU.add)
                ins.then_inc(slot_free[kv_use[0]], 1)
                dve.wait_ge(slot_free[kv_use[0]], kv_use[1] + 1)
                if u == 3:
                    dve.wait_ge(kv_chain, kv_uses[0])
                dve.tensor_copy(vals[par][:, 3 * u:3 * u + 3, :, 0:32],
                                kv[:, 3 * u:3 * u + 3, D:2 * D].rearrange("p t (j c) -> p t j c", c=32)).then_inc(vhi_done, 1)

            def sums(n, u):
                dve.wait_ge(sq_done, n + 1)
                dve.tensor_reduce(newt[:, u * 3 * H:(u + 1) * 3 * H],
                                  sq[u % 2][:].rearrange("p t (h d) -> p (t h) d", d=HD), AX.X, ALU.add).then_inc(ss_done, 1)

            def variances(n):
                dve.wait_ge(ss_done, 4 * n + 4)
                dve.tensor_scalar(var[:], newt[:], 1.0 / HD, EPS_ATTN, ALU.mult, ALU.add).then_inc(var_ready, 1)

            def newton_step(n):
                dve.wait_ge(r0_ready, n + 1)
                dve.wait_ge(var_ready, n + 1)
                dve.tensor_tensor(newt[:], rstd[:], rstd[:], ALU.mult).then_inc(newton, 1)
                dve.wait_ge(newton, 3 * n + 1)
                dve.scalar_tensor_tensor(out=newt[:], in0=newt[:], scalar=-0.5, in1=var[:],
                                         op0=ALU.mult, op1=ALU.mult).then_inc(newton, 1)
                dve.wait_ge(newton, 3 * n + 2)
                dve.scalar_tensor_tensor(out=rstd[:], in0=newt[:], scalar=1.5, in1=rstd[:],
                                         op0=ALU.add, op1=ALU.mult).then_inc(newton, 1)

            def maxima(b, j, use):
                ps = slot[use[0]]
                dve.wait_ge(slot_full[use[0]], use[1] + 1)
                if j == 0 and (not isinstance(b, int) or b > 0):
                    dve.wait_ge(slot_free[1], Slots.p7_before(b) + 1)
                dve.tensor_reduce(negmax[0:PR, j:j + 1], ps[0:PR, 0:MAIN], AX.X, ALU.max, negate=True).then_inc(max_ready, 1)
                dve.tensor_reduce(negmax_dca[0:PR, j:j + 1], ps[0:PR, DCOL:KW], AX.X, ALU.max, negate=True).then_inc(max_ready, 1)

            def rescale_dca(b, j, par, use):
                dve.wait_ge(slot_free[use[0]], use[1] + 1)
                dve.reciprocal(rtotal_dca[0:PR, j:j + 1], total_dca[0:PR, j:j + 1]).then_inc(dca_chain, 1)
                dve.wait_ge(dca_chain, PAIRS * b + j + 1)
                p = P[j % 2][0:PR, DCOL:KW]
                dve.tensor_scalar(p, p, rtotal_dca[0:PR, j:j + 1], total[par][0:PR, j:j + 1],
                                  ALU.mult, ALU.mult).then_inc(dca_ready, 1)

            def low(b, j):
                hi = pt[j % 2][:].bitcast(BF16)[:, 1::2]
                for h in range(3):
                    dve.wait_ge(pt_free, PT_USES * b + 3 * j + h + 1)
                    if h == 0 and (j >= 2 or not isinstance(b, int) or b > 0):
                        dve.wait_ge(pv_done, PAIRS * b + j - 1)
                    c = slice(h * PTW, (h + 1) * PTW)
                    dve.tensor_tensor(pt_lo[j % 2][:, c], pt[j % 2][:, c], hi[:, c], ALU.subtract).then_inc(lo_done, 1)

            def output(b, par):
                dve.reciprocal(rtotal[0:PR], total[par][0:PR]).then_inc(o_chain, 1)
                dve.wait_ge(o_chain, 5 * b + 1)
                dve.tensor_tensor(coef[0:PR], rtotal[0:PR].unsqueeze(2).broadcast_to([PR, PAIRS, 2]),
                                  pair_out[0:PR].unsqueeze(1).broadcast_to([PR, PAIRS, 2]), ALU.mult).then_inc(o_chain, 1)
                dve.wait_ge(o_chain, 5 * b + 2)
                dve.wait_ge(pv_done, PAIRS * b + PAIRS)
                cb = coef[0:PR].rearrange("p j i -> p (j i)").unsqueeze(2).broadcast_to([PR, H, HD]).rearrange(
                    "p (j i) d -> p j i d", i=2)
                for k, o in enumerate((o_hi, o_lo)):
                    ins = dve.tensor_tensor(o[0:PR].rearrange("p (j i d) -> p j i d", i=2, d=HD),
                                            acc[0:PR, :, 32 * k:32 * k + 32].rearrange("p j (i d) -> p j i d", d=HD), cb, ALU.mult)
                    ins.then_inc(o_chain, 1)
                dve.wait_ge(o_chain, 5 * b + 4)
                dve.tensor_tensor(o_sum[0:PR], o_hi[0:PR], o_lo[0:PR], ALU.add).then_inc(o_chain, 1)
                dve.wait_ge(pt_full, PT_USES * b + PT_USES)
                dst = env.ctxT[:, :, b * S1:(b + 1) * S1] if isinstance(b, int) else env.ctxT[:, :, bass.ds(b * S1, S1)]
                dve.tensor_copy(dst, pt_ps[:, 0:G * S1].rearrange("p (g q) -> p g q", g=G)).then_inc(pt_free, 1)

            kn_uses, kv_uses = [0], [1]
            use = Slots.prologue
            for u in range(4):
                ev_kv(u, u, use(f"KV{u}"), 0)
                if u:
                    sums(u - 1, u - 1)
            sums(3, 3)
            variances(0)
            newton_step(0)

            def batch(b, par, prep):
                use = (lambda u: Slots.body(u, b)) if prep else Slots.last
                kn_uses[0], kv_uses[0] = b + 1, b + 2
                maxima(b, 0, use("P0"))
                maxima(b, 1, use("P1"))
                if prep:
                    ev_kv(4 * b + 4, 0, use("KV0"), 1 - par)
                rescale_dca(b, 0, par, use("P0"))
                low(b, 0)
                maxima(b, 2, use("P2"))
                if prep:
                    sums(4 * b + 4, 0)
                rescale_dca(b, 1, par, use("P1"))
                low(b, 1)
                maxima(b, 3, use("P3"))
                if prep:
                    ev_kv(4 * b + 5, 1, use("KV1"), 1 - par)
                rescale_dca(b, 2, par, use("P2"))
                low(b, 2)
                maxima(b, 4, use("P4"))
                if prep:
                    ev_kv(4 * b + 6, 2, use("KV2"), 1 - par)
                    sums(4 * b + 5, 1)
                rescale_dca(b, 3, par, use("P3"))
                low(b, 3)
                maxima(b, 5, use("P5"))
                if prep:
                    ev_kv(4 * b + 7, 3, use("KV3"), 1 - par)
                    sums(4 * b + 6, 2)
                rescale_dca(b, 4, par, use("P4"))
                low(b, 4)
                maxima(b, 6, use("P6"))
                if prep:
                    sums(4 * b + 7, 3)
                    variances(b + 1)
                rescale_dca(b, 5, par, use("P5"))
                low(b, 5)
                maxima(b, 7, use("P7"))
                if prep:
                    newton_step(b + 1)
                rescale_dca(b, 6, par, use("P6"))
                low(b, 6)
                rescale_dca(b, 7, par, use("P7"))
                low(b, 7)
                output(b, par)

            batch(0, 0, True)
            with dve.Fori(0, B // 2 - 1) as i:
                batch(2 * i + 1, 1, True)
                batch(2 * i + 2, 0, True)
            batch(B - 1, 1, False)


def dump_x1(env):
    nc = env.nc
    with ExitStack() as ctx:
        done = ctx.enter_context(nc.semaphore("dump_done"))
        block = ctx.enter_context(nc.Block())

        @block.sync
        def _(sp):

            sp.dma_start(EXTRA.rearrange("g f t -> f g t"), env.ctxT[:]).then_inc(done, 16)
            sp.wait_ge(done, 16)


def feed_forward(env):
    nc = env.nc
    with ExitStack() as ctx:
        def sb(name, shape, dt=F32):
            return ctx.enter_context(nc.sbuf_tensor(name, shape, dt))
        sh = FfnShared(sb, ctx.enter_context(nc.semaphore("group_loaded0")), ctx.enter_context(nc.semaphore("group_loaded1")))
        shared_expert(env, sh)
        routed_experts(env, sh)


class FfnShared:

    def __init__(self, sb, loaded0, loaded1):
        self.h_hi = sb("h_hi", [128, NT, D], BF16)
        self.h_lo = sb("h_lo", [128, NT, D], BF16)
        self.place = sb("place", [128, NT, E])
        self.w_hi = sb("w_hi", [128, NT, E], BF16)
        self.w_lo = sb("w_lo", [128, NT, E], BF16)
        self.iota = sb("iota", [128, E])
        self.w_up = [sb(f"w_up{i}", [128, 2, 4, 2 * F]) for i in range(2)]
        self.w_down = [sb(f"w_down{i}", [FH, 2, 4, D]) for i in range(2)]
        self.loaded = [loaded0, loaded1]

    def load(self, sp, a, q, par):
        for c in range(2):
            for k, name in enumerate(("Wg", "Wu")):
                sp.dma_start(self.w_up[par][:, c, :, k * F:(k + 1) * F],
                             a[name][bass.ds(q * 4, 4), c * 128:(c + 1) * 128, :].rearrange("e k f -> k e f")
                             if not isinstance(q, int) else
                             a[name][q * 4:q * 4 + 4, c * 128:(c + 1) * 128, :].rearrange("e k f -> k e f")
                             ).then_inc(self.loaded[par], 16)
            sp.dma_start(self.w_down[par][:, c],
                         a["Wd"][bass.ds(q * 4, 4), c * FH:(c + 1) * FH, :].rearrange("e f n -> f e n")
                         if not isinstance(q, int) else
                         a["Wd"][q * 4:q * 4 + 4, c * FH:(c + 1) * FH, :].rearrange("e f n -> f e n")
                         ).then_inc(self.loaded[par], 16)


LOADS = 6 * 16


def shared_expert(env, sh):
    nc, a = env.nc, env.a
    with ExitStack() as ctx:
        def sb(name, shape, dt=F32):
            return ctx.enter_context(nc.sbuf_tensor("s_" + name, shape, dt))

        def sem(name):
            return ctx.enter_context(nc.semaphore("s_" + name))

        x, ident = env.x, env.ident
        sq = env.ctxT[:].rearrange("p g t -> p (g t)").rearrange("p (n d) -> p n d", d=D)
        h = sb("h", [128, NT, D])
        hT = sb("hT", [128, 2, T])
        w_route = sb("w_route", [128, 2, E + 1])
        w_sup = sb("w_sup", [128, 2, 2, FS])
        w_sdown = sb("w_sdown", [128, FC, D])
        mean_x = sb("mean_x", [128, NT])
        var, lnv, rstd, tmp = (sb(n, [128, NT]) for n in ("var", "lnv", "rstd", "tmp"))
        logits = sb("logits", [128, NT, E + 1])
        top = sb("top", [128, NT, 8])
        top_at = sb("top_at", [128, NT, 8], U32)
        top_atf = sb("top_atf", [128, NT, 4])
        wtop = sb("wtop", [128, NT, 4])
        wsum = sb("wsum", [128, NT])
        onehot = sb("onehot", [128, NT, 4, E])
        sel = sb("sel", [128, NT, E])
        sel_b = sb("sel_b", [128, NT, E], BF16)
        w_tok = sb("w_tok", [128, NT, E])
        before = sb("before", [128, 128])
        before_b = sb("before_b", [128, 128], BF16)
        ones_b = sb("ones_b", [128, 128], BF16)
        sig = sb("sig", [128, NT])
        en = [sb(f"en{i}", [128, 512]) for i in range(2)]
        act_g = [sb(f"act_g{i}", [128, 512]) for i in range(2)]
        gu = [sb(f"gu{i}", [128, FC, 512]) for i in range(2)]
        wide = ctx.enter_context(nc.psum_tensor("wide", [128, 2048], F32))
        rest = ctx.enter_context(nc.psum_tensor("rest", [128, 2048], F32))

        loaded = sem("loaded")
        chain_done = sem("chain_done")
        proj_done = sem("proj_done")
        bias_added = sem("bias_added")
        x1_ready = sem("x1_ready")
        centred = sem("centred")
        squared = sem("squared")
        var_done = sem("var_done")
        act_chain = sem("act_chain")
        r0_done = sem("r0_done")
        h_ready = sem("h_ready")
        turned = sem("turned")
        hT_ready = sem("hT_ready")
        routed = sem("routed")
        logits_ready = sem("logits_ready")
        top_ready = sem("top_ready")
        exp_done = sem("exp_done")
        sel_ready = sem("sel_ready")
        counted = sem("counted")
        place_ready = sem("place_ready")
        up_done = sem("up_done")
        en_done = sem("en_done")
        gu_done = sem("gu_done")
        down_done = sem("down_done")
        added = sem("added")

        block = ctx.enter_context(nc.Block())
        GROUPS = [(n, min(n + 4, NT)) for n in range(0, NT, 4)]
        STEPS = [(tg, f) for tg in range(len(GROUPS)) for f in range(FC)]

        def rows_of(f):
            return min(128, FS - f * 128)

        @block.sync
        def _(sp):
            for dst, src in (
                (w_route[:], a["Wroute"].rearrange("(c k) e -> k c e", k=128)),
                (before[:], a["before"]),
                (sh.iota[:], a["iota"]),
                (w_sup[:, :, 0, :], a["Wsg"].rearrange("(c k) f -> k c f", k=128)),
                (w_sup[:, :, 1, :], a["Wsu"].rearrange("(c k) f -> k c f", k=128)),
                (w_sdown[:, 0:FC - 1, :], a["Wsd"][0:(FC - 1) * 128].rearrange("(c k) n -> k c n", k=128)),
                (w_sdown[0:rows_of(FC - 1), FC - 1, :], a["Wsd"][(FC - 1) * 128:FS]),
            ):
                sp.dma_start(dst, src).then_inc(loaded, 16)
            sh.load(sp, a, 0, 0)
            sh.load(sp, a, 1, 1)

        @block.gpsimd
        def _(pool):
            pool.tensor_tensor(x[:], x[:], env.bo[:].unsqueeze(1).broadcast_to([128, NT, D]), ALU.add).then_inc(bias_added, 1)
            pool.wait_ge(h_ready, 2)
            pool.tensor_tensor(sh.h_lo[:], h[:], sh.h_hi[:], ALU.subtract).then_inc(h_ready, 1)

        @block.tensor
        def _(pe):
            for n in range(NT):
                o = (wide if n < 8 else rest)[:, (n % 8) * D:(n % 8 + 1) * D]
                for c in range(2):
                    m = pe.matmul(o, env.ctxT[:, c, n * 128:(n + 1) * 128], env.wo[:, c], start=(c == 0), stop=(c == 1))
                if n in (7, NT - 1):
                    m.then_inc(proj_done, 1)
            pe.wait_ge(h_ready, 1)
            for k in range(2 * NT):
                c, n = k // NT, k % NT
                o = (wide if k < 16 else rest)[:, (k % 16) * 128:(k % 16 + 1) * 128]
                m = pe.transpose(o, h[:, n, c * 128:(c + 1) * 128], ident[:])
                if k in (15, 2 * NT - 1):
                    m.then_inc(turned, 1)
            pe.wait_ge(hT_ready, 2)
            pe.wait_ge(loaded, 7 * 16)
            for n in range(NT):
                for c in range(2):
                    m = pe.matmul(rest[:, 1536 + n * (E + 1):1536 + (n + 1) * (E + 1)], hT[:, c, n * 128:(n + 1) * 128],
                                  w_route[:, c], start=(c == 0), stop=(c == 1))
            m.then_inc(routed, 1)

            def up(s):
                tg, f = STEPS[s]
                n0, n1 = GROUPS[tg]
                if s >= 2:
                    pe.wait_ge(gu_done, s - 1)
                r, w = rows_of(f), (n1 - n0) * 128
                for k in range(2):
                    for c in range(2):
                        m = pe.matmul(rest[0:r, (2 * (s % 2) + k) * 512:(2 * (s % 2) + k) * 512 + w],
                                      w_sup[:, c, k, f * 128:f * 128 + r], hT[:, c, n0 * 128:n1 * 128],
                                      start=(c == 0), stop=(c == 1))
                m.then_inc(up_done, 1)

            def down(tg):
                pe.wait_ge(gu_done, FC * (tg + 1))
                n0, n1 = GROUPS[tg]
                for n in range(n0, n1):
                    if n >= 4:
                        pe.wait_ge(added, n - 3)
                    for f in range(FC):
                        r = rows_of(f)
                        m = pe.matmul(wide[:, (n % 4) * 512:(n % 4) * 512 + D], gu[tg % 2][0:r, f, (n - n0) * 128:(n - n0 + 1) * 128],
                                      w_sdown[0:r, f], start=(f == 0), stop=(f == FC - 1))
                    m.then_inc(down_done, 1)

            pe.wait_ge(logits_ready, 1)
            pe.wait_ge(sel_ready, 1)
            for n in range(NT):
                o = wide[:, n * E:(n + 1) * E]
                for m_ in range(n):
                    pe.matmul(o, ones_b[:], sel_b[:, m_], start=(m_ == 0), stop=False)
                m = pe.matmul(o, before_b[:], sel_b[:, n], start=(n == 0), stop=True)
            m.then_inc(counted, 1)
            for tg in range(len(GROUPS)):
                for f in range(FC):
                    up(FC * tg + f)
                if tg == 0:
                    pe.wait_ge(place_ready, 1)
                if tg:
                    down(tg - 1)
            down(len(GROUPS) - 1)

        @block.scalar
        def _(act):
            act.preload_act_table_set("natural_log_exp_and_others")
            act.wait_ge(centred, 1)
            act.activation(sq, h[:], ACT.Square).then_inc(squared, 1)
            act.wait_ge(var_done, 1)
            act.activation(lnv[:], var[:], ACT.Ln).then_inc(act_chain, 1)
            act.wait_ge(act_chain, 1)
            act.activation(rstd[:], lnv[:], ACT.Exp, scale=-0.5).then_inc(r0_done, 1)
            flat = hT[:].rearrange("p c t -> p (c t)")
            for k, (src, w) in enumerate(((wide, 2048), (rest, 1536))):
                act.wait_ge(turned, k + 1)
                act.activation(flat[:, 2048 * k:2048 * k + w], src[:, 0:w], ACT.Copy).then_inc(hT_ready, 1)
            act.wait_ge(top_ready, 1)
            act.activation(wtop[:], wtop[:], ACT.Exp).then_inc(exp_done, 1)
            act.activation(sig[:], logits[:, :, E], ACT.Exp, scale=-1.0).then_inc(exp_done, 1)
            for s, (tg, f) in enumerate(STEPS):
                r, w = rows_of(f), (GROUPS[tg][1] - GROUPS[tg][0]) * 128
                act.wait_ge(up_done, s + 1)
                if s >= 2:
                    act.wait_ge(gu_done, s - 1)
                act.activation(en[s % 2][0:r, 0:w], rest[0:r, 1024 * (s % 2):1024 * (s % 2) + w], ACT.Exp,
                               scale=-1.0).then_inc(en_done, 1)

        @block.vector
        def _(dve):
            step = [0]

            def chain(ins):
                step[0] += 1
                ins.then_inc(chain_done, 1)
                dve.wait_ge(chain_done, step[0])

            dve.wait_ge(bias_added, 1)
            for k, (src, n0, n1) in enumerate(((wide, 0, 8), (rest, 8, NT))):
                dve.wait_ge(proj_done, k + 1)
                ins = dve.tensor_tensor(x[:, n0:n1], x[:, n0:n1], src[:, 0:(n1 - n0) * D].rearrange("p (n d) -> p n d", d=D), ALU.add)
                ins.then_inc(x1_ready, 1)
            dve.wait_ge(x1_ready, 2)
            chain(dve.tensor_reduce(mean_x[:], x[:], AX.X, ALU.add))
            dve.scalar_tensor_tensor(out=h[:], in0=mean_x[:].unsqueeze(2).broadcast_to([128, NT, D]), scalar=-1.0 / D,
                                     in1=x[:], op0=ALU.mult, op1=ALU.add).then_inc(centred, 1)
            dve.wait_ge(squared, 1)
            chain(dve.tensor_reduce(tmp[:], sq, AX.X, ALU.add))
            dve.tensor_scalar(var[:], tmp[:], 1.0 / D, EPS_LN, ALU.mult, ALU.add).then_inc(var_done, 1)
            dve.wait_ge(r0_done, 1)
            chain(dve.tensor_tensor(tmp[:], rstd[:], rstd[:], ALU.mult))
            chain(dve.scalar_tensor_tensor(out=tmp[:], in0=tmp[:], scalar=-0.5, in1=var[:], op0=ALU.mult, op1=ALU.mult))
            chain(dve.scalar_tensor_tensor(out=rstd[:], in0=tmp[:], scalar=1.5, in1=rstd[:], op0=ALU.add, op1=ALU.mult))
            dve.wait_ge(centred, 1)
            dve.tensor_tensor(h[:], h[:], rstd[:].unsqueeze(2).broadcast_to([128, NT, D]), ALU.mult).then_inc(h_ready, 1)
            dve.wait_ge(h_ready, 1)
            dve.tensor_copy(sh.h_hi[:], h[:]).then_inc(h_ready, 1)
            dve.wait_ge(loaded, 7 * 16)
            dve.tensor_copy(before_b[:], before[:])
            chain(dve.memset(ones_b[:], 1.0))

            dve.wait_ge(routed, 1)
            dve.tensor_copy(logits[:], rest[:, 1536:1536 + NT * (E + 1)].rearrange("p (n e) -> p n e", n=NT)).then_inc(logits_ready, 1)
            dve.wait_ge(logits_ready, 1)
            for n in range(NT):
                ins = dve.max(top[:, n], logits[:, n, 0:E])
            chain(ins)
            for n in range(NT):
                ins = dve.max_index(top_at[:, n], top[:, n], logits[:, n, 0:E])
            chain(ins)
            dve.tensor_copy(top_atf[:], top_at[:, :, 0:4]).then_inc(chain_done, 1)
            dve.tensor_tensor(wtop[:], top[:, :, 0:4], top[:, :, 0:1].broadcast_to([128, NT, 4]), ALU.subtract).then_inc(top_ready, 1)
            step[0] += 1
            dve.wait_ge(chain_done, step[0])
            chain(dve.tensor_tensor(onehot[:], sh.iota[:].unsqueeze(1).unsqueeze(1).broadcast_to([128, NT, 4, E]),
                                    top_atf[:].unsqueeze(3).broadcast_to([128, NT, 4, E]), ALU.is_equal))
            chain(dve.tensor_reduce(sel[:], onehot[:].rearrange("p n k e -> p n e k"), AX.X, ALU.add))
            dve.tensor_copy(sel_b[:], sel[:]).then_inc(sel_ready, 1)
            dve.wait_ge(exp_done, 1)
            chain(dve.tensor_reduce(wsum[:], wtop[:], AX.X, ALU.add))
            chain(dve.reciprocal(tmp[:], wsum[:]))
            chain(dve.tensor_tensor(wtop[:], wtop[:], tmp[:].unsqueeze(2).broadcast_to([128, NT, 4]), ALU.mult))
            chain(dve.tensor_tensor(onehot[:], onehot[:], wtop[:].unsqueeze(3).broadcast_to([128, NT, 4, E]), ALU.mult))
            chain(dve.tensor_reduce(w_tok[:], onehot[:].rearrange("p n k e -> p n e k"), AX.X, ALU.add))
            chain(dve.tensor_copy(sh.w_hi[:], w_tok[:]))
            dve.tensor_tensor(sh.w_lo[:], w_tok[:], sh.w_hi[:], ALU.subtract)
            dve.wait_ge(exp_done, 2)
            chain(dve.tensor_scalar(wsum[:], sig[:], 1.0, None, ALU.add))
            chain(dve.reciprocal(sig[:], wsum[:]))
            dve.wait_ge(counted, 1)
            dve.scalar_tensor_tensor(out=sh.place[:], in0=wide[:, 0:NT * E].rearrange("p (n e) -> p n e", e=E), scalar=1.0,
                                     in1=sel[:], op0=ALU.add, op1=ALU.mult).then_inc(place_ready, 1)

            def silu_up(s):
                tg, f = STEPS[s]
                r, w = rows_of(f), (GROUPS[tg][1] - GROUPS[tg][0]) * 128
                g_ps = rest[0:r, 1024 * (s % 2):1024 * (s % 2) + w]
                u_ps = rest[0:r, 1024 * (s % 2) + 512:1024 * (s % 2) + 512 + w]
                e, t = en[s % 2][0:r, 0:w], act_g[s % 2][0:r, 0:w]
                dve.wait_ge(en_done, s + 1)
                chain(dve.tensor_scalar(e, e, 1.0, None, ALU.add))
                chain(dve.reciprocal(t, e))
                chain(dve.tensor_tensor(t, g_ps, t, ALU.mult))
                if f == 0 and tg >= 2:
                    dve.wait_ge(down_done, GROUPS[tg - 2][1])
                dve.tensor_tensor(gu[tg % 2][0:r, f, 0:w], u_ps, t, ALU.mult).then_inc(gu_done, 1)

            def add_shared(tg):
                for n in range(*GROUPS[tg]):
                    dve.wait_ge(down_done, n + 1)
                    dve.scalar_tensor_tensor(out=x[:, n], in0=wide[:, (n % 4) * 512:(n % 4) * 512 + D], scalar=sig[:, n:n + 1],
                                             in1=x[:, n], op0=ALU.mult, op1=ALU.add).then_inc(added, 1)

            for tg in range(len(GROUPS)):
                for f in range(FC):
                    silu_up(FC * tg + f)
                if tg:
                    add_shared(tg - 1)
            add_shared(len(GROUPS) - 1)


def routed_experts(env, sh):
    nc, a = env.nc, env.a
    QN = E // 4
    with ExitStack() as ctx:
        def sb(name, shape, dt=F32):
            return ctx.enter_context(nc.sbuf_tensor("r_" + name, shape, dt))

        def sem(name):
            return ctx.enter_context(nc.semaphore("r_" + name))

        x, ident = env.x, env.ident
        slots = sb("slots", [128, NT, E * CAP], BF16)
        ident_b = sb("ident_b", [128, 128], BF16)
        iota1 = sb("iota1", [128, CAP])
        own = sb("own", [128, QN, E])
        w_all = sb("w_all", [128, QN, 2 * E])
        w_mine = sb("w_mine", [128, QN, 2, E])
        w_slot = sb("w_slot", [128, QN])
        xeT = sb("xeT", [128, 2, E * CAP])
        xg = [sb(f"xg{i}", [128, 2, 128]) for i in range(2)]
        en = sb("en", [128, F])
        t_g = sb("t_g", [128, F])
        gu = sb("gu", [128, F])
        guT = [sb(f"guT{i}", [FH, 2, 128]) for i in range(2)]
        ye = sb("ye", [128, D])
        ye_hi = sb("ye_hi", [128, QN, D], BF16)
        ye_lo = sb("ye_lo", [128, QN, D], BF16)
        slotsT = [sb(f"slotsT{i}", [128, QN, 128], BF16) for i in range(2)]
        gather = ctx.enter_context(nc.psum_tensor("gather", [128, 2, E * CAP], F32))
        up_ps = ctx.enter_context(nc.psum_tensor("up_ps", [128, 512], F32))
        turn_ps = ctx.enter_context(nc.psum_tensor("turn_ps", [128, 512], F32))
        down_ps = ctx.enter_context(nc.psum_tensor("down_ps", [128, 512], F32))
        w_ps_flat = ctx.enter_context(nc.psum_tensor("w_ps", [128, QN * 2 * E], F32))
        w_ps = w_ps_flat[:].rearrange("p (q k) -> p q k", q=QN)

        loaded = sem("loaded")
        chain_done = sem("chain_done")
        slots_ready = sem("slots_ready")
        gathered = sem("gathered")
        xeT_ready = sem("xeT_ready")
        w_slot_ready = sem("w_slot_ready")
        xg_ready = sem("xg_ready")
        up_done = sem("up_done")
        en_done = sem("en_done")
        gu_chain = sem("gu_chain")
        gu_ready = sem("gu_ready")
        turned = sem("turned")
        guT_ready = sem("guT_ready")
        down_done = sem("down_done")
        ye_chain = sem("ye_chain")
        ye_ready = sem("ye_ready")
        st_turned = sem("st_turned")
        st_ready = sem("st_ready")
        combined = sem("combined")
        out_ready = sem("out_ready")
        stored = sem("stored")

        block = ctx.enter_context(nc.Block())
        x_out = env.out.rearrange("b s d -> (b s) d").rearrange("(n p) d -> p n d", p=128)

        @block.sync
        def _(sp):
            sp.dma_start(own[:].rearrange("p q e -> p (q e)"), a["own"]).then_inc(loaded, 16)
            with sp.Fori(0, QN // 2 - 1) as i:
                for par in range(2):
                    sp.wait_ge(down_done, 2 * i + par + 1)
                    sh.load(sp, a, 2 * i + par + 2, par)
            for n in range(NT):
                sp.wait_ge(out_ready, n + 1)
                sp.dma_start(x_out[:, n], x[:, n]).then_inc(stored, 16)
            sp.wait_ge(stored, 16 * NT)

        @block.gpsimd
        def _(pool):
            pool.wait_ge(xeT_ready, 4)

            def fetch(q, par):
                src = xeT[:, :, q * 128:(q + 1) * 128] if isinstance(q, int) else xeT[:, :, bass.ds(q * 128, 128)]
                pool.tensor_copy(xg[par][:], src).then_inc(xg_ready, 1)

            fetch(0, 0)
            fetch(1, 1)
            with pool.Fori(0, QN // 2 - 1) as i:
                for par in range(2):
                    pool.wait_ge(up_done, 2 * i + par + 1)
                    fetch(2 * i + par + 2, par)

        @block.tensor
        def _(pe):
            for n in range(NT):
                pe.wait_ge(slots_ready, n + 1)
                for c in range(2):
                    for part, hp in enumerate((sh.h_hi, sh.h_lo)):
                        for k in range(2):
                            m = pe.matmul(gather[:, c, k * 512:(k + 1) * 512], hp[:, n, c * 128:(c + 1) * 128],
                                          slots[:, n, k * 512:(k + 1) * 512], start=(n == 0 and part == 0),
                                          stop=(n == NT - 1 and part == 1))
                for q in range(QN):
                    for part, wp in enumerate((sh.w_hi, sh.w_lo)):
                        m = pe.matmul(w_ps[:, q, part * E:(part + 1) * E], slots[:, n, q * 128:(q + 1) * 128], wp[:, n],
                                      start=(n == 0 and q == 0 and part == 0), stop=(n == NT - 1), skip_group_check=True)
            m.then_inc(gathered, 1)

            def group(q, par, n_loads):
                pe.wait_ge(xg_ready, q + 1)
                pe.wait_ge(sh.loaded[par], n_loads)
                if not isinstance(q, int) or q > 0:
                    pe.wait_ge(gu_ready, q)
                for e in range(4):
                    for c in range(2):
                        m = pe.matmul(up_ps[32 * e:32 * e + 32, 0:2 * F], xg[par][:, c, 32 * e:32 * e + 32],
                                      sh.w_up[par][:, c, e], start=(c == 0), stop=(c == 1))
                m.then_inc(up_done, 1)
                pe.wait_ge(gu_ready, q + 1)
                for k in range(2):
                    m = pe.transpose(turn_ps[0:FH, k * 128:(k + 1) * 128], gu[:, k * FH:(k + 1) * FH], ident[:])
                m.then_inc(turned, 1)
                pe.wait_ge(guT_ready, q + 1)
                if not isinstance(q, int) or q > 0:
                    pe.wait_ge(ye_chain, 2 * q)
                for e in range(4):
                    for k in range(2):
                        m = pe.matmul(down_ps[32 * e:32 * e + 32, 0:D], guT[par][:, k, 32 * e:32 * e + 32],
                                      sh.w_down[par][:, k, e], start=(k == 0), stop=(k == 1))
                m.then_inc(down_done, 1)

            group(0, 0, LOADS)
            with pe.Fori(0, QN // 2 - 1) as i:
                group(2 * i + 1, 1, LOADS * i + LOADS)
                group(2 * i + 2, 0, LOADS * i + 2 * LOADS)
            group(QN - 1, 1, QN // 2 * LOADS)

            st = [turn_ps[:].bitcast(BF16), up_ps[:].bitcast(BF16)]
            out_ps = [down_ps, w_ps_flat]
            pe.wait_ge(ye_ready, QN)
            for n in range(NT + 1):
                if n < NT:
                    if n >= 2:
                        pe.wait_ge(st_ready, n - 1)
                    for q in range(QN):
                        m = pe.transpose(st[n % 2][:, q * 128:(q + 1) * 128], slots[:, n, q * 128:(q + 1) * 128], ident_b[:])
                    m.then_inc(st_turned, 1)
                if n >= 1:
                    k = n - 1
                    pe.wait_ge(st_ready, k + 1)
                    if k >= 2:
                        pe.wait_ge(out_ready, k - 1)
                    for q in range(QN):
                        for part, yp in enumerate((ye_hi, ye_lo)):
                            m = pe.matmul(out_ps[k % 2][:, 0:D], slotsT[k % 2][:, q], yp[:, q],
                                          start=(q == 0 and part == 0), stop=(q == QN - 1 and part == 1))
                    m.then_inc(combined, 1)

        @block.scalar
        def _(act):
            act.preload_act_table_set("natural_log_exp_and_others")
            act.wait_ge(gathered, 1)
            for c in range(2):
                for k in range(2):
                    act.activation(xeT[:, c, k * 512:(k + 1) * 512], gather[:, c, k * 512:(k + 1) * 512], ACT.Copy).then_inc(xeT_ready, 1)

            def group(q, par):
                act.wait_ge(up_done, q + 1)
                act.activation(en[:], up_ps[:, 0:F], ACT.Exp, scale=-1.0).then_inc(en_done, 1)
                act.wait_ge(turned, q + 1)
                act.activation(guT[par][:].rearrange("p k t -> p (k t)"), turn_ps[0:FH, 0:256], ACT.Copy).then_inc(guT_ready, 1)

            with act.Fori(0, QN // 2) as i:
                group(2 * i, 0)
                group(2 * i + 1, 1)
            st = [turn_ps[:].bitcast(BF16), up_ps[:].bitcast(BF16)]
            for n in range(NT):
                act.wait_ge(st_turned, n + 1)
                if n >= 2:
                    act.wait_ge(combined, n - 1)
                act.activation(slotsT[n % 2][:].rearrange("p q t -> p (q t)"), st[n % 2], ACT.Copy).then_inc(st_ready, 1)

        @block.vector
        def _(dve):
            step = [0]

            def chain(ins):
                step[0] += 1
                ins.then_inc(chain_done, 1)
                dve.wait_ge(chain_done, step[0])

            dve.tensor_copy(ident_b[:], ident[:])
            chain(dve.tensor_scalar(iota1[:], sh.iota[:, 0:CAP], 1.0, None, ALU.add))
            for n in range(NT):
                dve.tensor_tensor(slots[:, n].rearrange("p (e c) -> p e c", c=CAP),
                                  iota1[:].unsqueeze(1).broadcast_to([128, E, CAP]),
                                  sh.place[:, n].unsqueeze(2).broadcast_to([128, E, CAP]), ALU.is_equal).then_inc(slots_ready, 1)
            dve.wait_ge(gathered, 1)
            dve.wait_ge(loaded, 16)
            chain(dve.tensor_tensor(w_mine[:], w_ps.rearrange("p q (k e) -> p q k e", k=2),
                                    own[:].unsqueeze(2).broadcast_to([128, QN, 2, E]), ALU.mult))
            chain(dve.tensor_reduce(w_slot[:], w_mine[:].rearrange("p q k e -> p q (k e)"), AX.X, ALU.add))

            def group(q):
                dve.wait_ge(en_done, q + 1)
                dve.tensor_scalar(en[:], en[:], 1.0, None, ALU.add).then_inc(gu_chain, 1)
                dve.wait_ge(gu_chain, 3 * q + 1)
                dve.reciprocal(t_g[:], en[:]).then_inc(gu_chain, 1)
                dve.wait_ge(gu_chain, 3 * q + 2)
                dve.tensor_tensor(t_g[:], up_ps[:, 0:F], t_g[:], ALU.mult).then_inc(gu_chain, 1)
                dve.wait_ge(gu_chain, 3 * q + 3)
                dve.tensor_tensor(gu[:], up_ps[:, F:2 * F], t_g[:], ALU.mult).then_inc(gu_ready, 1)
                dve.wait_ge(down_done, q + 1)
                w = w_slot[:, q:q + 1] if isinstance(q, int) else w_slot[:, bass.ds(q, 1)]
                dve.tensor_tensor(ye[:], down_ps[:, 0:D], w.broadcast_to([128, D]), ALU.mult).then_inc(ye_chain, 1)
                dve.wait_ge(ye_chain, 2 * q + 1)

                def at(t):
                    return t[:, q] if isinstance(q, int) else t[:, bass.ds(q, 1)].rearrange("p o d -> p (o d)")
                dve.tensor_copy(at(ye_hi), ye[:]).then_inc(ye_chain, 1)
                dve.wait_ge(ye_chain, 2 * q + 2)
                dve.tensor_tensor(at(ye_lo), ye[:], at(ye_hi), ALU.subtract).then_inc(ye_ready, 1)

            with dve.Fori(0, QN // 2) as i:
                group(2 * i)
                group(2 * i + 1)
            out_ps = [down_ps, w_ps_flat]
            for n in range(NT):
                dve.wait_ge(combined, n + 1)
                dve.tensor_tensor(x[:, n], x[:, n], out_ps[n % 2][:, 0:D], ALU.add).then_inc(out_ready, 1)


def kernel(**inputs):
    import concourse.bacc as bacc
    from concourse.bass_utils import run_bass_kernel_spmd

    pre = "L0_xattn_"
    f = {k: np.ascontiguousarray(v) for k, v in inputs.items()}

    def rows(*names):
        return np.ascontiguousarray(np.broadcast_to(np.concatenate([f[pre + n] for n in names])[None], (128, sum(f[pre + n].size for n in names))))

    kvb = np.concatenate([f[pre + "bk"], f[pre + "bv"]]).reshape(H, 2, HD).transpose(1, 0, 2).reshape(1, -1)
    arrays = {
        "x": f["x"], "ctx": f["ctx_1024"],
        "Wq": f[pre + "Wq"], "Wk": f[pre + "Wk"], "Wv": f[pre + "Wv"], "Wkv_dca": f[pre + "Wkv_dca"], "Wo": f[pre + "Wo"],
        "bq_rows": rows("bq"), "bo_rows": rows("bo"), "bkv_dca_rows": rows("bkv_dca"),
        "bkv_rows": np.ascontiguousarray(np.broadcast_to(kvb, (128, 2 * D))),
        "ln_cols": np.ascontiguousarray(np.tile(np.stack([f[pre + n] for n in (
            "qn_w", "qn_b", "kn_w", "kn_b", "kn_dca_w", "kn_dca_b")], 1), (128 // HD, 1))),
        "ident": np.eye(128, dtype=np.float32),
        "fold": np.tile(np.eye(S1, dtype=np.float32), (2, 1)),
    }
    p = np.arange(128)
    arrays["before"] = (p[:, None] < p[None, :]).astype(np.float32)
    arrays["iota"] = np.tile(np.arange(E, dtype=np.float32), (128, 1))
    arrays["own"] = (4 * np.arange(E // 4)[None, :, None] + p[:, None, None] // CAP == np.arange(E)).astype(
        np.float32).reshape(128, -1)
    arrays["pair_masks"] = np.stack([p // HD % 2 == 0, p // HD % 2 == 1, p < S1, (p >= S1) & (p < PR)], 1).astype(np.float32)
    arrays["Wroute"] = np.concatenate([f["L0_ffn_Wr"], f["L0_ffn_Wse"]], 1)
    for n in ("Wg", "Wu", "Wd", "Wsg", "Wsu", "Wsd"):
        arrays[n] = f["L0_ffn_" + n]

    nc = bacc.Bacc("TRN2", target_bir_lowering=False, num_devices=1)
    aps, feed = {}, {}
    for name, arr in arrays.items():
        feed[f"in_{name}_dram"] = arr
        aps[name] = nc.dram_tensor(f"in_{name}_dram", arr.shape, mybir.dt.from_np(arr.dtype), kind="ExternalInput").ap()
    out = nc.dram_tensor("out_0_dram", (B, S1, D), F32, kind="ExternalOutput").ap()
    program(nc, aps, out)
    r = run_bass_kernel_spmd(nc, [feed], core_ids=[0])
    return r.results[0]["out_0_dram"]
```

```python
from contextlib import ExitStack

import numpy as np
import concourse.bass as bass
from concourse import mybir

F32 = mybir.dt.float32
BF16 = mybir.dt.bfloat16
U32 = mybir.dt.uint32
ALU = mybir.AluOpType
ACT = mybir.ActivationFunctionType
AX = mybir.AxisListType

B, S1, D = 32, 56, 256
SK, DY = 1500, 128
DCA = 16
H, HD = 16, 16
G = 2
T = B * S1
NT = T // 128
MAIN = SK - DCA
KT = 12
REST = MAIN - (KT - 1) * 128
DROW = 96
DCOL = (KT - 1) * 128 + DROW
KW = DCOL + DCA
PAIRS = H // 2
PR = 2 * S1
SLOT = 1536
E, CAP = 32, 32
F, FH = 176, 88
FS, FC = 704, 6
EPS_ATTN, EPS_LN = 1e-6, 1e-5
SCALE = HD ** -0.5


class Slots:
    PROLOGUE = ["Y", "KV0", "KV1", "KV2", "KV3", "KT0", "KT1", "Y'", "KV0'", "KV1'", "KV2'", "KV3'"]
    BODY = ["P0", "P1", "KT0", "KT1", "P2", "P3", "Y", "KV0", "P4", "KV1", "KV2", "P5", "P6", "KV3", "P7"]
    SLOT_OF = dict(P0=0, P1=1, KT0=0, KT1=1, P2=0, P3=1, Y=0, KV0=1, P4=0, KV1=1, KV2=0, P5=1, P6=0, KV3=1, P7=0)
    FULL, KEYS, LAST = range(3)

    @classmethod
    def units(cls, kind):
        return [u for u in cls.BODY if u[0] == "P" or (u[:2] == "KT" and kind < cls.LAST) or kind == cls.FULL]

    @classmethod
    def count(cls, names, s):
        return sum(cls.SLOT_OF[u.rstrip("'")] == s for u in names)

    @classmethod
    def prologue(cls, unit):
        s = cls.SLOT_OF[unit.rstrip("'")]
        return s, cls.count(cls.PROLOGUE[:cls.PROLOGUE.index(unit)], s)

    @classmethod
    def body(cls, unit, b, kind=0):
        s = cls.SLOT_OF[unit]
        n = cls.count(cls.PROLOGUE, s) + cls.count(cls.units(kind)[:cls.units(kind).index(unit)], s)
        if kind == cls.FULL:
            return s, n + cls.count(cls.BODY, s) * b
        n += cls.count(cls.BODY, s) * (B - 2)
        return s, n + (cls.count(cls.units(cls.KEYS), s) if kind == cls.LAST else 0)


def program(nc, a, out, stage="all"):
    with ExitStack() as ctx:
        env = Env(nc, a, out, ctx)
        with ExitStack() as part:
            shared = AttentionShared(env, part)
            project_queries(env, shared)
            attention(env, shared)
        if stage == "attn":
            dump_x1(env)
        else:
            feed_forward(env)


class Env:

    def __init__(self, nc, a, out, ctx):
        self.nc, self.a, self.out = nc, a, out
        self.sb = lambda name, shape, dt=F32: ctx.enter_context(nc.sbuf_tensor(name, shape, dt))
        self.ctxT = self.sb("ctxT", [128, G, T])
        self.ident = self.sb("ident", [128, 128])


class AttentionShared:

    def __init__(self, env, ctx):
        def sb(name, shape, dt=F32):
            return ctx.enter_context(env.nc.sbuf_tensor(name, shape, dt))
        self.wkv = [sb("wkv", [128, 2, H, HD]), sb("wkv_dca", [128, 2, H, HD])]
        self.bkv = [sb("bkv", [128, 2, H, HD]), sb("bkv_dca", [128, 2, H, HD])]
        self.bias_last = sb("bias_last", [128, 2, H, HD])
        self.ln_cols = sb("ln_cols", [128, 8])
        self.pair_row = sb("pair_row", [128, 2])
        self.pair_out = sb("pair_out", [128, 2])
        self.fold = sb("fold", [128, S1])
        self.qT = sb("qT", [128, G, T])


def project_queries(env, sh):
    nc, a = env.nc, env.a
    with ExitStack() as ctx:
        def sb(name, shape, dt=F32):
            return ctx.enter_context(nc.sbuf_tensor("q_" + name, shape, dt))

        def sem(name):
            return ctx.enter_context(nc.semaphore("q_" + name))

        ident = env.ident
        x = sb("x", [128, NT, D])
        wkv, bkv, ln_cols = sh.wkv, sh.bkv, sh.ln_cols
        wq = sb("wq", [128, 2, H, HD])
        bq = sb("bq", [128, H, HD])
        means = sb("means", [128, 7, H])
        xn = sb("xn", [128, NT, D])
        sqx = sb("sqx", [128, NT, D])
        xnT = sb("xnT", [128, G * T])
        q = sb("q", [128, NT, H, HD])
        mean_x = sb("mean_x", [128, NT])
        var = [sb("var_x", [128, NT]), sb("var_q", [128, NT * H])]
        lnv = [sb("lnv_x", [128, NT]), sb("lnv_q", [128, NT * H])]
        rstd = [sb("rstd_x", [128, NT]), sb("rstd_q", [128, NT * H])]
        tmp = [sb("tmp_x", [128, NT]), sb("tmp_q", [128, NT * H])]
        slot = [ctx.enter_context(nc.psum_tensor(f"qslot{i}", [128, SLOT], F32)) for i in range(2)]

        x_loaded, consts_loaded = sem("x_loaded"), sem("consts_loaded")
        chain_done = sem("chain_done")
        centred = sem("centred")
        squared = sem("squared")
        var_done = sem("var_done")
        ln_done = sem("ln_done")
        r0_done = sem("r0_done")
        normed = sem("normed")
        w_ready = sem("w_ready")
        full = sem("full")
        free = sem("free")

        block = ctx.enter_context(nc.Block())

        def cols(i):
            return min(12, G * NT - 12 * i) * 128

        @block.sync
        def _(sp):
            sp.dma_start(x[:], a["x"].rearrange("b s d -> (b s) d").rearrange("(n p) d -> p n d", p=128)).then_inc(x_loaded, 16)

            def const(dst, src):
                sp.dma_start(dst, src).then_inc(consts_loaded, 16)
            for half, name in enumerate(("Wk", "Wv")):
                hs = slice(half * H // 2, (half + 1) * H // 2)
                src = a[name].rearrange("k (h a d) -> k a h d", a=2, d=HD)
                for part in range(2):
                    const(wkv[0][:, part, hs, :], src[:, part])
            const(wkv[1][:], a["Wkv_dca"].rearrange("k (a h d) -> k a h d", a=2, d=HD))
            const(wq[:], a["Wq"].rearrange("(c k) (h d) -> k c h d", k=128, d=HD))
            const(bkv[0][:].rearrange("p a h d -> p (a h d)"), a["bkv_rows"])
            const(bkv[1][:].rearrange("p a h d -> p (a h d)"), a["bkv_dca_rows"])
            const(bq[:].rearrange("p h d -> p (h d)"), a["bq_rows"])
            const(ln_cols[:, 0:6], a["ln_cols"])
            const(ident[:], a["ident"])
            const(sh.pair_row[:], a["pair_masks"][:, 0:2])
            const(sh.pair_out[:], a["pair_masks"][:, 2:4])
            const(sh.fold[0:PR, :], a["fold"])

        N_CONSTS = 14

        @block.tensor
        def _(pe):
            pe.wait_ge(consts_loaded, 16 * N_CONSTS)

            def turn(unit, src):
                if unit >= 2:
                    pe.wait_ge(free, unit - 1)
                for k in range(12 * (unit % 3), min(12 * (unit % 3) + 12, G * NT)):
                    g, n = k // NT, k % NT
                    m = pe.transpose(slot[unit % 2][:, (k % 12) * 128:(k % 12) * 128 + 128], src(n, g), ident[:])
                m.then_inc(full, 1)

            pe.wait_ge(normed, 1)
            for unit in range(3):
                turn(unit, lambda n, g: xn[:, n, g * 128:(g + 1) * 128])
            pe.wait_ge(w_ready, 1)
            for unit in range(3, 6):
                pe.wait_ge(free, 3 if unit == 3 else unit - 1)
                for n in range(6 * (unit - 3), min(6 * (unit - 3) + 6, NT)):
                    for c in range(G):
                        m = pe.matmul(slot[unit % 2][:, (n % 6) * D:(n % 6 + 1) * D],
                                      xnT[:, c * T + n * 128:c * T + (n + 1) * 128],
                                      wq[:, c].rearrange("p h d -> p (h d)"), start=(c == 0), stop=(c == 1))
                m.then_inc(full, 1)
            pe.wait_ge(normed, 2)
            for unit in range(6, 9):
                turn(unit, lambda n, g: q[:, n, g * 8:(g + 1) * 8, :].rearrange("p h d -> p (h d)"))

        @block.scalar
        def _(act):
            act.preload_act_table_set("natural_log_exp_and_others")

            def rstd_start(k, src, dst):
                act.wait_ge(centred, k + 1)
                act.activation(dst, src, ACT.Square).then_inc(squared, 1)
                act.wait_ge(var_done, k + 1)
                act.activation(lnv[k][:], var[k][:], ACT.Ln).then_inc(ln_done, 1)
                act.wait_ge(ln_done, k + 1)
                act.activation(rstd[k][:], lnv[k][:], ACT.Exp, scale=-0.5).then_inc(r0_done, 1)

            rstd_start(0, xn[:], sqx[:])
            for unit in range(3):
                act.wait_ge(full, unit + 1)
                act.activation(xnT[:, unit * SLOT:unit * SLOT + cols(unit)], slot[unit % 2][:, 0:cols(unit)],
                               ACT.Copy).then_inc(free, 1)
            rstd_start(1, q[:].rearrange("p n h d -> p n (h d)"), sqx[:])
            act.wait_ge(w_ready, 1)
            for unit in range(6, 9):
                c0, n = (unit - 6) * SLOT, cols(unit - 6)
                act.wait_ge(full, unit + 1)
                act.activation(sh.qT[:].rearrange("p c t -> p (c t)")[:, c0:c0 + n], slot[unit % 2][:, 0:n],
                               ACT.Identity, scale=ln_cols[:, 6:7], bias=ln_cols[:, 7:8]).then_inc(free, 1)

        @block.vector
        def _(dve):
            step = [0]

            def chain(ins):
                step[0] += 1
                ins.then_inc(chain_done, 1)
                dve.wait_ge(chain_done, step[0])

            def normalise(k, sq, n, eps, values):
                dve.wait_ge(squared, k + 1)
                chain(dve.tensor_reduce(tmp[k][:], sq, AX.X, ALU.add))
                dve.tensor_scalar(var[k][:], tmp[k][:], 1.0 / n, eps, ALU.mult, ALU.add).then_inc(var_done, 1)
                r, t = rstd[k][:], tmp[k][:]
                dve.wait_ge(r0_done, k + 1)
                chain(dve.tensor_tensor(t, r, r, ALU.mult))
                chain(dve.scalar_tensor_tensor(out=t, in0=t, scalar=-0.5, in1=var[k][:], op0=ALU.mult, op1=ALU.mult))
                chain(dve.scalar_tensor_tensor(out=r, in0=t, scalar=1.5, in1=r, op0=ALU.add, op1=ALU.mult))
                dve.tensor_tensor(values, values, r.unsqueeze(2).broadcast_to([128, r.shape[1], n]),
                                  ALU.mult).then_inc(normed, 1)

            dve.wait_ge(x_loaded, 16)
            chain(dve.tensor_reduce(mean_x[:], x[:], AX.X, ALU.add))
            dve.scalar_tensor_tensor(out=xn[:], in0=mean_x[:].unsqueeze(2).broadcast_to([128, NT, D]), scalar=-1.0 / D,
                                     in1=x[:], op0=ALU.mult, op1=ALU.add).then_inc(centred, 1)
            dve.wait_ge(consts_loaded, 16 * N_CONSTS)
            mats = [wkv[0][:, 0], wkv[1][:, 0], bkv[0][:, 0], bkv[1][:, 0], wq[:, 0], wq[:, 1], bq[:]]
            for k, w in enumerate(mats):
                last = dve.tensor_reduce(means[:, k, :], w, AX.X, ALU.add)
            chain(last)
            for k, w in enumerate(mats):
                last = dve.scalar_tensor_tensor(out=w, in0=means[:, k, :].unsqueeze(2).broadcast_to([128, H, HD]),
                                                scalar=-1.0 / HD, in1=w, op0=ALU.mult, op1=ALU.add)
            chain(last)
            dve.tensor_copy(sh.bias_last[0:DROW], bkv[0][0:DROW])
            dve.tensor_copy(sh.bias_last[DROW:], bkv[1][DROW:])
            dve.tensor_scalar(ln_cols[:, 6:8], ln_cols[:, 0:2], SCALE, None, ALU.mult).then_inc(w_ready, 1)

            dve.wait_ge(centred, 1)
            normalise(0, sqx[:], D, EPS_LN, xn[:])
            for unit in range(3, 6):
                n0, n1 = 6 * (unit - 3), min(6 * (unit - 3) + 6, NT)
                dve.wait_ge(full, unit + 1)
                ins = dve.tensor_tensor(q[:, n0:n1].rearrange("p n h d -> p n (h d)"),
                                        slot[unit % 2][:, 0:(n1 - n0) * D].rearrange("p (n f) -> p n f", f=D),
                                        bq[:].rearrange("p h d -> p (h d)").unsqueeze(1).broadcast_to([128, n1 - n0, D]),
                                        ALU.add)
                ins.then_inc(free, 1)
            dve.wait_ge(free, 6)
            dve.memset(mean_x[:], 0.0).then_inc(centred, 1)
            normalise(1, sqx[:].rearrange("p n (h d) -> p (n h) d", d=HD), HD, EPS_ATTN,
                      q[:].rearrange("p n h d -> p (n h) d"))



def attention(env, sh):
    nc, a = env.nc, env.a
    with ExitStack() as ctx:
        def sb(name, shape, dt=F32):
            return ctx.enter_context(nc.sbuf_tensor("a_" + name, shape, dt))

        def sem(name):
            return ctx.enter_context(nc.semaphore("a_" + name))

        ident = env.ident
        wkv, bkv, bias_last, ln_cols = sh.wkv, sh.bkv, sh.bias_last, sh.ln_cols
        pair_row, pair_out, fold, qT = sh.pair_row, sh.pair_out, sh.fold, sh.qT
        q_mask = sb("q_mask", [128, G, 2, S1])
        q_parts = sb("q_parts", [128, 2, G, PR], BF16)
        q_pack = [sb(f"q_pack{i}", [128, PAIRS, PR], BF16) for i in range(2)]
        kf = sb("kf", [128, KW])
        k_parts = [sb(f"k_parts{i}", [128, 2, KW], BF16) for i in range(G)]
        k_pack = [sb(f"k_pack{i}", [128, PAIRS, KW], BF16) for i in range(2)]
        y = sb("y", [128, KT, DY])
        yT = sb("yT", [128, SLOT])
        kv = sb("kv", [128, KT, 2 * D])
        sq = [sb(f"sq{i}", [128, 3, D]) for i in range(2)]
        var = sb("var", [128, KT * H])
        rstd = sb("rstd", [128, KT * H])
        newt = sb("newt", [128, KT * H])
        vals = [sb(f"vals{i}", [128, KT, PAIRS, 64], BF16) for i in range(2)]
        P = [sb(f"P{i}", [128, SLOT]) for i in range(2)]
        pt = [sb(f"pt{i}", [128, KT * PR + 16]) for i in range(2)]
        pt_lo = [sb(f"pt_lo{i}", [128, KT * PR + 16], BF16) for i in range(2)]
        negmax = sb("negmax", [128, PAIRS])
        negmax_dca = sb("negmax_dca", [128, PAIRS])
        total = [sb(f"total{i}", [128, PAIRS]) for i in range(2)]
        total_dca = sb("total_dca", [128, PAIRS])
        rtotal_dca = sb("rtotal_dca", [128, PAIRS])
        rtotal = sb("rtotal", [128, PAIRS])
        coef = sb("coef", [128, PAIRS, 2])
        o_hi = sb("o_hi", [128, D])
        o_lo = sb("o_lo", [128, D])

        slot = [ctx.enter_context(nc.psum_tensor(f"slot{i}", [128, SLOT], F32)) for i in range(2)]
        pt_ps = ctx.enter_context(nc.psum_tensor("pt_ps", [128, 512], F32))
        acc = ctx.enter_context(nc.psum_tensor("acc", [128, PAIRS, 64], F32))

        slot_full = [sem("slot_full0"), sem("slot_full1")]
        slot_free = [sem("slot_free0"), sem("slot_free1")]
        y_loaded = sem("y_loaded")
        zeroed = sem("zeroed")
        q_chain = sem("q_chain")
        q_ready = sem("q_ready")
        q_loaded = [sem("q_loaded0"), sem("q_loaded1")]
        kf_ready = sem("kf_ready")
        khi_ready = sem("khi_ready")
        klo_ready = sem("klo_ready")
        k_loaded = [[sem(f"k_loaded{i}{g}") for g in range(G)] for i in range(2)]
        max_ready = sem("max_ready")
        dca_ready = sem("dca_ready")
        dca_chain = sem("dca_chain")
        pt_full = sem("pt_full")
        pt_free = sem("pt_free")
        lo_done = sem("lo_done")
        pv_done = sem("pv_done")
        sq_done = sem("sq_done")
        ss_done = sem("ss_done")
        vhi_done = sem("vhi_done")
        vlo_done = sem("vlo_done")
        var_ready = sem("var_ready")
        ln_done = sem("ln_done")
        r0_ready = sem("r0_ready")
        newton = sem("newton")
        kn_ready = sem("kn_ready")
        o_chain = sem("o_chain")

        block = ctx.enter_context(nc.Block())
        PT_USES = 3 * PAIRS + 1
        PTW = 4 * PR

        def bcast_bias(ap, n):
            return ap[:].rearrange("p a h d -> p (a h d)").unsqueeze(1).broadcast_to([128, n, 2 * D])

        PACKS = 16 * 16

        @block.sync
        def _(sp):
            def load_y(b):
                sp.dma_start(y[:, 0:KT - 1, :], a["ctx"][b, 0:(KT - 1) * 128, :].rearrange("(p t) d -> p t d", p=128)).then_inc(y_loaded, 16)
                sp.dma_start(y[0:REST, KT - 1, :], a["ctx"][b, (KT - 1) * 128:MAIN, :]).then_inc(y_loaded, 16)
                sp.dma_start(y[DROW:DROW + DCA, KT - 1, :], a["ctx"][b, MAIN:SK, :]).then_inc(y_loaded, 16)

            def after_y(use):
                sp.wait_ge(slot_full[use[0]], use[1] + 1)

            def pack_q(n, par):
                sp.wait_ge(q_ready, n + 1)
                for block_, part in enumerate((0, 0, 1, 1)):
                    for jj in range(4):
                        sp.dma_start(q_pack[par][32 * block_:32 * block_ + 32, jj::4, :],
                                     q_parts[32 * jj:32 * jj + 32, part]).then_inc(q_loaded[par], 16)

            def pack_k(n, g, par):
                sp.wait_ge(khi_ready, 2 * n + g + 1)
                sp.wait_ge(klo_ready, 2 * n + g + 1)
                for block_, part in enumerate((0, 1, 0, 1)):
                    for jj in range(4):
                        sp.dma_start(k_pack[par][32 * block_:32 * block_ + 32, 4 * g + jj, :],
                                     k_parts[g][32 * jj:32 * jj + 32, part, :]).then_inc(k_loaded[par][g], 16)

            sp.wait_ge(zeroed, 1)
            load_y(0)
            after_y(Slots.prologue("Y"))
            load_y(1)
            pack_q(0, 0)
            for g in range(G):
                pack_k(0, g, 0)
            after_y(Slots.prologue("Y'"))
            load_y(2)

            def batch(b, par, load, kind=Slots.FULL):
                pack_q(b + 1, 1 - par)
                for g in range(G):
                    pack_k(b + 1, g, 1 - par)
                if load:
                    after_y(Slots.body("Y", b))
                    load_y(b + 3)

            batch(0, 0, True)
            with sp.Fori(0, (B - 4) // 2) as i:
                batch(2 * i + 1, 1, True)
                batch(2 * i + 2, 0, True)
            batch(B - 3, 1, False)
            batch(B - 2, 0, False)

        @block.tensor
        def _(pe):
            def put(use):
                sl, n = use
                if not (isinstance(n, int) and n == 0):
                    pe.wait_ge(slot_free[sl], n)
                return slot[sl]

            def unit_y(use, n):
                ps = put(use)
                pe.wait_ge(y_loaded, 48 * (n + 1))
                for t in range(KT):
                    m = pe.transpose(ps[:, t * 128:t * 128 + 128], y[:, t, :], ident[:])
                m.then_inc(slot_full[use[0]], 1)

            def unit_kv(use, u, y_use):
                ps = put(use)
                if u == 0:
                    pe.wait_ge(slot_free[y_use[0]], y_use[1] + 1)
                w = [wkv[k][:].rearrange("p a h d -> p (a h d)") for k in range(2)]
                for k in range(3):
                    t = 3 * u + k
                    o = ps[:, k * 512:(k + 1) * 512]
                    if t < KT - 1:
                        m = pe.matmul(o, yT[:, t * 128:(t + 1) * 128], w[0], start=True, stop=True)
                    else:
                        pe.matmul(o[0:DROW], yT[:, t * 128:t * 128 + DROW], w[0], start=True, stop=True)
                        m = pe.matmul(o[DROW:DROW + DCA], yT[:, DCOL:DCOL + DCA], w[1], start=True, stop=True)
                m.then_inc(slot_full[use[0]], 1)

            def unit_kt(use, g, n_kn):
                ps = put(use)
                pe.wait_ge(kn_ready, n_kn)
                for t in range(KT):
                    m = pe.transpose(ps[:, t * 128:t * 128 + 128], kv[:, t, g * 128:(g + 1) * 128], ident[:])
                m.then_inc(slot_full[use[0]], 1)

            def unit_p(use, j, par):
                ps = put(use)
                for c0 in range(0, KW, 512):
                    c1 = min(c0 + 512, KW)
                    m = pe.matmul(ps[0:PR, c0:c1], q_pack[par][:, j, :], k_pack[par][:, j, c0:c1], start=True, stop=True)
                m.then_inc(slot_full[use[0]], 1)

            def pt_put(n):
                if not isinstance(n, int) or n >= 1:
                    pe.wait_ge(pt_free, n)

            def turn(b, j, h):
                pt_put(PT_USES * b + 3 * j + h)
                for k in range(4):
                    t = 4 * h + k
                    m = pe.transpose(pt_ps[:, k * PR:(k + 1) * PR], P[j % 2][0:PR, t * 128:(t + 1) * 128],
                                     ident[0:PR, 0:PR])
                m.then_inc(pt_full, 1)

            def pv(b, j, h, par):
                if h == 0:
                    pe.wait_ge(pt_free, PT_USES * b + 3 * j + 3)
                    if j == 0:
                        if not isinstance(b, int) or b > 0:
                            pe.wait_ge(o_chain, 5 * b)
                        pe.wait_ge(vhi_done, b + 1)
                        pe.wait_ge(vlo_done, 4 * b + 4)
                pe.wait_ge(lo_done, 3 * PAIRS * b + 3 * j + min(h + 2, 3))
                hi = pt[j % 2][:].bitcast(BF16)[:, 1::2]
                for k in range(4):
                    t = 4 * h + k
                    rows = 128 if t < KT - 1 else DROW + DCA
                    for part, w in enumerate((hi, pt_lo[j % 2][:])):
                        m = pe.matmul(acc[:, j, :], w[0:rows, t * PR:t * PR + 128], vals[par][0:rows, t, j, :],
                                      start=(j == 0 and t == 0 and part == 0), stop=(t == KT - 1 and part == 1),
                                      skip_group_check=True)
                if h == 2:
                    m.then_inc(pv_done, 1)

            def turns(b, j, par, p_use):
                pe.wait_ge(slot_free[p_use[0]], p_use[1] + 1)
                for h in range(3):
                    if h == 2:
                        pe.wait_ge(dca_ready, PAIRS * b + j + 1)
                    turn(b, j, h)
                    if j > 0:
                        pv(b, j - 1, h, par)

            def output(b):
                pe.wait_ge(o_chain, 5 * b + 5)
                pt_put(PT_USES * b + 3 * PAIRS)
                for g in range(G):
                    m = pe.matmul(pt_ps[:, g * S1:(g + 1) * S1], o_hi[0:PR, g * 128:(g + 1) * 128], fold[0:PR, :],
                                  start=True, stop=True)
                m.then_inc(pt_full, 1)

            use = Slots.prologue
            unit_y(use("Y"), 0)
            for u in range(4):
                unit_kv(use(f"KV{u}"), u, use("Y"))
            for g in range(G):
                unit_kt(use(f"KT{g}"), g, 1)
            unit_y(use("Y'"), 1)
            for u in range(4):
                unit_kv(use(f"KV{u}'"), u, use("Y'"))

            def batch(b, par, kind=Slots.FULL):
                def use(unit):
                    return Slots.body(unit, b, kind)
                project = kind == Slots.FULL
                packs = PACKS * (b // 2 + 1) if isinstance(b, int) else PACKS // 2 * (b + (2 - par))
                pe.wait_ge(q_loaded[par], packs)
                pe.wait_ge(k_loaded[par][0], packs)
                unit_p(use("P0"), 0, par)
                unit_p(use("P1"), 1, par)
                if kind != Slots.LAST:
                    unit_kt(use("KT0"), 0, b + 2)
                    unit_kt(use("KT1"), 1, b + 2)
                turns(b, 0, par, use("P0"))
                unit_p(use("P2"), 2, par)
                turns(b, 1, par, use("P1"))
                unit_p(use("P3"), 3, par)
                if project:
                    unit_y(use("Y"), b + 2)
                    unit_kv(use("KV0"), 0, use("Y"))
                turns(b, 2, par, use("P2"))
                pe.wait_ge(k_loaded[par][1], packs)
                unit_p(use("P4"), 4, par)
                if project:
                    unit_kv(use("KV1"), 1, None)
                turns(b, 3, par, use("P3"))
                if project:
                    unit_kv(use("KV2"), 2, None)
                unit_p(use("P5"), 5, par)
                turns(b, 4, par, use("P4"))
                unit_p(use("P6"), 6, par)
                if project:
                    unit_kv(use("KV3"), 3, None)
                turns(b, 5, par, use("P5"))
                unit_p(use("P7"), 7, par)
                turns(b, 6, par, use("P6"))
                turns(b, 7, par, use("P7"))
                for h in range(3):
                    pv(b, 7, h, par)
                output(b)

            batch(0, 0)
            with pe.Fori(0, (B - 4) // 2) as i:
                batch(2 * i + 1, 1)
                batch(2 * i + 2, 0)
            batch(B - 3, 1)
            batch(B - 2, 0, Slots.KEYS)
            batch(B - 1, 1, Slots.LAST)

        @block.scalar
        def _(act):
            act.preload_act_table_set("natural_log_exp_and_others")
            def take(use):
                sl, n = use
                act.wait_ge(slot_full[sl], n + 1)
                return slot[sl]

            def free(ins, use):
                ins.then_inc(slot_free[use[0]], 1)

            def ev_y(use):
                free(act.activation(yT[:], take(use)[:], ACT.Copy), use)

            def squares(n, u, kv_use):
                act.wait_ge(slot_free[kv_use[0]], kv_use[1] + 1)
                if not isinstance(n, int) or n >= 2:
                    act.wait_ge(ss_done, n - 1)
                act.activation(sq[u % 2][:], kv[:, 3 * u:3 * u + 3, 0:D], ACT.Square).then_inc(sq_done, 1)

            def rstd_start(n):
                act.wait_ge(var_ready, n + 1)
                act.activation(rstd[:], var[:], ACT.Ln).then_inc(ln_done, 1)
                act.wait_ge(ln_done, n + 1)
                act.activation(rstd[:], rstd[:], ACT.Exp, scale=-0.5).then_inc(r0_ready, 1)

            def ev_kt(n, g, use):
                ps = take(use)
                if not (isinstance(n, int) and n == 0 and g == 0):
                    act.wait_ge(klo_ready, 2 * n + g)
                act.activation(kf[:, 0:DCOL], ps[:, 0:DCOL], ACT.Identity, scale=ln_cols[:, 2:3],
                               bias=ln_cols[:, 3:4]).then_inc(kf_ready, 1)
                free(act.activation(kf[:, DCOL:KW], ps[:, DCOL:KW], ACT.Identity, scale=ln_cols[:, 4:5],
                                    bias=ln_cols[:, 5:6]), use)

            def probs(b, j, par, use):
                ps = slot[use[0]]
                act.wait_ge(max_ready, 2 * (PAIRS * b + j + 1))
                if j >= 2:
                    act.wait_ge(pt_full, PT_USES * b + 3 * (j - 1))
                elif not isinstance(b, int) or b > 0:
                    act.wait_ge(pt_full, PT_USES * (b - 1) + 3 * (PAIRS - 1 + j))
                act.activation(P[j % 2][0:PR, 0:MAIN], ps[0:PR, 0:MAIN], ACT.Exp, bias=negmax[0:PR, j:j + 1],
                               accum_out=total[par][0:PR, j:j + 1])
                free(act.activation(P[j % 2][0:PR, DCOL:KW], ps[0:PR, DCOL:KW], ACT.Exp, bias=negmax_dca[0:PR, j:j + 1],
                                    accum_out=total_dca[0:PR, j:j + 1]), use)

            def turned(b, j):
                for h in range(3):
                    act.wait_ge(pt_full, PT_USES * b + 3 * j + h + 1)
                    if h == 0 and (j >= 2 or not isinstance(b, int) or b > 0):
                        act.wait_ge(pv_done, PAIRS * b + j - 1)
                    act.activation(pt[j % 2][:, h * PTW:(h + 1) * PTW], pt_ps[:, 0:PTW], ACT.Copy).then_inc(pt_free, 1)

            use = Slots.prologue
            ev_y(use("Y"))
            for u in range(4):
                squares(u, u, use(f"KV{u}"))
            rstd_start(0)
            for g in range(G):
                ev_kt(0, g, use(f"KT{g}"))
            ev_y(use("Y'"))
            for u in range(4):
                squares(4 + u, u, use(f"KV{u}'"))
            rstd_start(1)

            def batch(b, par, kind=Slots.FULL):
                def use(unit):
                    return Slots.body(unit, b, kind)
                project = kind == Slots.FULL
                probs(b, 0, par, use("P0"))
                probs(b, 1, par, use("P1"))
                if kind != Slots.LAST:
                    ev_kt(b + 1, 0, use("KT0"))
                    ev_kt(b + 1, 1, use("KT1"))
                turned(b, 0)
                probs(b, 2, par, use("P2"))
                turned(b, 1)
                probs(b, 3, par, use("P3"))
                if project:
                    ev_y(use("Y"))
                turned(b, 2)
                probs(b, 4, par, use("P4"))
                if project:
                    squares(4 * b + 8, 0, use("KV0"))
                turned(b, 3)
                if project:
                    squares(4 * b + 9, 1, use("KV1"))
                probs(b, 5, par, use("P5"))
                turned(b, 4)
                probs(b, 6, par, use("P6"))
                if project:
                    squares(4 * b + 10, 2, use("KV2"))
                turned(b, 5)
                probs(b, 7, par, use("P7"))
                if project:
                    squares(4 * b + 11, 3, use("KV3"))
                turned(b, 6)
                if project:
                    rstd_start(b + 2)
                turned(b, 7)

            batch(0, 0)
            with act.Fori(0, (B - 4) // 2) as i:
                batch(2 * i + 1, 1)
                batch(2 * i + 2, 0)
            batch(B - 3, 1)
            batch(B - 2, 0, Slots.KEYS)
            batch(B - 1, 1, Slots.LAST)

        @block.gpsimd
        def _(pool):
            def queries(b):
                src = qT[:, :, b * S1:b * S1 + S1] if isinstance(b, int) else qT[:, :, bass.ds(b * S1, S1)]
                src = src.unsqueeze(2).broadcast_to([128, G, 2, S1])
                mask = pair_row[:].unsqueeze(1).unsqueeze(3).broadcast_to([128, G, 2, S1])
                hi, lo = (q_parts[:, k].rearrange("p g (i q) -> p g i q", i=2) for k in range(2))
                if not isinstance(b, int) or b >= 1:
                    pool.wait_ge(q_loaded[(b - 1) % 2] if isinstance(b, int) else q_loaded[b_par[0]],
                                 PACKS * ((b - 1) // 2 + 1) if isinstance(b, int) else q_count[0])
                pool.tensor_tensor(q_mask[:], src, mask, ALU.mult).then_inc(q_chain, 1)
                pool.tensor_tensor(hi, src, mask, ALU.mult).then_inc(q_chain, 1)
                pool.wait_ge(q_chain, 2 * b + 2)
                pool.tensor_tensor(lo, q_mask[:], hi, ALU.subtract).then_inc(q_ready, 1)

            b_par, q_count = [0], [0]

            def low_vals(n, u, par):
                if u == 0:
                    pool.wait_ge(vhi_done, n + 1)
                v = vals[par][:, 3 * u:3 * u + 3]
                pool.tensor_tensor(v[:, :, :, 32:64], kv[:, 3 * u:3 * u + 3, D:2 * D].rearrange("p t (j c) -> p t j c", c=32),
                                   v[:, :, :, 0:32], ALU.subtract).then_inc(vlo_done, 1)

            def low_keys(n, g):
                pool.wait_ge(khi_ready, 2 * n + g + 1)
                pool.tensor_tensor(k_parts[g][:, 1], kf[:], k_parts[g][:, 0], ALU.subtract).then_inc(klo_ready, 1)

            def norm_keys(n):
                pool.wait_ge(newton, 3 * n + 3)
                k = kv[:, :, 0:D].rearrange("p t (h d) -> p t h d", d=HD)
                pool.tensor_tensor(k, k, rstd[:].rearrange("p (t h) -> p t h", h=H).unsqueeze(3).broadcast_to([128, KT, H, HD]),
                                   ALU.mult).then_inc(kn_ready, 1)

            queries(0)
            norm_keys(0)
            for g in range(G):
                low_keys(0, g)
            for u in range(4):
                low_vals(0, u, 0)
            norm_keys(1)

            def batch(b, par, kind=Slots.FULL):
                if not isinstance(b, int):
                    b_par[0], q_count[0] = par, PACKS // 2 * (b + 2 - par)
                queries(b + 1)
                for g in range(G):
                    low_keys(b + 1, g)
                for u in range(4):
                    low_vals(b + 1, u, 1 - par)
                if kind == Slots.FULL:
                    norm_keys(b + 2)

            batch(0, 0)
            with pool.Fori(0, (B - 4) // 2) as i:
                batch(2 * i + 1, 1)
                batch(2 * i + 2, 0)
            batch(B - 3, 1)
            batch(B - 2, 0, Slots.KEYS)

        @block.vector
        def _(dve):
            dve.memset(y[:, KT - 1, :], 0.0).then_inc(zeroed, 1)
            for t in (P[0], P[1]):
                dve.memset(t[:], 0.0).then_inc(zeroed, 1)
            for t in (*pt, *pt_lo):
                dve.memset(t[:, KT * PR:], 0.0).then_inc(zeroed, 1)
            dve.memset(kv[:, KT - 1, :], 0.0).then_inc(zeroed, 1)
            dve.wait_ge(zeroed, 8)

            def ev_kv(n, u, kv_use):
                ps = slot[kv_use[0]]
                dve.wait_ge(slot_full[kv_use[0]], kv_use[1] + 1)
                if not isinstance(n, int) or n >= 1:
                    dve.wait_ge(vlo_done, 4 * (n - 1) + u + 1)
                whole = 3 if u < 3 else 2
                ins = dve.tensor_tensor(kv[:, 3 * u:3 * u + whole, :],
                                        ps[:, 0:whole * 512].rearrange("p (t f) -> p t f", f=512),
                                        bkv[0][:].rearrange("p a h d -> p (a h d)").unsqueeze(1).broadcast_to([128, whole, 512]),
                                        ALU.add)
                if u == 3:
                    rows = DROW + DCA
                    ins = dve.tensor_tensor(kv[0:rows, KT - 1, :], ps[0:rows, 1024:1536],
                                            bias_last[0:rows].rearrange("p a h d -> p (a h d)"), ALU.add)
                ins.then_inc(slot_free[kv_use[0]], 1)

            def high_vals(par, last_kv):
                dve.wait_ge(slot_free[last_kv[0]], last_kv[1] + 1)
                dve.tensor_copy(vals[par][:, :, :, 0:32],
                                kv[:, :, D:2 * D].rearrange("p t (j c) -> p t j c", c=32)).then_inc(vhi_done, 1)

            def high_keys(n, g, par, use):
                dve.wait_ge(slot_free[use[0]], use[1] + 1)
                dve.wait_ge(kf_ready, 2 * n + g + 1)
                if not isinstance(n, int) or n >= 1:
                    dve.wait_ge(k_loaded[1 - par][g], PACKS * ((n - 1) // 2 + 1) if isinstance(n, int)
                                else PACKS // 2 * (n + par))
                dve.tensor_copy(k_parts[g][:, 0], kf[:]).then_inc(khi_ready, 1)

            def sums(n, u):
                dve.wait_ge(sq_done, n + 1)
                dve.tensor_reduce(newt[:, u * 3 * H:(u + 1) * 3 * H],
                                  sq[u % 2][:].rearrange("p t (h d) -> p (t h) d", d=HD), AX.X, ALU.add).then_inc(ss_done, 1)

            def variances(n):
                dve.wait_ge(ss_done, 4 * n + 4)
                dve.tensor_scalar(var[:], newt[:], 1.0 / HD, EPS_ATTN, ALU.mult, ALU.add).then_inc(var_ready, 1)

            def newton_step(n):
                dve.wait_ge(r0_ready, n + 1)
                dve.wait_ge(var_ready, n + 1)
                dve.tensor_tensor(newt[:], rstd[:], rstd[:], ALU.mult).then_inc(newton, 1)
                dve.wait_ge(newton, 3 * n + 1)
                dve.scalar_tensor_tensor(out=newt[:], in0=newt[:], scalar=-0.5, in1=var[:],
                                         op0=ALU.mult, op1=ALU.mult).then_inc(newton, 1)
                dve.wait_ge(newton, 3 * n + 2)
                dve.scalar_tensor_tensor(out=rstd[:], in0=newt[:], scalar=1.5, in1=rstd[:],
                                         op0=ALU.add, op1=ALU.mult).then_inc(newton, 1)

            def maxima(b, j, use, last_p=None):
                ps = slot[use[0]]
                dve.wait_ge(slot_full[use[0]], use[1] + 1)
                if j == 0 and (not isinstance(b, int) or b > 0):
                    dve.wait_ge(slot_free[last_p[0]], last_p[1] + 1)
                dve.tensor_reduce(negmax[0:PR, j:j + 1], ps[0:PR, 0:MAIN], AX.X, ALU.max, negate=True).then_inc(max_ready, 1)
                dve.tensor_reduce(negmax_dca[0:PR, j:j + 1], ps[0:PR, DCOL:KW], AX.X, ALU.max, negate=True).then_inc(max_ready, 1)

            def rescale_dca(b, j, par, use):
                dve.wait_ge(slot_free[use[0]], use[1] + 1)
                dve.reciprocal(rtotal_dca[0:PR, j:j + 1], total_dca[0:PR, j:j + 1]).then_inc(dca_chain, 1)
                dve.wait_ge(dca_chain, PAIRS * b + j + 1)
                p = P[j % 2][0:PR, DCOL:KW]
                dve.tensor_scalar(p, p, rtotal_dca[0:PR, j:j + 1], total[par][0:PR, j:j + 1],
                                  ALU.mult, ALU.mult).then_inc(dca_ready, 1)

            def low(b, j):
                hi = pt[j % 2][:].bitcast(BF16)[:, 1::2]
                for h in range(3):
                    dve.wait_ge(pt_free, PT_USES * b + 3 * j + h + 1)
                    if h == 0 and (j >= 2 or not isinstance(b, int) or b > 0):
                        dve.wait_ge(pv_done, PAIRS * b + j - 1)
                    c = slice(h * PTW, (h + 1) * PTW)
                    dve.tensor_tensor(pt_lo[j % 2][:, c], pt[j % 2][:, c], hi[:, c], ALU.subtract).then_inc(lo_done, 1)

            def output(b, par):
                dve.reciprocal(rtotal[0:PR], total[par][0:PR]).then_inc(o_chain, 1)
                dve.wait_ge(o_chain, 5 * b + 1)
                dve.tensor_tensor(coef[0:PR], rtotal[0:PR].unsqueeze(2).broadcast_to([PR, PAIRS, 2]),
                                  pair_out[0:PR].unsqueeze(1).broadcast_to([PR, PAIRS, 2]), ALU.mult).then_inc(o_chain, 1)
                dve.wait_ge(o_chain, 5 * b + 2)
                dve.wait_ge(pv_done, PAIRS * b + PAIRS)
                cb = coef[0:PR].rearrange("p j i -> p (j i)").unsqueeze(2).broadcast_to([PR, H, HD]).rearrange(
                    "p (j i) d -> p j i d", i=2)
                for k, o in enumerate((o_hi, o_lo)):
                    ins = dve.tensor_tensor(o[0:PR].rearrange("p (j i d) -> p j i d", i=2, d=HD),
                                            acc[0:PR, :, 32 * k:32 * k + 32].rearrange("p j (i d) -> p j i d", d=HD), cb, ALU.mult)
                    ins.then_inc(o_chain, 1)
                dve.wait_ge(o_chain, 5 * b + 4)
                dve.tensor_tensor(o_hi[0:PR], o_hi[0:PR], o_lo[0:PR], ALU.add).then_inc(o_chain, 1)
                dve.wait_ge(pt_full, PT_USES * b + PT_USES)
                dst = env.ctxT[:, :, b * S1:(b + 1) * S1] if isinstance(b, int) else env.ctxT[:, :, bass.ds(b * S1, S1)]
                dve.tensor_copy(dst, pt_ps[:, 0:G * S1].rearrange("p (g q) -> p g q", g=G)).then_inc(pt_free, 1)

            use = Slots.prologue
            for u in range(4):
                ev_kv(0, u, use(f"KV{u}"))
                if u:
                    sums(u - 1, u - 1)
            sums(3, 3)
            variances(0)
            newton_step(0)
            high_vals(0, use("KV3"))
            for g in range(G):
                high_keys(0, g, 0, use(f"KT{g}"))
            for u in range(4):
                ev_kv(1, u, use(f"KV{u}'"))
                if u:
                    sums(3 + u, u - 1)
            sums(7, 3)
            variances(1)
            newton_step(1)

            def batch(b, par, kind=Slots.FULL):
                def use(unit):
                    return Slots.body(unit, b, kind)
                project = kind == Slots.FULL
                first = isinstance(b, int) and b == 0
                last_p = None if first else Slots.body("P7", b - 1, max(kind - 1, 0))
                maxima(b, 0, use("P0"), last_p)
                maxima(b, 1, use("P1"))
                if kind != Slots.LAST:
                    high_vals(1 - par, Slots.prologue("KV3'") if first else Slots.body("KV3", b - 1))
                    high_keys(b + 1, 0, 1 - par, use("KT0"))
                    high_keys(b + 1, 1, 1 - par, use("KT1"))
                rescale_dca(b, 0, par, use("P0"))
                low(b, 0)
                maxima(b, 2, use("P2"))
                rescale_dca(b, 1, par, use("P1"))
                low(b, 1)
                maxima(b, 3, use("P3"))
                rescale_dca(b, 2, par, use("P2"))
                low(b, 2)
                if project:
                    ev_kv(b + 2, 0, use("KV0"))
                maxima(b, 4, use("P4"))
                rescale_dca(b, 3, par, use("P3"))
                if project:
                    ev_kv(b + 2, 1, use("KV1"))
                    sums(4 * b + 8, 0)
                low(b, 3)
                if project:
                    ev_kv(b + 2, 2, use("KV2"))
                    sums(4 * b + 9, 1)
                maxima(b, 5, use("P5"))
                rescale_dca(b, 4, par, use("P4"))
                low(b, 4)
                maxima(b, 6, use("P6"))
                if project:
                    ev_kv(b + 2, 3, use("KV3"))
                    sums(4 * b + 10, 2)
                rescale_dca(b, 5, par, use("P5"))
                low(b, 5)
                maxima(b, 7, use("P7"))
                rescale_dca(b, 6, par, use("P6"))
                if project:
                    sums(4 * b + 11, 3)
                    variances(b + 2)
                low(b, 6)
                if project:
                    newton_step(b + 2)
                rescale_dca(b, 7, par, use("P7"))
                low(b, 7)
                output(b, par)

            batch(0, 0)
            with dve.Fori(0, (B - 4) // 2) as i:
                batch(2 * i + 1, 1)
                batch(2 * i + 2, 0)
            batch(B - 3, 1)
            batch(B - 2, 0, Slots.KEYS)
            batch(B - 1, 1, Slots.LAST)


def dump_x1(env):
    nc = env.nc
    with ExitStack() as ctx:
        done = ctx.enter_context(nc.semaphore("dump_done"))
        block = ctx.enter_context(nc.Block())

        @block.sync
        def _(sp):

            sp.dma_start(EXTRA.rearrange("g f t -> f g t"), env.ctxT[:]).then_inc(done, 16)
            sp.wait_ge(done, 16)


def feed_forward(env):
    nc = env.nc
    with ExitStack() as ctx:
        def sb(name, shape, dt=F32):
            return ctx.enter_context(nc.sbuf_tensor(name, shape, dt))
        sh = FfnShared(sb, ctx.enter_context(nc.semaphore("group_loaded0")), ctx.enter_context(nc.semaphore("group_loaded1")))
        env.x = sb("x_tokens", [128, NT, D])
        shared_expert(env, sh)
        routed_experts(env, sh)


class FfnShared:

    def __init__(self, sb, loaded0, loaded1):
        self.h_hi = sb("h_hi", [128, NT, D], BF16)
        self.h_lo = sb("h_lo", [128, NT, D], BF16)
        self.place = sb("place", [128, NT, E])
        self.w_hi = sb("w_hi", [128, NT, E], BF16)
        self.w_lo = sb("w_lo", [128, NT, E], BF16)
        self.iota = sb("iota", [128, E])
        self.w_up = [sb(f"w_up{i}", [128, 2, 4, 2 * F]) for i in range(2)]
        self.w_down = [sb(f"w_down{i}", [FH, 2, 4, D]) for i in range(2)]
        self.loaded = [loaded0, loaded1]

    def load(self, sp, a, q, par):
        for c in range(2):
            for k, name in enumerate(("Wg", "Wu")):
                sp.dma_start(self.w_up[par][:, c, :, k * F:(k + 1) * F],
                             a[name][bass.ds(q * 4, 4), c * 128:(c + 1) * 128, :].rearrange("e k f -> k e f")
                             if not isinstance(q, int) else
                             a[name][q * 4:q * 4 + 4, c * 128:(c + 1) * 128, :].rearrange("e k f -> k e f")
                             ).then_inc(self.loaded[par], 16)
            sp.dma_start(self.w_down[par][:, c],
                         a["Wd"][bass.ds(q * 4, 4), c * FH:(c + 1) * FH, :].rearrange("e f n -> f e n")
                         if not isinstance(q, int) else
                         a["Wd"][q * 4:q * 4 + 4, c * FH:(c + 1) * FH, :].rearrange("e f n -> f e n")
                         ).then_inc(self.loaded[par], 16)


LOADS = 6 * 16


def shared_expert(env, sh):
    nc, a = env.nc, env.a
    with ExitStack() as ctx:
        def sb(name, shape, dt=F32):
            return ctx.enter_context(nc.sbuf_tensor("s_" + name, shape, dt))

        def sem(name):
            return ctx.enter_context(nc.semaphore("s_" + name))

        x, ident = env.x, env.ident
        sq = env.ctxT[:].rearrange("p g t -> p (g t)").rearrange("p (n d) -> p n d", d=D)
        h = sb("h", [128, NT, D])
        wo = sb("wo", [128, G, D])
        bo = sb("bo", [128, D])
        hT = sb("hT", [128, 2, T])
        w_route = sb("w_route", [128, 2, E + 1])
        w_sup = sb("w_sup", [128, 2, 2, FS])
        w_sdown = sb("w_sdown", [128, FC, D])
        mean_x = sb("mean_x", [128, NT])
        var, lnv, rstd, tmp = (sb(n, [128, NT]) for n in ("var", "lnv", "rstd", "tmp"))
        logits = sb("logits", [128, NT, E + 1])
        top = sb("top", [128, NT, 8])
        top_at = sb("top_at", [128, NT, 8], U32)
        top_atf = sb("top_atf", [128, NT, 4])
        wtop = sb("wtop", [128, NT, 4])
        wsum = sb("wsum", [128, NT])
        onehot = sb("onehot", [128, NT, 4, E])
        sel = sb("sel", [128, NT, E])
        sel_b = sb("sel_b", [128, NT, E], BF16)
        w_tok = sb("w_tok", [128, NT, E])
        before = sb("before", [128, 128])
        before_b = sb("before_b", [128, 128], BF16)
        ones_b = sb("ones_b", [128, 128], BF16)
        sig = sb("sig", [128, NT])
        en = [sb(f"en{i}", [128, 512]) for i in range(2)]
        act_g = [sb(f"act_g{i}", [128, 512]) for i in range(2)]
        gu = [sb(f"gu{i}", [128, FC, 512]) for i in range(2)]
        wide = ctx.enter_context(nc.psum_tensor("wide", [128, 2048], F32))
        rest = ctx.enter_context(nc.psum_tensor("rest", [128, 2048], F32))

        loaded = sem("loaded")
        chain_done = sem("chain_done")
        x_loaded = sem("x_loaded")
        proj_done = sem("proj_done")
        bias_added = sem("bias_added")
        x1_ready = sem("x1_ready")
        centred = sem("centred")
        squared = sem("squared")
        var_done = sem("var_done")
        act_chain = sem("act_chain")
        r0_done = sem("r0_done")
        h_ready = sem("h_ready")
        turned = sem("turned")
        hT_ready = sem("hT_ready")
        routed = sem("routed")
        logits_ready = sem("logits_ready")
        top_ready = sem("top_ready")
        exp_done = sem("exp_done")
        sel_ready = sem("sel_ready")
        counted = sem("counted")
        place_ready = sem("place_ready")
        up_done = sem("up_done")
        en_done = sem("en_done")
        gu_done = sem("gu_done")
        down_done = sem("down_done")
        added = sem("added")

        block = ctx.enter_context(nc.Block())
        GROUPS = [(n, min(n + 4, NT)) for n in range(0, NT, 4)]
        STEPS = [(tg, f) for tg in range(len(GROUPS)) for f in range(FC)]

        def rows_of(f):
            return min(128, FS - f * 128)

        @block.sync
        def _(sp):
            for dst, src in (
                (wo[:], a["Wo"].rearrange("(c k) n -> k c n", k=128)),
                (x[:], a["x"].rearrange("b s d -> (b s) d").rearrange("(n p) d -> p n d", p=128)),
                (bo[:], a["bo_rows"]),
            ):
                sp.dma_start(dst, src).then_inc(x_loaded, 16)
            for dst, src in (
                (w_route[:], a["Wroute"].rearrange("(c k) e -> k c e", k=128)),
                (before[:], a["before"]),
                (sh.iota[:], a["iota"]),
                (w_sup[:, :, 0, :], a["Wsg"].rearrange("(c k) f -> k c f", k=128)),
                (w_sup[:, :, 1, :], a["Wsu"].rearrange("(c k) f -> k c f", k=128)),
                (w_sdown[:, 0:FC - 1, :], a["Wsd"][0:(FC - 1) * 128].rearrange("(c k) n -> k c n", k=128)),
                (w_sdown[0:rows_of(FC - 1), FC - 1, :], a["Wsd"][(FC - 1) * 128:FS]),
            ):
                sp.dma_start(dst, src).then_inc(loaded, 16)
            sh.load(sp, a, 0, 0)
            sh.load(sp, a, 1, 1)

        @block.gpsimd
        def _(pool):
            pool.wait_ge(x_loaded, 3 * 16)
            pool.tensor_tensor(x[:], x[:], bo[:].unsqueeze(1).broadcast_to([128, NT, D]), ALU.add).then_inc(bias_added, 1)
            pool.wait_ge(h_ready, 2)
            pool.tensor_tensor(sh.h_lo[:], h[:], sh.h_hi[:], ALU.subtract).then_inc(h_ready, 1)

        @block.tensor
        def _(pe):
            pe.wait_ge(x_loaded, 3 * 16)
            for n in range(NT):
                o = (wide if n < 8 else rest)[:, (n % 8) * D:(n % 8 + 1) * D]
                for c in range(2):
                    m = pe.matmul(o, env.ctxT[:, c, n * 128:(n + 1) * 128], wo[:, c], start=(c == 0), stop=(c == 1))
                if n in (7, NT - 1):
                    m.then_inc(proj_done, 1)
            pe.wait_ge(h_ready, 1)
            for k in range(2 * NT):
                c, n = k // NT, k % NT
                o = (wide if k < 16 else rest)[:, (k % 16) * 128:(k % 16 + 1) * 128]
                m = pe.transpose(o, h[:, n, c * 128:(c + 1) * 128], ident[:])
                if k in (15, 2 * NT - 1):
                    m.then_inc(turned, 1)
            pe.wait_ge(hT_ready, 2)
            pe.wait_ge(loaded, 7 * 16)
            for n in range(NT):
                for c in range(2):
                    m = pe.matmul(rest[:, 1536 + n * (E + 1):1536 + (n + 1) * (E + 1)], hT[:, c, n * 128:(n + 1) * 128],
                                  w_route[:, c], start=(c == 0), stop=(c == 1))
            m.then_inc(routed, 1)

            def up(s):
                tg, f = STEPS[s]
                n0, n1 = GROUPS[tg]
                if s >= 2:
                    pe.wait_ge(gu_done, s - 1)
                r, w = rows_of(f), (n1 - n0) * 128
                for k in range(2):
                    for c in range(2):
                        m = pe.matmul(rest[0:r, (2 * (s % 2) + k) * 512:(2 * (s % 2) + k) * 512 + w],
                                      w_sup[:, c, k, f * 128:f * 128 + r], hT[:, c, n0 * 128:n1 * 128],
                                      start=(c == 0), stop=(c == 1))
                m.then_inc(up_done, 1)

            def down(tg):
                pe.wait_ge(gu_done, FC * (tg + 1))
                n0, n1 = GROUPS[tg]
                for n in range(n0, n1):
                    if n >= 4:
                        pe.wait_ge(added, n - 3)
                    for f in range(FC):
                        r = rows_of(f)
                        m = pe.matmul(wide[:, (n % 4) * 512:(n % 4) * 512 + D], gu[tg % 2][0:r, f, (n - n0) * 128:(n - n0 + 1) * 128],
                                      w_sdown[0:r, f], start=(f == 0), stop=(f == FC - 1))
                    m.then_inc(down_done, 1)

            pe.wait_ge(logits_ready, 1)
            pe.wait_ge(sel_ready, 1)
            for n in range(NT):
                o = wide[:, n * E:(n + 1) * E]
                for m_ in range(n):
                    pe.matmul(o, ones_b[:], sel_b[:, m_], start=(m_ == 0), stop=False)
                m = pe.matmul(o, before_b[:], sel_b[:, n], start=(n == 0), stop=True)
            m.then_inc(counted, 1)
            for tg in range(len(GROUPS)):
                for f in range(FC):
                    up(FC * tg + f)
                if tg == 0:
                    pe.wait_ge(place_ready, 1)
                if tg:
                    down(tg - 1)
            down(len(GROUPS) - 1)

        @block.scalar
        def _(act):
            act.preload_act_table_set("natural_log_exp_and_others")
            act.wait_ge(centred, 1)
            act.activation(sq, h[:], ACT.Square).then_inc(squared, 1)
            act.wait_ge(var_done, 1)
            act.activation(lnv[:], var[:], ACT.Ln).then_inc(act_chain, 1)
            act.wait_ge(act_chain, 1)
            act.activation(rstd[:], lnv[:], ACT.Exp, scale=-0.5).then_inc(r0_done, 1)
            flat = hT[:].rearrange("p c t -> p (c t)")
            for k, (src, w) in enumerate(((wide, 2048), (rest, 1536))):
                act.wait_ge(turned, k + 1)
                act.activation(flat[:, 2048 * k:2048 * k + w], src[:, 0:w], ACT.Copy).then_inc(hT_ready, 1)
            act.wait_ge(top_ready, 1)
            act.activation(wtop[:], wtop[:], ACT.Exp).then_inc(exp_done, 1)
            act.activation(sig[:], logits[:, :, E], ACT.Exp, scale=-1.0).then_inc(exp_done, 1)
            for s, (tg, f) in enumerate(STEPS):
                r, w = rows_of(f), (GROUPS[tg][1] - GROUPS[tg][0]) * 128
                act.wait_ge(up_done, s + 1)
                if s >= 2:
                    act.wait_ge(gu_done, s - 1)
                act.activation(en[s % 2][0:r, 0:w], rest[0:r, 1024 * (s % 2):1024 * (s % 2) + w], ACT.Exp,
                               scale=-1.0).then_inc(en_done, 1)

        @block.vector
        def _(dve):
            step = [0]

            def chain(ins):
                step[0] += 1
                ins.then_inc(chain_done, 1)
                dve.wait_ge(chain_done, step[0])

            dve.wait_ge(bias_added, 1)
            for k, (src, n0, n1) in enumerate(((wide, 0, 8), (rest, 8, NT))):
                dve.wait_ge(proj_done, k + 1)
                ins = dve.tensor_tensor(x[:, n0:n1], x[:, n0:n1], src[:, 0:(n1 - n0) * D].rearrange("p (n d) -> p n d", d=D), ALU.add)
                ins.then_inc(x1_ready, 1)
            dve.wait_ge(x1_ready, 2)
            chain(dve.tensor_reduce(mean_x[:], x[:], AX.X, ALU.add))
            dve.scalar_tensor_tensor(out=h[:], in0=mean_x[:].unsqueeze(2).broadcast_to([128, NT, D]), scalar=-1.0 / D,
                                     in1=x[:], op0=ALU.mult, op1=ALU.add).then_inc(centred, 1)
            dve.wait_ge(squared, 1)
            chain(dve.tensor_reduce(tmp[:], sq, AX.X, ALU.add))
            dve.tensor_scalar(var[:], tmp[:], 1.0 / D, EPS_LN, ALU.mult, ALU.add).then_inc(var_done, 1)
            dve.wait_ge(r0_done, 1)
            chain(dve.tensor_tensor(tmp[:], rstd[:], rstd[:], ALU.mult))
            chain(dve.scalar_tensor_tensor(out=tmp[:], in0=tmp[:], scalar=-0.5, in1=var[:], op0=ALU.mult, op1=ALU.mult))
            chain(dve.scalar_tensor_tensor(out=rstd[:], in0=tmp[:], scalar=1.5, in1=rstd[:], op0=ALU.add, op1=ALU.mult))
            dve.wait_ge(centred, 1)
            dve.tensor_tensor(h[:], h[:], rstd[:].unsqueeze(2).broadcast_to([128, NT, D]), ALU.mult).then_inc(h_ready, 1)
            dve.wait_ge(h_ready, 1)
            dve.tensor_copy(sh.h_hi[:], h[:]).then_inc(h_ready, 1)
            dve.wait_ge(loaded, 7 * 16)
            dve.tensor_copy(before_b[:], before[:])
            chain(dve.memset(ones_b[:], 1.0))

            dve.wait_ge(routed, 1)
            dve.tensor_copy(logits[:], rest[:, 1536:1536 + NT * (E + 1)].rearrange("p (n e) -> p n e", n=NT)).then_inc(logits_ready, 1)
            dve.wait_ge(logits_ready, 1)
            for n in range(NT):
                ins = dve.max(top[:, n], logits[:, n, 0:E])
            chain(ins)
            for n in range(NT):
                ins = dve.max_index(top_at[:, n], top[:, n], logits[:, n, 0:E])
            chain(ins)
            dve.tensor_copy(top_atf[:], top_at[:, :, 0:4]).then_inc(chain_done, 1)
            dve.tensor_tensor(wtop[:], top[:, :, 0:4], top[:, :, 0:1].broadcast_to([128, NT, 4]), ALU.subtract).then_inc(top_ready, 1)
            step[0] += 1
            dve.wait_ge(chain_done, step[0])
            chain(dve.tensor_tensor(onehot[:], sh.iota[:].unsqueeze(1).unsqueeze(1).broadcast_to([128, NT, 4, E]),
                                    top_atf[:].unsqueeze(3).broadcast_to([128, NT, 4, E]), ALU.is_equal))
            chain(dve.tensor_reduce(sel[:], onehot[:].rearrange("p n k e -> p n e k"), AX.X, ALU.add))
            dve.tensor_copy(sel_b[:], sel[:]).then_inc(sel_ready, 1)
            dve.wait_ge(exp_done, 1)
            chain(dve.tensor_reduce(wsum[:], wtop[:], AX.X, ALU.add))
            chain(dve.reciprocal(tmp[:], wsum[:]))
            chain(dve.tensor_tensor(wtop[:], wtop[:], tmp[:].unsqueeze(2).broadcast_to([128, NT, 4]), ALU.mult))
            chain(dve.tensor_tensor(onehot[:], onehot[:], wtop[:].unsqueeze(3).broadcast_to([128, NT, 4, E]), ALU.mult))
            chain(dve.tensor_reduce(w_tok[:], onehot[:].rearrange("p n k e -> p n e k"), AX.X, ALU.add))
            chain(dve.tensor_copy(sh.w_hi[:], w_tok[:]))
            dve.tensor_tensor(sh.w_lo[:], w_tok[:], sh.w_hi[:], ALU.subtract)
            dve.wait_ge(exp_done, 2)
            chain(dve.tensor_scalar(wsum[:], sig[:], 1.0, None, ALU.add))
            chain(dve.reciprocal(sig[:], wsum[:]))
            dve.wait_ge(counted, 1)
            dve.scalar_tensor_tensor(out=sh.place[:], in0=wide[:, 0:NT * E].rearrange("p (n e) -> p n e", e=E), scalar=1.0,
                                     in1=sel[:], op0=ALU.add, op1=ALU.mult).then_inc(place_ready, 1)

            def silu_up(s):
                tg, f = STEPS[s]
                r, w = rows_of(f), (GROUPS[tg][1] - GROUPS[tg][0]) * 128
                g_ps = rest[0:r, 1024 * (s % 2):1024 * (s % 2) + w]
                u_ps = rest[0:r, 1024 * (s % 2) + 512:1024 * (s % 2) + 512 + w]
                e, t = en[s % 2][0:r, 0:w], act_g[s % 2][0:r, 0:w]
                dve.wait_ge(en_done, s + 1)
                chain(dve.tensor_scalar(e, e, 1.0, None, ALU.add))
                chain(dve.reciprocal(t, e))
                chain(dve.tensor_tensor(t, g_ps, t, ALU.mult))
                if f == 0 and tg >= 2:
                    dve.wait_ge(down_done, GROUPS[tg - 2][1])
                dve.tensor_tensor(gu[tg % 2][0:r, f, 0:w], u_ps, t, ALU.mult).then_inc(gu_done, 1)

            def add_shared(tg):
                for n in range(*GROUPS[tg]):
                    dve.wait_ge(down_done, n + 1)
                    dve.scalar_tensor_tensor(out=x[:, n], in0=wide[:, (n % 4) * 512:(n % 4) * 512 + D], scalar=sig[:, n:n + 1],
                                             in1=x[:, n], op0=ALU.mult, op1=ALU.add).then_inc(added, 1)

            for tg in range(len(GROUPS)):
                for f in range(FC):
                    silu_up(FC * tg + f)
                if tg:
                    add_shared(tg - 1)
            add_shared(len(GROUPS) - 1)


def routed_experts(env, sh):
    nc, a = env.nc, env.a
    QN = E // 4
    with ExitStack() as ctx:
        def sb(name, shape, dt=F32):
            return ctx.enter_context(nc.sbuf_tensor("r_" + name, shape, dt))

        def sem(name):
            return ctx.enter_context(nc.semaphore("r_" + name))

        x, ident = env.x, env.ident
        slots = sb("slots", [128, NT, E * CAP], BF16)
        ident_b = sb("ident_b", [128, 128], BF16)
        iota1 = sb("iota1", [128, CAP])
        own = sb("own", [128, QN, E])
        w_all = sb("w_all", [128, QN, 2 * E])
        w_mine = sb("w_mine", [128, QN, 2, E])
        w_slot = sb("w_slot", [128, QN])
        xeT = sb("xeT", [128, 2, E * CAP])
        xg = [sb(f"xg{i}", [128, 2, 128]) for i in range(2)]
        en = sb("en", [128, F])
        t_g = sb("t_g", [128, F])
        gu = sb("gu", [128, F])
        guT = [sb(f"guT{i}", [FH, 2, 128]) for i in range(2)]
        ye = sb("ye", [128, D])
        ye_hi = sb("ye_hi", [128, QN, D], BF16)
        ye_lo = sb("ye_lo", [128, QN, D], BF16)
        slotsT = [sb(f"slotsT{i}", [128, QN, 128], BF16) for i in range(2)]
        gather = ctx.enter_context(nc.psum_tensor("gather", [128, 2, E * CAP], F32))
        up_ps = ctx.enter_context(nc.psum_tensor("up_ps", [128, 512], F32))
        turn_ps = ctx.enter_context(nc.psum_tensor("turn_ps", [128, 512], F32))
        down_ps = ctx.enter_context(nc.psum_tensor("down_ps", [128, 512], F32))
        w_ps_flat = ctx.enter_context(nc.psum_tensor("w_ps", [128, QN * 2 * E], F32))
        w_ps = w_ps_flat[:].rearrange("p (q k) -> p q k", q=QN)

        loaded = sem("loaded")
        chain_done = sem("chain_done")
        slots_ready = sem("slots_ready")
        gathered = sem("gathered")
        xeT_ready = sem("xeT_ready")
        w_slot_ready = sem("w_slot_ready")
        xg_ready = sem("xg_ready")
        up_done = sem("up_done")
        en_done = sem("en_done")
        gu_chain = sem("gu_chain")
        gu_ready = sem("gu_ready")
        turned = sem("turned")
        guT_ready = sem("guT_ready")
        down_done = sem("down_done")
        ye_chain = sem("ye_chain")
        ye_ready = sem("ye_ready")
        st_turned = sem("st_turned")
        st_ready = sem("st_ready")
        combined = sem("combined")
        out_ready = sem("out_ready")
        stored = sem("stored")

        block = ctx.enter_context(nc.Block())
        x_out = env.out.rearrange("b s d -> (b s) d").rearrange("(n p) d -> p n d", p=128)

        @block.sync
        def _(sp):
            sp.dma_start(own[:].rearrange("p q e -> p (q e)"), a["own"]).then_inc(loaded, 16)
            with sp.Fori(0, QN // 2 - 1) as i:
                for par in range(2):
                    sp.wait_ge(down_done, 2 * i + par + 1)
                    sh.load(sp, a, 2 * i + par + 2, par)
            for n in range(NT):
                sp.wait_ge(out_ready, n + 1)
                sp.dma_start(x_out[:, n], x[:, n]).then_inc(stored, 16)
            sp.wait_ge(stored, 16 * NT)

        @block.gpsimd
        def _(pool):
            pool.wait_ge(xeT_ready, 4)

            def fetch(q, par):
                src = xeT[:, :, q * 128:(q + 1) * 128] if isinstance(q, int) else xeT[:, :, bass.ds(q * 128, 128)]
                pool.tensor_copy(xg[par][:], src).then_inc(xg_ready, 1)

            fetch(0, 0)
            fetch(1, 1)
            with pool.Fori(0, QN // 2 - 1) as i:
                for par in range(2):
                    pool.wait_ge(up_done, 2 * i + par + 1)
                    fetch(2 * i + par + 2, par)

        @block.tensor
        def _(pe):
            for n in range(NT):
                pe.wait_ge(slots_ready, n + 1)
                for c in range(2):
                    for part, hp in enumerate((sh.h_hi, sh.h_lo)):
                        for k in range(2):
                            m = pe.matmul(gather[:, c, k * 512:(k + 1) * 512], hp[:, n, c * 128:(c + 1) * 128],
                                          slots[:, n, k * 512:(k + 1) * 512], start=(n == 0 and part == 0),
                                          stop=(n == NT - 1 and part == 1))
                for q in range(QN):
                    for part, wp in enumerate((sh.w_hi, sh.w_lo)):
                        m = pe.matmul(w_ps[:, q, part * E:(part + 1) * E], slots[:, n, q * 128:(q + 1) * 128], wp[:, n],
                                      start=(n == 0 and q == 0 and part == 0), stop=(n == NT - 1), skip_group_check=True)
            m.then_inc(gathered, 1)

            def group(q, par, n_loads):
                pe.wait_ge(xg_ready, q + 1)
                pe.wait_ge(sh.loaded[par], n_loads)
                if not isinstance(q, int) or q > 0:
                    pe.wait_ge(gu_ready, q)
                for e in range(4):
                    for c in range(2):
                        m = pe.matmul(up_ps[32 * e:32 * e + 32, 0:2 * F], xg[par][:, c, 32 * e:32 * e + 32],
                                      sh.w_up[par][:, c, e], start=(c == 0), stop=(c == 1))
                m.then_inc(up_done, 1)
                pe.wait_ge(gu_ready, q + 1)
                for k in range(2):
                    m = pe.transpose(turn_ps[0:FH, k * 128:(k + 1) * 128], gu[:, k * FH:(k + 1) * FH], ident[:])
                m.then_inc(turned, 1)
                pe.wait_ge(guT_ready, q + 1)
                if not isinstance(q, int) or q > 0:
                    pe.wait_ge(ye_chain, 2 * q)
                for e in range(4):
                    for k in range(2):
                        m = pe.matmul(down_ps[32 * e:32 * e + 32, 0:D], guT[par][:, k, 32 * e:32 * e + 32],
                                      sh.w_down[par][:, k, e], start=(k == 0), stop=(k == 1))
                m.then_inc(down_done, 1)

            group(0, 0, LOADS)
            with pe.Fori(0, QN // 2 - 1) as i:
                group(2 * i + 1, 1, LOADS * i + LOADS)
                group(2 * i + 2, 0, LOADS * i + 2 * LOADS)
            group(QN - 1, 1, QN // 2 * LOADS)

            st = [turn_ps[:].bitcast(BF16), up_ps[:].bitcast(BF16)]
            out_ps = [down_ps, w_ps_flat]
            pe.wait_ge(ye_ready, QN)
            for n in range(NT + 1):
                if n < NT:
                    if n >= 2:
                        pe.wait_ge(st_ready, n - 1)
                    for q in range(QN):
                        m = pe.transpose(st[n % 2][:, q * 128:(q + 1) * 128], slots[:, n, q * 128:(q + 1) * 128], ident_b[:])
                    m.then_inc(st_turned, 1)
                if n >= 1:
                    k = n - 1
                    pe.wait_ge(st_ready, k + 1)
                    if k >= 2:
                        pe.wait_ge(out_ready, k - 1)
                    for q in range(QN):
                        for part, yp in enumerate((ye_hi, ye_lo)):
                            m = pe.matmul(out_ps[k % 2][:, 0:D], slotsT[k % 2][:, q], yp[:, q],
                                          start=(q == 0 and part == 0), stop=(q == QN - 1 and part == 1))
                    m.then_inc(combined, 1)

        @block.scalar
        def _(act):
            act.preload_act_table_set("natural_log_exp_and_others")
            act.wait_ge(gathered, 1)
            for c in range(2):
                for k in range(2):
                    act.activation(xeT[:, c, k * 512:(k + 1) * 512], gather[:, c, k * 512:(k + 1) * 512], ACT.Copy).then_inc(xeT_ready, 1)

            def group(q, par):
                act.wait_ge(up_done, q + 1)
                act.activation(en[:], up_ps[:, 0:F], ACT.Exp, scale=-1.0).then_inc(en_done, 1)
                act.wait_ge(turned, q + 1)
                act.activation(guT[par][:].rearrange("p k t -> p (k t)"), turn_ps[0:FH, 0:256], ACT.Copy).then_inc(guT_ready, 1)

            with act.Fori(0, QN // 2) as i:
                group(2 * i, 0)
                group(2 * i + 1, 1)
            st = [turn_ps[:].bitcast(BF16), up_ps[:].bitcast(BF16)]
            for n in range(NT):
                act.wait_ge(st_turned, n + 1)
                if n >= 2:
                    act.wait_ge(combined, n - 1)
                act.activation(slotsT[n % 2][:].rearrange("p q t -> p (q t)"), st[n % 2], ACT.Copy).then_inc(st_ready, 1)

        @block.vector
        def _(dve):
            step = [0]

            def chain(ins):
                step[0] += 1
                ins.then_inc(chain_done, 1)
                dve.wait_ge(chain_done, step[0])

            dve.tensor_copy(ident_b[:], ident[:])
            chain(dve.tensor_scalar(iota1[:], sh.iota[:, 0:CAP], 1.0, None, ALU.add))
            for n in range(NT):
                dve.tensor_tensor(slots[:, n].rearrange("p (e c) -> p e c", c=CAP),
                                  iota1[:].unsqueeze(1).broadcast_to([128, E, CAP]),
                                  sh.place[:, n].unsqueeze(2).broadcast_to([128, E, CAP]), ALU.is_equal).then_inc(slots_ready, 1)
            dve.wait_ge(gathered, 1)
            dve.wait_ge(loaded, 16)
            chain(dve.tensor_tensor(w_mine[:], w_ps.rearrange("p q (k e) -> p q k e", k=2),
                                    own[:].unsqueeze(2).broadcast_to([128, QN, 2, E]), ALU.mult))
            chain(dve.tensor_reduce(w_slot[:], w_mine[:].rearrange("p q k e -> p q (k e)"), AX.X, ALU.add))

            def group(q):
                dve.wait_ge(en_done, q + 1)
                dve.tensor_scalar(en[:], en[:], 1.0, None, ALU.add).then_inc(gu_chain, 1)
                dve.wait_ge(gu_chain, 3 * q + 1)
                dve.reciprocal(t_g[:], en[:]).then_inc(gu_chain, 1)
                dve.wait_ge(gu_chain, 3 * q + 2)
                dve.tensor_tensor(t_g[:], up_ps[:, 0:F], t_g[:], ALU.mult).then_inc(gu_chain, 1)
                dve.wait_ge(gu_chain, 3 * q + 3)
                dve.tensor_tensor(gu[:], up_ps[:, F:2 * F], t_g[:], ALU.mult).then_inc(gu_ready, 1)
                dve.wait_ge(down_done, q + 1)
                w = w_slot[:, q:q + 1] if isinstance(q, int) else w_slot[:, bass.ds(q, 1)]
                dve.tensor_tensor(ye[:], down_ps[:, 0:D], w.broadcast_to([128, D]), ALU.mult).then_inc(ye_chain, 1)
                dve.wait_ge(ye_chain, 2 * q + 1)

                def at(t):
                    return t[:, q] if isinstance(q, int) else t[:, bass.ds(q, 1)].rearrange("p o d -> p (o d)")
                dve.tensor_copy(at(ye_hi), ye[:]).then_inc(ye_chain, 1)
                dve.wait_ge(ye_chain, 2 * q + 2)
                dve.tensor_tensor(at(ye_lo), ye[:], at(ye_hi), ALU.subtract).then_inc(ye_ready, 1)

            with dve.Fori(0, QN // 2) as i:
                group(2 * i)
                group(2 * i + 1)
            out_ps = [down_ps, w_ps_flat]
            for n in range(NT):
                dve.wait_ge(combined, n + 1)
                dve.tensor_tensor(x[:, n], x[:, n], out_ps[n % 2][:, 0:D], ALU.add).then_inc(out_ready, 1)


def kernel(**inputs):
    import concourse.bacc as bacc
    from concourse.bass_utils import run_bass_kernel_spmd

    pre = "L0_xattn_"
    f = {k: np.ascontiguousarray(v) for k, v in inputs.items()}

    def rows(*names):
        return np.ascontiguousarray(np.broadcast_to(np.concatenate([f[pre + n] for n in names])[None], (128, sum(f[pre + n].size for n in names))))

    kvb = np.concatenate([f[pre + "bk"], f[pre + "bv"]]).reshape(H, 2, HD).transpose(1, 0, 2).reshape(1, -1)
    arrays = {
        "x": f["x"], "ctx": f["ctx_1024"],
        "Wq": f[pre + "Wq"], "Wk": f[pre + "Wk"], "Wv": f[pre + "Wv"], "Wkv_dca": f[pre + "Wkv_dca"], "Wo": f[pre + "Wo"],
        "bq_rows": rows("bq"), "bo_rows": rows("bo"), "bkv_dca_rows": rows("bkv_dca"),
        "bkv_rows": np.ascontiguousarray(np.broadcast_to(kvb, (128, 2 * D))),
        "ln_cols": np.ascontiguousarray(np.tile(np.stack([f[pre + n] for n in (
            "qn_w", "qn_b", "kn_w", "kn_b", "kn_dca_w", "kn_dca_b")], 1), (128 // HD, 1))),
        "ident": np.eye(128, dtype=np.float32),
        "fold": np.tile(np.eye(S1, dtype=np.float32), (2, 1)),
    }
    p = np.arange(128)
    arrays["before"] = (p[:, None] < p[None, :]).astype(np.float32)
    arrays["iota"] = np.tile(np.arange(E, dtype=np.float32), (128, 1))
    arrays["own"] = (4 * np.arange(E // 4)[None, :, None] + p[:, None, None] // CAP == np.arange(E)).astype(
        np.float32).reshape(128, -1)
    arrays["pair_masks"] = np.stack([p // HD % 2 == 0, p // HD % 2 == 1, p < S1, (p >= S1) & (p < PR)], 1).astype(np.float32)
    arrays["Wroute"] = np.concatenate([f["L0_ffn_Wr"], f["L0_ffn_Wse"]], 1)
    for n in ("Wg", "Wu", "Wd", "Wsg", "Wsu", "Wsd"):
        arrays[n] = f["L0_ffn_" + n]

    nc = bacc.Bacc("TRN2", target_bir_lowering=False, num_devices=1)
    aps, feed = {}, {}
    for name, arr in arrays.items():
        feed[f"in_{name}_dram"] = arr
        aps[name] = nc.dram_tensor(f"in_{name}_dram", arr.shape, mybir.dt.from_np(arr.dtype), kind="ExternalInput").ap()
    out = nc.dram_tensor("out_0_dram", (B, S1, D), F32, kind="ExternalOutput").ap()
    program(nc, aps, out)
    r = run_bass_kernel_spmd(nc, [feed], core_ids=[0])
    return r.results[0]["out_0_dram"]
```

```python
from contextlib import ExitStack

import numpy as np
import concourse.bass as bass
from concourse import mybir

F32 = mybir.dt.float32
BF16 = mybir.dt.bfloat16
U32 = mybir.dt.uint32
ALU = mybir.AluOpType
ACT = mybir.ActivationFunctionType
AX = mybir.AxisListType

B, S1, D = 32, 56, 256
SK, DY = 1500, 128
DCA = 16
H, HD = 16, 16
G = 2
T = B * S1
NT = T // 128
MAIN = SK - DCA
KT = 12
REST = MAIN - (KT - 1) * 128
DROW = 96
DCOL = (KT - 1) * 128 + DROW
KW = DCOL + DCA
KP = KT * 128
VW = 66
PAIRS = H // 2
PR = 2 * S1
SLOT = 1536
E, CAP = 32, 32
F, FH = 176, 88
FS, FC = 704, 6
EPS_ATTN, EPS_LN = 1e-6, 1e-5
SCALE = HD ** -0.5


class Slots:
    PROLOGUE = [["Y", "Y'", "KT0", "KT1", "Y''", "KT0'", "KT1'"],
                ["K0", "K1", "V0", "V1", "K0'", "K1'", "S0", "S1", "S2", "S3", "M0", "S4", "S5", "S6", "S7"]]
    BODY = [["E0", "E1", "E2", "O1", "E3", "E4", "E5", "Y", "E6", "O0", "KT0", "E7", "KT1"],
            ["K0", "M1", "K1", "V0", "S0", "S1", "S2", "V1", "S3", "M0", "S4", "S5", "S6", "S7"]]
    FIRST, FULL, NO_CONTEXT, NO_KEYS, LAST, AFTER = range(6)
    KEYS = ("Y", "K0", "K1", "KT0", "KT1")
    SCORES = KEYS + ("V0", "V1", "M0") + tuple(f"S{j}" for j in range(8))
    DROPPED = [("O1",), (), ("Y",), KEYS, SCORES, SCORES + ("M1", "O0") + tuple(f"E{j}" for j in range(8))]

    @classmethod
    def units(cls, s, kind):
        return [u for u in cls.BODY[s] if u not in cls.DROPPED[kind]]

    @classmethod
    def prologue(cls, unit):
        s = 0 if unit in cls.PROLOGUE[0] else 1
        return s, cls.PROLOGUE[s].index(unit)

    @classmethod
    def body(cls, unit, b, kind):
        s = 0 if unit in cls.BODY[0] else 1
        n = len(cls.PROLOGUE[s]) + cls.units(s, kind).index(unit)
        if kind == cls.FIRST:
            return s, n
        n += len(cls.units(s, cls.FIRST)) - len(cls.BODY[s])
        if kind == cls.FULL:
            return s, n + len(cls.BODY[s]) * b
        return s, n + len(cls.BODY[s]) * (B - 3) + sum(len(cls.units(s, k)) for k in range(cls.NO_CONTEXT, kind))


def program(nc, a, out):
    with ExitStack() as ctx:
        env = Env(nc, a, out, ctx)
        with ExitStack() as part:
            shared = AttentionShared(env, part)
            project_queries(env, shared)
            attention(env, shared)
        feed_forward(env)


class Env:

    def __init__(self, nc, a, out, ctx):
        self.nc, self.a, self.out = nc, a, out
        self.sb = lambda name, shape, dt=F32: ctx.enter_context(nc.sbuf_tensor(name, shape, dt))
        self.ctxT = self.sb("ctxT", [128, G, T])
        self.ident = self.sb("ident", [128, 128])


class AttentionShared:

    def __init__(self, env, ctx):
        def sb(name, shape, dt=F32):
            return ctx.enter_context(env.nc.sbuf_tensor(name, shape, dt))
        self.wkv = [sb("wkv", [128, 2, H, HD]), sb("wkv_dca", [128, 2, H, HD])]
        self.bk = sb("bk", [128, D])
        self.bk_last = sb("bk_last", [128, D])
        self.v_bias = sb("v_bias", [128, G])
        self.ln_cols = sb("ln_cols", [128, 8])
        self.pair_out = sb("pair_out", [128, 2])
        self.fold = sb("fold", [128, S1])
        self.sel = sb("sel", [128, 4, 2, 128], BF16)
        self.q_scratch = env.nc.dram_tensor("q_scratch", [128, PAIRS, B * PR], BF16, kind="Internal").ap()


def project_queries(env, sh):
    nc, a = env.nc, env.a
    with ExitStack() as ctx:
        def sb(name, shape, dt=F32):
            return ctx.enter_context(nc.sbuf_tensor("q_" + name, shape, dt))

        def sem(name):
            return ctx.enter_context(nc.semaphore("q_" + name))

        ident = env.ident
        x = sb("x", [128, NT, D])
        wkv, ln_cols = sh.wkv, sh.ln_cols
        bk_dca = sb("bk_dca", [128, D])
        bv_cols = sb("bv_cols", [128, G, 2])
        sel = sb("sel", [128, 4, 2, 128])
        pair_row = sb("pair_row", [128, 2])
        qT = sb("qT", [128, G, T])
        q_parts = sb("q_parts", [128, 2, G * B, 2, S1], BF16)
        wq = sb("wq", [128, 2, H, HD])
        bq = sb("bq", [128, H, HD])
        means = sb("means", [128, 7, H])
        xn = sb("xn", [128, NT, D])
        sqx = sb("sqx", [128, NT, D])
        xnT = sb("xnT", [128, G * T])
        q = sb("q", [128, NT, H, HD])
        mean_x = sb("mean_x", [128, NT])
        var = [sb("var_x", [128, NT]), sb("var_q", [128, NT * H])]
        lnv = [sb("lnv_x", [128, NT]), sb("lnv_q", [128, NT * H])]
        rstd = [sb("rstd_x", [128, NT]), sb("rstd_q", [128, NT * H])]
        tmp = [sb("tmp_x", [128, NT]), sb("tmp_q", [128, NT * H])]
        slot = [ctx.enter_context(nc.psum_tensor(f"qslot{i}", [128, SLOT], F32)) for i in range(2)]

        x_loaded, consts_loaded = sem("x_loaded"), sem("consts_loaded")
        chain_done = sem("chain_done")
        centred = sem("centred")
        squared = sem("squared")
        var_done = sem("var_done")
        ln_done = sem("ln_done")
        r0_done = sem("r0_done")
        normed = sem("normed")
        w_ready = sem("w_ready")
        full = sem("full")
        free = sem("free")
        q_hi_done = sem("q_hi_done")
        q_lo_done = sem("q_lo_done")
        q_stored = sem("q_stored")

        block = ctx.enter_context(nc.Block())

        def cols(i):
            return min(12, G * NT - 12 * i) * 128

        @block.sync
        def _(sp):
            sp.dma_start(x[:], a["x"].rearrange("b s d -> (b s) d").rearrange("(n p) d -> p n d", p=128)).then_inc(x_loaded, 16)

            def const(dst, src):
                sp.dma_start(dst, src).then_inc(consts_loaded, 16)
            for half, name in enumerate(("Wk", "Wv")):
                hs = slice(half * H // 2, (half + 1) * H // 2)
                src = a[name].rearrange("k (h a d) -> k a h d", a=2, d=HD)
                for part in range(2):
                    const(wkv[0][:, part, hs, :], src[:, part])
            const(wkv[1][:], a["Wkv_dca"].rearrange("k (a h d) -> k a h d", a=2, d=HD))
            const(wq[:], a["Wq"].rearrange("(c k) (h d) -> k c h d", k=128, d=HD))
            const(sh.bk[:], a["bk_rows"])
            const(bk_dca[:], a["bk_dca_rows"])
            const(bv_cols[:], a["bv_cols"])
            const(sel[:], a["sel"])
            const(bq[:].rearrange("p h d -> p (h d)"), a["bq_rows"])
            const(ln_cols[:, 0:6], a["ln_cols"])
            const(ident[:], a["ident"])
            const(pair_row[:], a["pair_masks"][:, 0:2])
            const(sh.pair_out[:], a["pair_masks"][:, 2:4])
            const(sh.fold[0:PR, :], a["fold"])
            for part, done in enumerate((q_hi_done, q_lo_done)):
                sp.wait_ge(done, 2)
                for block_ in (2 * part, 2 * part + 1):
                    for jj in range(4):
                        sp.dma_start(sh.q_scratch[32 * block_:32 * block_ + 32, jj::4, :],
                                     q_parts[32 * jj:32 * jj + 32, part].rearrange("p (g b) i q -> p g (b i q)", g=G)).then_inc(q_stored, 16)
            sp.wait_ge(q_stored, 16 * 16)

        N_CONSTS = 16

        @block.tensor
        def _(pe):
            pe.wait_ge(consts_loaded, 16 * N_CONSTS)

            def turn(unit, src):
                if unit >= 2:
                    pe.wait_ge(free, unit - 1)
                for k in range(12 * (unit % 3), min(12 * (unit % 3) + 12, G * NT)):
                    g, n = k // NT, k % NT
                    m = pe.transpose(slot[unit % 2][:, (k % 12) * 128:(k % 12) * 128 + 128], src(n, g), ident[:])
                m.then_inc(full, 1)

            pe.wait_ge(normed, 1)
            for unit in range(3):
                turn(unit, lambda n, g: xn[:, n, g * 128:(g + 1) * 128])
            pe.wait_ge(w_ready, 1)
            for unit in range(3, 6):
                pe.wait_ge(free, 3 if unit == 3 else unit - 1)
                for n in range(6 * (unit - 3), min(6 * (unit - 3) + 6, NT)):
                    for c in range(G):
                        m = pe.matmul(slot[unit % 2][:, (n % 6) * D:(n % 6 + 1) * D],
                                      xnT[:, c * T + n * 128:c * T + (n + 1) * 128],
                                      wq[:, c].rearrange("p h d -> p (h d)"), start=(c == 0), stop=(c == 1))
                m.then_inc(full, 1)
            pe.wait_ge(normed, 2)
            for unit in range(6, 9):
                turn(unit, lambda n, g: q[:, n, g * 8:(g + 1) * 8, :].rearrange("p h d -> p (h d)"))

        @block.scalar
        def _(act):
            act.preload_act_table_set("natural_log_exp_and_others")

            def rstd_start(k, src, dst):
                act.wait_ge(centred, k + 1)
                act.activation(dst, src, ACT.Square).then_inc(squared, 1)
                act.wait_ge(var_done, k + 1)
                act.activation(lnv[k][:], var[k][:], ACT.Ln).then_inc(ln_done, 1)
                act.wait_ge(ln_done, k + 1)
                act.activation(rstd[k][:], lnv[k][:], ACT.Exp, scale=-0.5).then_inc(r0_done, 1)

            rstd_start(0, xn[:], sqx[:])
            for unit in range(3):
                act.wait_ge(full, unit + 1)
                act.activation(xnT[:, unit * SLOT:unit * SLOT + cols(unit)], slot[unit % 2][:, 0:cols(unit)],
                               ACT.Copy).then_inc(free, 1)
            rstd_start(1, q[:].rearrange("p n h d -> p n (h d)"), sqx[:])
            act.wait_ge(w_ready, 1)
            for unit in range(6, 9):
                c0, n = (unit - 6) * SLOT, cols(unit - 6)
                act.wait_ge(full, unit + 1)
                act.activation(qT[:].rearrange("p c t -> p (c t)")[:, c0:c0 + n], slot[unit % 2][:, 0:n],
                               ACT.Identity, scale=ln_cols[:, 6:7], bias=ln_cols[:, 7:8]).then_inc(free, 1)
            act.wait_ge(free, 9)
            for i in range(2):
                act.activation(q_parts[:, 0, :, i, :], qT[:].rearrange("p g (b q) -> p (g b) q", q=S1), ACT.Copy,
                               scale=pair_row[:, i:i + 1]).then_inc(q_hi_done, 1)

        @block.vector
        def _(dve):
            step = [0]

            def chain(ins):
                step[0] += 1
                ins.then_inc(chain_done, 1)
                dve.wait_ge(chain_done, step[0])

            def normalise(k, sq, n, eps, values):
                dve.wait_ge(squared, k + 1)
                chain(dve.tensor_reduce(tmp[k][:], sq, AX.X, ALU.add))
                dve.tensor_scalar(var[k][:], tmp[k][:], 1.0 / n, eps, ALU.mult, ALU.add).then_inc(var_done, 1)
                r, t = rstd[k][:], tmp[k][:]
                dve.wait_ge(r0_done, k + 1)
                chain(dve.tensor_tensor(t, r, r, ALU.mult))
                chain(dve.scalar_tensor_tensor(out=t, in0=t, scalar=-0.5, in1=var[k][:], op0=ALU.mult, op1=ALU.mult))
                chain(dve.scalar_tensor_tensor(out=r, in0=t, scalar=1.5, in1=r, op0=ALU.add, op1=ALU.mult))
                dve.tensor_tensor(values, values, r.unsqueeze(2).broadcast_to([128, r.shape[1], n]),
                                  ALU.mult).then_inc(normed, 1)

            dve.wait_ge(x_loaded, 16)
            chain(dve.tensor_reduce(mean_x[:], x[:], AX.X, ALU.add))
            dve.scalar_tensor_tensor(out=xn[:], in0=mean_x[:].unsqueeze(2).broadcast_to([128, NT, D]), scalar=-1.0 / D,
                                     in1=x[:], op0=ALU.mult, op1=ALU.add).then_inc(centred, 1)
            dve.wait_ge(consts_loaded, 16 * N_CONSTS)
            mats = [wkv[0][:, 0], wkv[1][:, 0], sh.bk[:].rearrange("p (h d) -> p h d", d=HD),
                    bk_dca[:].rearrange("p (h d) -> p h d", d=HD), wq[:, 0], wq[:, 1], bq[:]]
            for k, w in enumerate(mats):
                last = dve.tensor_reduce(means[:, k, :], w, AX.X, ALU.add)
            chain(last)
            for k, w in enumerate(mats):
                last = dve.scalar_tensor_tensor(out=w, in0=means[:, k, :].unsqueeze(2).broadcast_to([128, H, HD]),
                                                scalar=-1.0 / HD, in1=w, op0=ALU.mult, op1=ALU.add)
            chain(last)
            dve.tensor_copy(sh.bk_last[0:DROW], sh.bk[0:DROW])
            dve.tensor_copy(sh.bk_last[DROW:], bk_dca[DROW:])
            dve.tensor_copy(sh.sel[:], sel[:])
            dve.tensor_tensor(sh.v_bias[:], bv_cols[:, :, 0], bv_cols[:, :, 1], ALU.add)
            dve.tensor_scalar(ln_cols[:, 6:8], ln_cols[:, 0:2], SCALE, None, ALU.mult).then_inc(w_ready, 1)

            dve.wait_ge(centred, 1)
            normalise(0, sqx[:], D, EPS_LN, xn[:])
            for unit in range(3, 6):
                n0, n1 = 6 * (unit - 3), min(6 * (unit - 3) + 6, NT)
                dve.wait_ge(full, unit + 1)
                ins = dve.tensor_tensor(q[:, n0:n1].rearrange("p n h d -> p n (h d)"),
                                        slot[unit % 2][:, 0:(n1 - n0) * D].rearrange("p (n f) -> p n f", f=D),
                                        bq[:].rearrange("p h d -> p (h d)").unsqueeze(1).broadcast_to([128, n1 - n0, D]),
                                        ALU.add)
                ins.then_inc(free, 1)
            dve.wait_ge(free, 6)
            dve.memset(mean_x[:], 0.0).then_inc(centred, 1)
            normalise(1, sqx[:].rearrange("p n (h d) -> p (n h) d", d=HD), HD, EPS_ATTN,
                      q[:].rearrange("p n h d -> p (n h) d"))
            dve.wait_ge(free, 9)
            for i in range(2):
                dve.wait_ge(q_hi_done, i + 1)
                dve.scalar_tensor_tensor(out=q_parts[:, 1, :, i, :], in0=qT[:].rearrange("p g (b q) -> p (g b) q", q=S1),
                                         scalar=pair_row[:, i:i + 1], in1=q_parts[:, 0, :, i, :], op0=ALU.mult,
                                         op1=ALU.subtract).then_inc(q_lo_done, 1)



def attention(env, sh):
    nc, a = env.nc, env.a
    with ExitStack() as ctx:
        def sb(name, shape, dt=F32):
            return ctx.enter_context(nc.sbuf_tensor("a_" + name, shape, dt))

        def sem(name):
            return ctx.enter_context(nc.semaphore("a_" + name))

        ident = env.ident
        wkv, bk, bk_last, ln_cols = sh.wkv, sh.bk, sh.bk_last, sh.ln_cols
        pair_out, fold, sel, v_bias = sh.pair_out, sh.fold, sh.sel, sh.v_bias
        q_pack = [sb(f"q_pack{i}", [128, PAIRS, PR], BF16) for i in range(2)]
        kf = [sb(f"kf{g}", [128, KP]) for g in range(G)]
        k_parts = [sb(f"k_parts{g}", [128, 2, KP], BF16) for g in range(G)]
        k_pack = [sb(f"k_pack{i}", [128, PAIRS, KP], BF16) for i in range(2)]
        y = sb("y", [128, KT, DY])
        yT = [sb(f"yT{i}", [128, SLOT]) for i in range(2)]
        v_raw = sb("v_raw", [128, KT // 2, D])
        kk = sb("kk", [128, KT, D])
        sq = sb("sq", [128, KT // 2, D])
        var = sb("var", [128, KT * H])
        rstd = sb("rstd", [128, KT * H])
        newt = sb("newt", [128, KT * H])
        vals = [sb(f"vals{i}", [128, KT, PAIRS, VW], BF16) for i in range(2)]
        vals_dca = [sb(f"vals_dca{i}", [128, PAIRS, VW], BF16) for i in range(2)]
        m_in = [sb(f"m_in{i}", [128, 128]) for i in range(2)]
        m_rows = [sb(f"m_rows{i}", [128, PR], BF16) for i in range(2)]
        pt = [sb(f"pt{i}", [128, KT * PR + 16]) for i in range(4)]
        pt_lo = [sb(f"pt_lo{i}", [128, KT * PR + 16], BF16) for i in range(4)]
        rtotal = [sb(f"rtotal{g}", [128, 4, 2]) for g in range(G)]
        coef = [sb(f"coef{g}", [128, 4, 2, 2]) for g in range(G)]
        o = [sb(f"o{i}", [128, D]) for i in range(3)]

        slot = [ctx.enter_context(nc.psum_tensor(f"slot{i}", [128, SLOT], F32)) for i in range(2)]
        acc = ctx.enter_context(nc.psum_tensor("acc", [128, PAIRS, 128], F32))

        slot_full = [sem("slot_full0"), sem("slot_full1")]
        slot_free = [sem("slot_free0"), sem("slot_free1")]
        y_loaded = sem("y_loaded")
        zeroed = sem("zeroed")
        q_loaded = [sem("q_loaded0"), sem("q_loaded1")]
        k_loaded = [[sem(f"k_loaded{i}{g}") for g in range(G)] for i in range(2)]
        khi_ready = sem("khi_ready")
        klo_ready = sem("klo_ready")
        vhi_done = sem("vhi_done")
        vlo_done = sem("vlo_done")
        vlo_chain = sem("vlo_chain")
        max_done = sem("max_done")
        m_ready = sem("m_ready")
        m_chain = sem("m_chain")
        lo_done = sem("lo_done")
        lo_rest_done = sem("lo_rest_done")
        pv_done = [sem("pv_done0"), sem("pv_done1")]
        sq_done = sem("sq_done")
        ss_done = sem("ss_done")
        var_ready = sem("var_ready")
        ln_done = sem("ln_done")
        r0_ready = sem("r0_ready")
        newton = sem("newton")
        kn_ready = sem("kn_ready")
        o_chain = [sem("o_chain0"), sem("o_chain1")]
        o_sum = [sem("o_sum0"), sem("o_sum1")]

        zeros = [y[:, KT - 1, :], kk[:, KT - 1, :], *(t[:] for t in m_in)]
        zeros += [t[:, KT * PR:] for t in (*pt, *pt_lo)]
        zeros += [t[:, c0:c1] for t in kf for c0, c1 in ((MAIN, DCOL), (KW, KP))]
        zeros += [t[:, KT - 1] for t in vals] + [t[:] for t in vals_dca]
        ones = [t[:, 0:KT - 1, :, 32:33] for t in vals] + [t[0:REST, KT - 1, :, 32:33] for t in vals]
        ones += [t[DROW:DROW + DCA, :, 32:33] for t in vals_dca]
        N_ZEROED = len(zeros) + len(ones)

        block = ctx.enter_context(nc.Block())
        PACKS = 16 * 16
        HALF = KT // 2
        LO = 8 * PR

        def packs(n, par):
            return PACKS // 2 * (n + (2 - par))

        @block.sync
        def _(sp):
            def load_y(b):
                sp.dma_start(y[:, 0:KT - 1, :], a["ctx"][b, 0:(KT - 1) * 128, :].rearrange("(p t) d -> p t d", p=128)).then_inc(y_loaded, 16)
                sp.dma_start(y[0:REST, KT - 1, :], a["ctx"][b, (KT - 1) * 128:MAIN, :]).then_inc(y_loaded, 16)
                sp.dma_start(y[DROW:DROW + DCA, KT - 1, :], a["ctx"][b, MAIN:SK, :]).then_inc(y_loaded, 16)

            def after_y(use):
                sp.wait_ge(slot_full[use[0]], use[1] + 1)

            def pack(n, par):
                for g in range(G):
                    sp.wait_ge(klo_ready, 2 * n + g + 1)
                    if g == 1:
                        src = sh.q_scratch[:, :, n * PR:(n + 1) * PR] if isinstance(n, int) else sh.q_scratch[:, :, bass.ds(n * PR, PR)]
                        sp.dma_start(q_pack[par][:], src).then_inc(q_loaded[par], 16)
                    for block_, part in enumerate((0, 1, 0, 1)):
                        for jj in range(4):
                            sp.dma_start(k_pack[par][32 * block_:32 * block_ + 32, 4 * g + jj, :],
                                         k_parts[g][32 * jj:32 * jj + 32, part, :]).then_inc(k_loaded[par][g], 16)

            sp.wait_ge(zeroed, 1)
            load_y(0)
            after_y(Slots.prologue("Y"))
            load_y(1)
            after_y(Slots.prologue("Y'"))
            load_y(2)
            sp.wait_ge(zeroed, N_ZEROED)
            pack(0, 0)
            after_y(Slots.prologue("Y''"))
            load_y(3)
            pack(1, 1)

            def batch(b, par, load=True, kind=Slots.FULL):
                if load:
                    after_y(Slots.body("Y", b, kind))
                    load_y(b + 4)
                pack(b + 2, par)

            batch(0, 0, kind=Slots.FIRST)
            with sp.Fori(0, (B - 6) // 2) as i:
                batch(2 * i + 1, 1)
                batch(2 * i + 2, 0)
            batch(B - 5, 1)
            batch(B - 4, 0, load=False)
            batch(B - 3, 1, load=False)

        @block.tensor
        def _(pe):
            def put(use):
                sl, n = use
                if not (isinstance(n, int) and n == 0):
                    pe.wait_ge(slot_free[sl], n)
                return slot[sl]

            def unit_y(use, n):
                ps = put(use)
                pe.wait_ge(y_loaded, 48 * (n + 1))
                for t in range(KT):
                    m = pe.transpose(ps[:, t * 128:t * 128 + 128], y[:, t, :], ident[:])
                m.then_inc(slot_full[0], 1)

            def project(use, u, kv, par):
                ps = put(use)
                w = [wkv[k][:, kv].rearrange("p h d -> p (h d)") for k in range(2)]
                for k in range(HALF):
                    t = HALF * u + k
                    out = ps[:, k * D:(k + 1) * D]
                    if t < KT - 1:
                        m = pe.matmul(out, yT[par][:, t * 128:(t + 1) * 128], w[0], start=True, stop=True)
                    else:
                        pe.matmul(out[0:DROW], yT[par][:, t * 128:t * 128 + DROW], w[0], start=True, stop=True)
                        m = pe.matmul(out[DROW:DROW + DCA], yT[par][:, DCOL:DCOL + DCA], w[1], start=True, stop=True)
                m.then_inc(slot_full[1], 1)

            def unit_k(use, u, par, y_use):
                if u == 0:
                    pe.wait_ge(slot_free[0], y_use[1] + 1)
                project(use, u, 0, par)

            def unit_kt(use, g, n):
                ps = put(use)
                pe.wait_ge(kn_ready, 2 * n + g + 1)
                for t in range(KT):
                    m = pe.transpose(ps[:, t * 128:t * 128 + 128], kk[:, t, g * 128:(g + 1) * 128], ident[:])
                m.then_inc(slot_full[0], 1)

            def unit_s(use, n, j, par):
                ps = put(use)
                if j % 4 == 0:
                    pe.wait_ge(k_loaded[par][j // 4], packs(n, par))
                if j == 0:
                    pe.wait_ge(q_loaded[par], 8 * (n + (2 - par)))
                for c0 in range(0, KP, 512):
                    m = pe.matmul(ps[0:PR, c0:c0 + 512], q_pack[par][:, j, :], k_pack[par][:, j, c0:c0 + 512], start=True, stop=True)
                m.then_inc(slot_full[1], 1)

            def unit_m(use, n, half):
                ps = put(use)
                pe.wait_ge(m_ready, 2 * n + half + 1)
                pe.transpose(ps[:, 0:PR], m_in[half][0:PR, :], ident[0:PR, 0:PR]).then_inc(slot_full[1], 1)

            def unit_e(use, j, par, m_use):
                ps = put(use)
                if j % 4 == 0:
                    pe.wait_ge(slot_free[1], m_use[1] + 1)
                rows = m_rows[j // 4][:].unsqueeze(1)
                for h in range(3):
                    c0 = 512 * h
                    n = 4 if h < 2 else 3
                    pe.matmul(ps[:, c0:c0 + n * PR].rearrange("p (t q) -> p t q", q=PR), sel[:, j % 4, 0, :],
                              rows.broadcast_to([128, n, PR]), start=True, stop=False, skip_group_check=True)
                    if h == 2:
                        pe.matmul(ps[:, c0 + 3 * PR:c0 + 4 * PR], sel[:, j % 4, 1, :], m_rows[j // 4][:], start=False,
                                  stop=False, skip_group_check=True)
                    for k in range(4):
                        t = 4 * h + k
                        m = pe.matmul(ps[:, c0 + k * PR:c0 + (k + 1) * PR], k_pack[par][:, j, t * 128:(t + 1) * 128],
                                      q_pack[par][:, j, :], start=False, stop=True, skip_group_check=True)
                m.then_inc(slot_full[0], 1)

            def pv(b, j, par):
                if j % 4 == 0 and (not isinstance(b, int) or b > 0):
                    pe.wait_ge(o_chain[j // 4], 5 * b)
                if j == 0:
                    pe.wait_ge(vlo_done, 2 * b + 2)
                pe.wait_ge(lo_done, PAIRS * b + j + 1)
                pe.wait_ge(lo_rest_done, PAIRS * b + j + 1)
                hi = pt[j % 4][:].bitcast(BF16)[:, 1::2]
                for t in range(KT):
                    for part, w in enumerate((hi, pt_lo[j % 4][:])):
                        pe.matmul(acc[:, j, 0:65], w[:, t * PR:t * PR + 128], vals[par][:, t, j, 0:65],
                                  start=(j % 4 == 0 and t == 0 and part == 0), stop=(t == KT - 1 and part == 1),
                                  skip_group_check=True)
                t = KT - 1
                for part, w in enumerate((hi, pt_lo[j % 4][:])):
                    w = w[:, t * PR:t * PR + 128]
                    pe.matmul(acc[:, j, 66:99], w, vals_dca[par][:, j, 0:33], start=False, stop=False, skip_group_check=True)
                    m = pe.matmul(acc[:, j, 66:98], w, vals_dca[par][:, j, 33:65], start=False, stop=(part == 1), skip_group_check=True)
                if j % 4 == 3:
                    m.then_inc(pv_done[j // 4], 1)

            def unit_o(use, b, g):
                ps = put(use)
                pe.wait_ge(o_sum[g], 2 * b + 2)
                pe.matmul(ps[:, 0:S1], o[0][0:PR, g * 128:(g + 1) * 128], fold[0:PR, :], start=True,
                          stop=True).then_inc(slot_full[0], 1)

            use = Slots.prologue
            pe.wait_ge(zeroed, N_ZEROED)
            unit_y(use("Y"), 0)
            unit_k(use("K0"), 0, 0, use("Y"))
            unit_k(use("K1"), 1, 0, None)
            unit_y(use("Y'"), 1)
            project(use("V0"), 0, 1, 0)
            project(use("V1"), 1, 1, 0)
            unit_kt(use("KT0"), 0, 0)
            unit_kt(use("KT1"), 1, 0)
            unit_k(use("K0'"), 0, 1, use("Y'"))
            unit_k(use("K1'"), 1, 1, None)
            unit_y(use("Y''"), 2)
            unit_kt(use("KT0'"), 0, 1)
            unit_kt(use("KT1'"), 1, 1)
            for j in range(PAIRS):
                unit_s(use(f"S{j}"), 0, j, 0)
                if j == 3:
                    unit_m(use("M0"), 0, 0)

            def batch(b, par, kind=Slots.FULL):
                def use(unit):
                    return Slots.body(unit, b, kind)

                def before(unit):
                    if kind == Slots.FIRST:
                        return Slots.prologue(unit + "''" if unit == "Y" else unit)
                    return Slots.body(unit, b - 1, max(kind - 1, Slots.FULL))
                keys, scores = kind < Slots.NO_KEYS, kind < Slots.LAST
                if keys:
                    unit_k(use("K0"), 0, par, before("Y"))
                unit_e(use("E0"), 0, par, before("M0"))
                unit_m(use("M1"), b, 1)
                unit_e(use("E1"), 1, par, None)
                if keys:
                    unit_k(use("K1"), 1, par, None)
                unit_e(use("E2"), 2, par, None)
                if kind != Slots.FIRST:
                    pv(b - 1, 7, 1 - par)
                if scores:
                    project(use("V0"), 0, 1, 1 - par)
                pv(b, 0, par)
                if kind != Slots.FIRST:
                    unit_o(use("O1"), b - 1, 1)
                if scores:
                    unit_s(use("S0"), b + 1, 0, 1 - par)
                unit_e(use("E3"), 3, par, None)
                pv(b, 1, par)
                if scores:
                    unit_s(use("S1"), b + 1, 1, 1 - par)
                unit_e(use("E4"), 4, par, use("M1"))
                pv(b, 2, par)
                if scores:
                    unit_s(use("S2"), b + 1, 2, 1 - par)
                unit_e(use("E5"), 5, par, None)
                pv(b, 3, par)
                if scores:
                    project(use("V1"), 1, 1, 1 - par)
                if kind <= Slots.FULL:
                    unit_y(use("Y"), b + 3)
                if scores:
                    unit_s(use("S3"), b + 1, 3, 1 - par)
                unit_e(use("E6"), 6, par, None)
                if scores:
                    unit_m(use("M0"), b + 1, 0)
                unit_o(use("O0"), b, 0)
                if scores:
                    unit_s(use("S4"), b + 1, 4, 1 - par)
                if keys:
                    unit_kt(use("KT0"), 0, b + 2)
                if scores:
                    unit_s(use("S5"), b + 1, 5, 1 - par)
                pv(b, 4, par)
                pv(b, 5, par)
                if scores:
                    unit_s(use("S6"), b + 1, 6, 1 - par)
                unit_e(use("E7"), 7, par, None)
                pv(b, 6, par)
                if scores:
                    unit_s(use("S7"), b + 1, 7, 1 - par)
                if keys:
                    unit_kt(use("KT1"), 1, b + 2)

            batch(0, 0, Slots.FIRST)
            with pe.Fori(0, (B - 4) // 2) as i:
                batch(2 * i + 1, 1)
                batch(2 * i + 2, 0)
            batch(B - 3, 1, Slots.NO_CONTEXT)
            batch(B - 2, 0, Slots.NO_KEYS)
            batch(B - 1, 1, Slots.LAST)
            pv(B - 1, 7, 1)
            unit_o(Slots.body("O1", B, Slots.AFTER), B - 1, 1)

        @block.scalar
        def _(act):
            act.preload_act_table_set("natural_log_exp_and_others")
            act.wait_ge(zeroed, N_ZEROED)

            def take(use):
                act.wait_ge(slot_full[use[0]], use[1] + 1)
                return slot[use[0]]

            def ev_y(use, par):
                act.activation(yT[par][:], take(use)[:], ACT.Copy).then_inc(slot_free[0], 1)

            def squares(n, u, k_use):
                act.wait_ge(slot_free[1], k_use[1] + 1)
                if not isinstance(n, int) or n >= 1 or u == 1:
                    act.wait_ge(ss_done, 2 * n + u)
                act.activation(sq[:], kk[:, HALF * u:HALF * (u + 1), :], ACT.Square).then_inc(sq_done, 1)

            def rstd_start(n):
                act.wait_ge(var_ready, n + 1)
                act.activation(rstd[:], var[:], ACT.Ln).then_inc(ln_done, 1)
                act.wait_ge(ln_done, n + 1)
                act.activation(rstd[:], rstd[:], ACT.Exp, scale=-0.5).then_inc(r0_ready, 1)

            def ev_kt(n, g, use):
                ps = take(use)
                if not isinstance(n, int) or n >= 1:
                    act.wait_ge(klo_ready, 2 * n + g - 1)
                act.activation(kf[g][:, 0:MAIN], ps[:, 0:MAIN], ACT.Identity, scale=ln_cols[:, 2:3], bias=ln_cols[:, 3:4])
                act.activation(kf[g][:, DCOL:KW], ps[:, DCOL:KW], ACT.Identity, scale=ln_cols[:, 4:5],
                               bias=ln_cols[:, 5:6]).then_inc(slot_free[0], 1)

            def high_keys(n, g, par, use):
                act.wait_ge(slot_free[0], use[1] + 1)
                if not isinstance(n, int) or n >= 1:
                    act.wait_ge(k_loaded[1 - par][g], packs(n - 1, 1 - par))
                act.activation(k_parts[g][:, 0], kf[g][:], ACT.Copy).then_inc(khi_ready, 1)

            def copy_vals(n, u, use):
                ps = take(use)
                if not isinstance(n, int) or n >= 1 or u == 1:
                    act.wait_ge(vlo_done, 2 * n + u)
                whole = HALF if u == 0 else HALF - 1
                ins = act.activation(v_raw[:, 0:whole, :], ps[:, 0:whole * D].rearrange("p (t f) -> p t f", f=D), ACT.Copy)
                if u == 1:
                    rows = DROW + DCA
                    ins = act.activation(v_raw[0:rows, whole, :], ps[0:rows, whole * D:(whole + 1) * D], ACT.Copy)
                ins.then_inc(slot_free[1], 1)

            def high_vals(n, u, par, use):
                act.wait_ge(slot_free[1], use[1] + 1)
                v = v_raw[:].rearrange("p t (j c) -> p t j c", c=32)
                whole = HALF if u == 0 else HALF - 1
                ins = act.activation(vals[par][:, HALF * u:HALF * u + whole, :, 0:32], v[:, 0:whole], ACT.Copy)
                if u == 1:
                    act.activation(vals[par][0:REST, KT - 1, :, 0:32], v[0:REST, whole], ACT.Copy)
                    ins = act.activation(vals_dca[par][DROW:DROW + DCA, :, 0:32], v[DROW:DROW + DCA, whole], ACT.Copy)
                ins.then_inc(vhi_done, 1)

            def probs(j, use):
                ps = take(use)
                act.activation(pt[j % 4][:, 0:KT * PR].rearrange("p (h c) -> p h c", h=3),
                               ps[:].rearrange("p (h c) -> p h c", h=3)[:, :, 0:4 * PR], ACT.Exp).then_inc(slot_free[0], 1)

            def ev_o(b, g, use):
                dst = env.ctxT[:, g, b * S1:(b + 1) * S1] if isinstance(b, int) else env.ctxT[:, g, bass.ds(b * S1, S1)]
                act.activation(dst, take(use)[:, 0:S1], ACT.Identity, bias=v_bias[:, g:g + 1]).then_inc(slot_free[0], 1)

            use = Slots.prologue
            ev_y(use("Y"), 0)
            squares(0, 0, use("K0"))
            squares(0, 1, use("K1"))
            ev_y(use("Y'"), 1)
            for u in range(2):
                copy_vals(0, u, use(f"V{u}"))
                high_vals(0, u, 0, use(f"V{u}"))
            rstd_start(0)
            ev_kt(0, 0, use("KT0"))
            high_keys(0, 0, 0, use("KT0"))
            ev_kt(0, 1, use("KT1"))
            high_keys(0, 1, 0, use("KT1"))
            squares(1, 0, use("K0'"))
            squares(1, 1, use("K1'"))
            ev_y(use("Y''"), 0)
            rstd_start(1)
            ev_kt(1, 0, use("KT0'"))
            high_keys(1, 0, 1, use("KT0'"))
            ev_kt(1, 1, use("KT1'"))
            high_keys(1, 1, 1, use("KT1'"))

            def batch(b, par, kind=Slots.FULL):
                def use(unit):
                    return Slots.body(unit, b, kind)
                keys, scores = kind < Slots.NO_KEYS, kind < Slots.LAST
                probs(0, use("E0"))
                if keys:
                    squares(b + 2, 0, use("K0"))
                probs(1, use("E1"))
                probs(2, use("E2"))
                if scores:
                    copy_vals(b + 1, 0, use("V0"))
                if kind != Slots.FIRST:
                    ev_o(b - 1, 1, use("O1"))
                if keys:
                    squares(b + 2, 1, use("K1"))
                probs(3, use("E3"))
                probs(4, use("E4"))
                if scores:
                    high_vals(b + 1, 0, 1 - par, use("V0"))
                probs(5, use("E5"))
                if scores:
                    copy_vals(b + 1, 1, use("V1"))
                if keys:
                    rstd_start(b + 2)
                if kind <= Slots.FULL:
                    ev_y(use("Y"), 1 - par)
                probs(6, use("E6"))
                ev_o(b, 0, use("O0"))
                if scores:
                    high_vals(b + 1, 1, 1 - par, use("V1"))
                if keys:
                    ev_kt(b + 2, 0, use("KT0"))
                probs(7, use("E7"))
                if keys:
                    high_keys(b + 2, 0, par, use("KT0"))
                    ev_kt(b + 2, 1, use("KT1"))
                    high_keys(b + 2, 1, par, use("KT1"))

            batch(0, 0, Slots.FIRST)
            with act.Fori(0, (B - 4) // 2) as i:
                batch(2 * i + 1, 1)
                batch(2 * i + 2, 0)
            batch(B - 3, 1, Slots.NO_CONTEXT)
            batch(B - 2, 0, Slots.NO_KEYS)
            batch(B - 1, 1, Slots.LAST)
            ev_o(B - 1, 1, Slots.body("O1", B, Slots.AFTER))

        @block.gpsimd
        def _(pool):
            def low_keys(n, g):
                pool.wait_ge(khi_ready, 2 * n + g + 1)
                pool.tensor_tensor(k_parts[g][:, 1], kf[g][:], k_parts[g][:, 0], ALU.subtract).then_inc(klo_ready, 1)

            def norm_keys(n, g):
                pool.wait_ge(newton, 3 * n + 3)
                k = kk[:, :, g * 128:(g + 1) * 128].rearrange("p t (h d) -> p t h d", d=HD)
                r = rstd[:].rearrange("p (t h) -> p t h", h=H)[:, :, 8 * g:8 * g + 8]
                pool.tensor_tensor(k, k, r.unsqueeze(3).broadcast_to([128, KT, 8, HD]), ALU.mult).then_inc(kn_ready, 1)

            def low_rest(j, use):
                pool.wait_ge(slot_free[0], use[1] + 1)
                hi = pt[j % 4][:].bitcast(BF16)[:, 1::2]
                c = slice(LO, KT * PR)
                pool.tensor_tensor(pt_lo[j % 4][:, c], pt[j % 4][:, c], hi[:, c], ALU.subtract).then_inc(lo_rest_done, 1)

            def add_parts(b, g):
                c = slice(g * 128, (g + 1) * 128)
                for part in (1, 2):
                    pool.wait_ge(o_chain[g], 5 * b + 5)
                    if part == 2:
                        pool.wait_ge(o_sum[g], 2 * b + 1)
                    pool.tensor_tensor(o[0][0:PR, c], o[0][0:PR, c], o[part][0:PR, c], ALU.add).then_inc(o_sum[g], 1)

            def low_vals(n, u, par):
                pool.wait_ge(vhi_done, 2 * n + u + 1)
                v = v_raw[:].rearrange("p t (j c) -> p t j c", c=32)
                whole = HALF if u == 0 else HALF - 1
                dst = vals[par][:, HALF * u:HALF * u + whole]
                ins = pool.tensor_tensor(dst[:, :, :, 33:65], v[:, 0:whole], dst[:, :, :, 0:32], ALU.subtract)
                if u == 1:
                    for k, (dst, rows) in enumerate(((vals[par][:, KT - 1], slice(0, REST)), (vals_dca[par][:], slice(DROW, DROW + DCA)))):
                        ins.then_inc(vlo_chain, 1)
                        pool.wait_ge(vlo_chain, 2 * n + k + 1)
                        ins = pool.tensor_tensor(dst[rows, :, 33:65], v[rows, whole], dst[rows, :, 0:32], ALU.subtract)
                ins.then_inc(vlo_done, 1)
                if u == 1:
                    pool.wait_ge(vlo_done, 2 * n + 2)

            for u in range(2):
                low_vals(0, u, 0)
            for n in range(2):
                for g in range(G):
                    norm_keys(n, g)
                for g in range(G):
                    low_keys(n, g)

            def batch(b, par, kind=Slots.FULL):
                def use(unit):
                    return Slots.body(unit, b, kind)
                keys, scores = kind < Slots.NO_KEYS, kind < Slots.LAST
                low_rest(0, use("E0"))
                low_rest(1, use("E1"))
                low_rest(2, use("E2"))
                if kind != Slots.FIRST:
                    add_parts(b - 1, 1)
                low_rest(3, use("E3"))
                if scores:
                    low_vals(b + 1, 0, 1 - par)
                add_parts(b, 0)
                low_rest(4, use("E4"))
                low_rest(5, use("E5"))
                if keys:
                    norm_keys(b + 2, 0)
                if scores:
                    low_vals(b + 1, 1, 1 - par)
                low_rest(6, use("E6"))
                if keys:
                    norm_keys(b + 2, 1)
                    low_keys(b + 2, 0)
                    low_keys(b + 2, 1)
                low_rest(7, use("E7"))

            batch(0, 0, Slots.FIRST)
            with pool.Fori(0, (B - 4) // 2) as i:
                batch(2 * i + 1, 1)
                batch(2 * i + 2, 0)
            batch(B - 3, 1, Slots.NO_CONTEXT)
            batch(B - 2, 0, Slots.NO_KEYS)
            batch(B - 1, 1, Slots.LAST)
            add_parts(B - 1, 1)

        @block.vector
        def _(dve):
            for t in zeros:
                dve.memset(t, 0.0).then_inc(zeroed, 1)
            dve.wait_ge(zeroed, len(zeros))
            for t in ones:
                dve.memset(t, 1.0).then_inc(zeroed, 1)

            def ev_k(u, use):
                ps = slot[1]
                dve.wait_ge(slot_full[1], use[1] + 1)
                whole = HALF if u == 0 else HALF - 1
                ins = dve.tensor_tensor(kk[:, HALF * u:HALF * u + whole, :],
                                        ps[:, 0:whole * D].rearrange("p (t f) -> p t f", f=D),
                                        bk[:].unsqueeze(1).broadcast_to([128, whole, D]), ALU.add)
                if u == 1:
                    rows = DROW + DCA
                    ins = dve.tensor_tensor(kk[0:rows, KT - 1, :], ps[0:rows, whole * D:(whole + 1) * D], bk_last[0:rows], ALU.add)
                ins.then_inc(slot_free[1], 1)

            def sums(n, u):
                dve.wait_ge(sq_done, 2 * n + u + 1)
                dve.tensor_reduce(newt[:, u * HALF * H:(u + 1) * HALF * H],
                                  sq[:].rearrange("p t (h d) -> p (t h) d", d=HD), AX.X, ALU.add).then_inc(ss_done, 1)

            def variances(n):
                dve.wait_ge(ss_done, 2 * n + 2)
                dve.tensor_scalar(var[:], newt[:], 1.0 / HD, EPS_ATTN, ALU.mult, ALU.add).then_inc(var_ready, 1)

            def newton_step(n):
                dve.wait_ge(r0_ready, n + 1)
                dve.wait_ge(var_ready, n + 1)
                dve.tensor_tensor(newt[:], rstd[:], rstd[:], ALU.mult).then_inc(newton, 1)
                dve.wait_ge(newton, 3 * n + 1)
                dve.scalar_tensor_tensor(out=newt[:], in0=newt[:], scalar=-0.5, in1=var[:],
                                         op0=ALU.mult, op1=ALU.mult).then_inc(newton, 1)
                dve.wait_ge(newton, 3 * n + 2)
                dve.scalar_tensor_tensor(out=rstd[:], in0=newt[:], scalar=1.5, in1=rstd[:],
                                         op0=ALU.add, op1=ALU.mult).then_inc(newton, 1)

            def maxima(n, j, use):
                ps, half, jj = slot[1], j // 4, j % 4
                dve.wait_ge(slot_full[1], use[1] + 1)
                dve.tensor_reduce(m_in[half][0:PR, jj:jj + 1], ps[0:PR, 0:MAIN], AX.X, ALU.max, negate=True).then_inc(max_done, 1)
                dve.tensor_reduce(m_in[half][0:PR, 4 + jj:5 + jj], ps[0:PR, DCOL:KW], AX.X, ALU.max, negate=True).then_inc(slot_free[1], 1)
                if jj == 3:
                    dve.wait_ge(slot_free[1], use[1] + 1)
                    dve.tensor_copy(m_in[half][0:PR, 32:40], m_in[half][0:PR, 0:8]).then_inc(m_ready, 1)

            def max_rows(n, half, use):
                ps, rows = slot[1], m_rows[half]
                dve.wait_ge(slot_full[1], use[1] + 1)
                dve.tensor_copy(rows[:], ps[:, 0:PR]).then_inc(m_chain, 1)
                dve.wait_ge(m_chain, 2 * n + half + 1)
                dve.tensor_tensor(rows[32:40], ps[32:40, 0:PR], rows[32:40], ALU.subtract).then_inc(slot_free[1], 1)

            def low(j, use):
                dve.wait_ge(slot_free[0], use[1] + 1)
                hi = pt[j % 4][:].bitcast(BF16)[:, 1::2]
                dve.tensor_tensor(pt_lo[j % 4][:, 0:LO], pt[j % 4][:, 0:LO], hi[:, 0:LO], ALU.subtract).then_inc(lo_done, 1)

            def output(b, g):
                at, pairs = slice(g * 128, (g + 1) * 128), slice(4 * g, 4 * g + 4)
                dve.wait_ge(pv_done[g], b + 1)
                dve.reciprocal(rtotal[g][0:PR], acc[0:PR, pairs, 32:99:66]).then_inc(o_chain[g], 1)
                dve.wait_ge(o_chain[g], 5 * b + 1)
                dve.tensor_tensor(coef[g][0:PR], rtotal[g][0:PR].unsqueeze(3).broadcast_to([PR, 4, 2, 2]),
                                  pair_out[0:PR].unsqueeze(1).unsqueeze(1).broadcast_to([PR, 4, 2, 2]), ALU.mult).then_inc(o_chain[g], 1)
                dve.wait_ge(o_chain[g], 5 * b + 2)
                for part, (c0, k) in enumerate(((0, 0), (33, 0), (66, 1))):
                    dve.tensor_tensor(o[part][0:PR, at].rearrange("p (j i d) -> p j i d", i=2, d=HD),
                                      acc[0:PR, pairs, c0:c0 + 32].rearrange("p j (i d) -> p j i d", d=HD),
                                      coef[g][0:PR, :, k, :].unsqueeze(3).broadcast_to([PR, 4, 2, HD]), ALU.mult).then_inc(o_chain[g], 1)

            use = Slots.prologue
            ev_k(0, use("K0"))
            ev_k(1, use("K1"))
            sums(0, 0)
            sums(0, 1)
            variances(0)
            newton_step(0)
            ev_k(0, use("K0'"))
            ev_k(1, use("K1'"))
            sums(1, 0)
            sums(1, 1)
            variances(1)
            newton_step(1)
            for j in range(PAIRS):
                maxima(0, j, use(f"S{j}"))
                if j == 3:
                    max_rows(0, 0, use("M0"))

            def batch(b, par, kind=Slots.FULL):
                def use(unit):
                    return Slots.body(unit, b, kind)
                keys, scores = kind < Slots.NO_KEYS, kind < Slots.LAST
                if keys:
                    ev_k(0, use("K0"))
                max_rows(b, 1, use("M1"))
                low(0, use("E0"))
                if keys:
                    ev_k(1, use("K1"))
                if kind != Slots.FIRST:
                    output(b - 1, 1)
                low(1, use("E1"))
                if keys:
                    sums(b + 2, 0)
                low(2, use("E2"))
                if scores:
                    maxima(b + 1, 0, use("S0"))
                    maxima(b + 1, 1, use("S1"))
                low(3, use("E3"))
                if scores:
                    maxima(b + 1, 2, use("S2"))
                if keys:
                    sums(b + 2, 1)
                    variances(b + 2)
                low(4, use("E4"))
                output(b, 0)
                if keys:
                    newton_step(b + 2)
                if scores:
                    maxima(b + 1, 3, use("S3"))
                low(5, use("E5"))
                if scores:
                    max_rows(b + 1, 0, use("M0"))
                low(6, use("E6"))
                if scores:
                    maxima(b + 1, 4, use("S4"))
                    maxima(b + 1, 5, use("S5"))
                    maxima(b + 1, 6, use("S6"))
                    maxima(b + 1, 7, use("S7"))
                low(7, use("E7"))

            batch(0, 0, Slots.FIRST)
            with dve.Fori(0, (B - 4) // 2) as i:
                batch(2 * i + 1, 1)
                batch(2 * i + 2, 0)
            batch(B - 3, 1, Slots.NO_CONTEXT)
            batch(B - 2, 0, Slots.NO_KEYS)
            batch(B - 1, 1, Slots.LAST)
            output(B - 1, 1)


def feed_forward(env):
    nc = env.nc
    with ExitStack() as ctx:
        def sb(name, shape, dt=F32):
            return ctx.enter_context(nc.sbuf_tensor(name, shape, dt))
        sh = FfnShared(sb, ctx.enter_context(nc.semaphore("group_loaded0")), ctx.enter_context(nc.semaphore("group_loaded1")))
        env.x = sb("x_tokens", [128, NT, D])
        shared_expert(env, sh)
        routed_experts(env, sh)


class FfnShared:

    def __init__(self, sb, loaded0, loaded1):
        self.h_hi = sb("h_hi", [128, NT, D], BF16)
        self.h_lo = sb("h_lo", [128, NT, D], BF16)
        self.place = sb("place", [128, NT, E])
        self.w_hi = sb("w_hi", [128, NT, E], BF16)
        self.w_lo = sb("w_lo", [128, NT, E], BF16)
        self.iota = sb("iota", [128, E])
        self.w_up = [sb(f"w_up{i}", [128, 2, 4, 2 * F]) for i in range(2)]
        self.w_down = [sb(f"w_down{i}", [FH, 2, 4, D]) for i in range(2)]
        self.loaded = [loaded0, loaded1]

    def load(self, sp, a, q, par):
        for c in range(2):
            for k, name in enumerate(("Wg", "Wu")):
                sp.dma_start(self.w_up[par][:, c, :, k * F:(k + 1) * F],
                             a[name][bass.ds(q * 4, 4), c * 128:(c + 1) * 128, :].rearrange("e k f -> k e f")
                             if not isinstance(q, int) else
                             a[name][q * 4:q * 4 + 4, c * 128:(c + 1) * 128, :].rearrange("e k f -> k e f")
                             ).then_inc(self.loaded[par], 16)
            sp.dma_start(self.w_down[par][:, c],
                         a["Wd"][bass.ds(q * 4, 4), c * FH:(c + 1) * FH, :].rearrange("e f n -> f e n")
                         if not isinstance(q, int) else
                         a["Wd"][q * 4:q * 4 + 4, c * FH:(c + 1) * FH, :].rearrange("e f n -> f e n")
                         ).then_inc(self.loaded[par], 16)


LOADS = 6 * 16


def shared_expert(env, sh):
    nc, a = env.nc, env.a
    with ExitStack() as ctx:
        def sb(name, shape, dt=F32):
            return ctx.enter_context(nc.sbuf_tensor("s_" + name, shape, dt))

        def sem(name):
            return ctx.enter_context(nc.semaphore("s_" + name))

        x, ident = env.x, env.ident
        sq = env.ctxT[:].rearrange("p g t -> p (g t)").rearrange("p (n d) -> p n d", d=D)
        h = sb("h", [128, NT, D])
        wo = sb("wo", [128, G, D])
        bo = sb("bo", [128, D])
        hT = sb("hT", [128, 2, T])
        w_route = sb("w_route", [128, 2, E + 1])
        w_sup = sb("w_sup", [128, 2, 2, FS])
        w_sdown = sb("w_sdown", [128, FC, D])
        mean_x = sb("mean_x", [128, NT])
        var, lnv, rstd, tmp = (sb(n, [128, NT]) for n in ("var", "lnv", "rstd", "tmp"))
        logits = sb("logits", [128, NT, E + 1])
        top = sb("top", [128, NT, 8])
        top_at = sb("top_at", [128, NT, 8], U32)
        top_atf = sb("top_atf", [128, NT, 4])
        wtop = sb("wtop", [128, NT, 4])
        wsum = sb("wsum", [128, NT])
        onehot = sb("onehot", [128, NT, 4, E])
        sel = sb("sel", [128, NT, E])
        sel_b = sb("sel_b", [128, NT, E], BF16)
        w_tok = sb("w_tok", [128, NT, E])
        before = sb("before", [128, 128])
        before_b = sb("before_b", [128, 128], BF16)
        ones_b = sb("ones_b", [128, 128], BF16)
        sig = sb("sig", [128, NT])
        en = [sb(f"en{i}", [128, 512]) for i in range(2)]
        act_g = [sb(f"act_g{i}", [128, 512]) for i in range(2)]
        gu = [sb(f"gu{i}", [128, FC, 512]) for i in range(2)]
        wide = ctx.enter_context(nc.psum_tensor("wide", [128, 2048], F32))
        rest = ctx.enter_context(nc.psum_tensor("rest", [128, 2048], F32))

        loaded = sem("loaded")
        chain_done = sem("chain_done")
        x_loaded = sem("x_loaded")
        proj_done = sem("proj_done")
        bias_added = sem("bias_added")
        x1_ready = sem("x1_ready")
        centred = sem("centred")
        squared = sem("squared")
        var_done = sem("var_done")
        act_chain = sem("act_chain")
        r0_done = sem("r0_done")
        h_ready = sem("h_ready")
        turned = sem("turned")
        hT_ready = sem("hT_ready")
        routed = sem("routed")
        logits_ready = sem("logits_ready")
        top_ready = sem("top_ready")
        exp_done = sem("exp_done")
        sel_ready = sem("sel_ready")
        counted = sem("counted")
        place_ready = sem("place_ready")
        up_done = sem("up_done")
        en_done = sem("en_done")
        gu_done = sem("gu_done")
        down_done = sem("down_done")
        added = sem("added")

        block = ctx.enter_context(nc.Block())
        GROUPS = [(n, min(n + 4, NT)) for n in range(0, NT, 4)]
        STEPS = [(tg, f) for tg in range(len(GROUPS)) for f in range(FC)]

        def rows_of(f):
            return min(128, FS - f * 128)

        @block.sync
        def _(sp):
            for dst, src in (
                (wo[:], a["Wo"].rearrange("(c k) n -> k c n", k=128)),
                (x[:], a["x"].rearrange("b s d -> (b s) d").rearrange("(n p) d -> p n d", p=128)),
                (bo[:], a["bo_rows"]),
            ):
                sp.dma_start(dst, src).then_inc(x_loaded, 16)
            for dst, src in (
                (w_route[:], a["Wroute"].rearrange("(c k) e -> k c e", k=128)),
                (before[:], a["before"]),
                (sh.iota[:], a["iota"]),
                (w_sup[:, :, 0, :], a["Wsg"].rearrange("(c k) f -> k c f", k=128)),
                (w_sup[:, :, 1, :], a["Wsu"].rearrange("(c k) f -> k c f", k=128)),
                (w_sdown[:, 0:FC - 1, :], a["Wsd"][0:(FC - 1) * 128].rearrange("(c k) n -> k c n", k=128)),
                (w_sdown[0:rows_of(FC - 1), FC - 1, :], a["Wsd"][(FC - 1) * 128:FS]),
            ):
                sp.dma_start(dst, src).then_inc(loaded, 16)
            sh.load(sp, a, 0, 0)
            sh.load(sp, a, 1, 1)

        @block.gpsimd
        def _(pool):
            pool.wait_ge(x_loaded, 3 * 16)
            pool.tensor_tensor(x[:], x[:], bo[:].unsqueeze(1).broadcast_to([128, NT, D]), ALU.add).then_inc(bias_added, 1)
            pool.wait_ge(h_ready, 2)
            pool.tensor_tensor(sh.h_lo[:], h[:], sh.h_hi[:], ALU.subtract).then_inc(h_ready, 1)

        @block.tensor
        def _(pe):
            pe.wait_ge(x_loaded, 3 * 16)
            for n in range(NT):
                o = (wide if n < 8 else rest)[:, (n % 8) * D:(n % 8 + 1) * D]
                for c in range(2):
                    m = pe.matmul(o, env.ctxT[:, c, n * 128:(n + 1) * 128], wo[:, c], start=(c == 0), stop=(c == 1))
                if n in (7, NT - 1):
                    m.then_inc(proj_done, 1)
            pe.wait_ge(h_ready, 1)
            for k in range(2 * NT):
                c, n = k // NT, k % NT
                o = (wide if k < 16 else rest)[:, (k % 16) * 128:(k % 16 + 1) * 128]
                m = pe.transpose(o, h[:, n, c * 128:(c + 1) * 128], ident[:])
                if k in (15, 2 * NT - 1):
                    m.then_inc(turned, 1)
            pe.wait_ge(hT_ready, 2)
            pe.wait_ge(loaded, 7 * 16)
            for n in range(NT):
                for c in range(2):
                    m = pe.matmul(rest[:, 1536 + n * (E + 1):1536 + (n + 1) * (E + 1)], hT[:, c, n * 128:(n + 1) * 128],
                                  w_route[:, c], start=(c == 0), stop=(c == 1))
            m.then_inc(routed, 1)

            def up(s):
                tg, f = STEPS[s]
                n0, n1 = GROUPS[tg]
                if s >= 2:
                    pe.wait_ge(gu_done, s - 1)
                r, w = rows_of(f), (n1 - n0) * 128
                for k in range(2):
                    for c in range(2):
                        m = pe.matmul(rest[0:r, (2 * (s % 2) + k) * 512:(2 * (s % 2) + k) * 512 + w],
                                      w_sup[:, c, k, f * 128:f * 128 + r], hT[:, c, n0 * 128:n1 * 128],
                                      start=(c == 0), stop=(c == 1))
                m.then_inc(up_done, 1)

            def down(tg):
                pe.wait_ge(gu_done, FC * (tg + 1))
                n0, n1 = GROUPS[tg]
                for n in range(n0, n1):
                    if n >= 4:
                        pe.wait_ge(added, n - 3)
                    for f in range(FC):
                        r = rows_of(f)
                        m = pe.matmul(wide[:, (n % 4) * 512:(n % 4) * 512 + D], gu[tg % 2][0:r, f, (n - n0) * 128:(n - n0 + 1) * 128],
                                      w_sdown[0:r, f], start=(f == 0), stop=(f == FC - 1))
                    m.then_inc(down_done, 1)

            pe.wait_ge(logits_ready, 1)
            pe.wait_ge(sel_ready, 1)
            for n in range(NT):
                o = wide[:, n * E:(n + 1) * E]
                for m_ in range(n):
                    pe.matmul(o, ones_b[:], sel_b[:, m_], start=(m_ == 0), stop=False)
                m = pe.matmul(o, before_b[:], sel_b[:, n], start=(n == 0), stop=True)
            m.then_inc(counted, 1)
            for tg in range(len(GROUPS)):
                for f in range(FC):
                    up(FC * tg + f)
                if tg == 0:
                    pe.wait_ge(place_ready, 1)
                if tg:
                    down(tg - 1)
            down(len(GROUPS) - 1)

        @block.scalar
        def _(act):
            act.preload_act_table_set("natural_log_exp_and_others")
            act.wait_ge(centred, 1)
            act.activation(sq, h[:], ACT.Square).then_inc(squared, 1)
            act.wait_ge(var_done, 1)
            act.activation(lnv[:], var[:], ACT.Ln).then_inc(act_chain, 1)
            act.wait_ge(act_chain, 1)
            act.activation(rstd[:], lnv[:], ACT.Exp, scale=-0.5).then_inc(r0_done, 1)
            flat = hT[:].rearrange("p c t -> p (c t)")
            for k, (src, w) in enumerate(((wide, 2048), (rest, 1536))):
                act.wait_ge(turned, k + 1)
                act.activation(flat[:, 2048 * k:2048 * k + w], src[:, 0:w], ACT.Copy).then_inc(hT_ready, 1)
            act.wait_ge(top_ready, 1)
            act.activation(wtop[:], wtop[:], ACT.Exp).then_inc(exp_done, 1)
            act.activation(sig[:], logits[:, :, E], ACT.Exp, scale=-1.0).then_inc(exp_done, 1)
            for s, (tg, f) in enumerate(STEPS):
                r, w = rows_of(f), (GROUPS[tg][1] - GROUPS[tg][0]) * 128
                act.wait_ge(up_done, s + 1)
                if s >= 2:
                    act.wait_ge(gu_done, s - 1)
                act.activation(en[s % 2][0:r, 0:w], rest[0:r, 1024 * (s % 2):1024 * (s % 2) + w], ACT.Exp,
                               scale=-1.0).then_inc(en_done, 1)

        @block.vector
        def _(dve):
            step = [0]

            def chain(ins):
                step[0] += 1
                ins.then_inc(chain_done, 1)
                dve.wait_ge(chain_done, step[0])

            dve.wait_ge(bias_added, 1)
            for k, (src, n0, n1) in enumerate(((wide, 0, 8), (rest, 8, NT))):
                dve.wait_ge(proj_done, k + 1)
                ins = dve.tensor_tensor(x[:, n0:n1], x[:, n0:n1], src[:, 0:(n1 - n0) * D].rearrange("p (n d) -> p n d", d=D), ALU.add)
                ins.then_inc(x1_ready, 1)
            dve.wait_ge(x1_ready, 2)
            chain(dve.tensor_reduce(mean_x[:], x[:], AX.X, ALU.add))
            dve.scalar_tensor_tensor(out=h[:], in0=mean_x[:].unsqueeze(2).broadcast_to([128, NT, D]), scalar=-1.0 / D,
                                     in1=x[:], op0=ALU.mult, op1=ALU.add).then_inc(centred, 1)
            dve.wait_ge(squared, 1)
            chain(dve.tensor_reduce(tmp[:], sq, AX.X, ALU.add))
            dve.tensor_scalar(var[:], tmp[:], 1.0 / D, EPS_LN, ALU.mult, ALU.add).then_inc(var_done, 1)
            dve.wait_ge(r0_done, 1)
            chain(dve.tensor_tensor(tmp[:], rstd[:], rstd[:], ALU.mult))
            chain(dve.scalar_tensor_tensor(out=tmp[:], in0=tmp[:], scalar=-0.5, in1=var[:], op0=ALU.mult, op1=ALU.mult))
            chain(dve.scalar_tensor_tensor(out=rstd[:], in0=tmp[:], scalar=1.5, in1=rstd[:], op0=ALU.add, op1=ALU.mult))
            dve.wait_ge(centred, 1)
            dve.tensor_tensor(h[:], h[:], rstd[:].unsqueeze(2).broadcast_to([128, NT, D]), ALU.mult).then_inc(h_ready, 1)
            dve.wait_ge(h_ready, 1)
            dve.tensor_copy(sh.h_hi[:], h[:]).then_inc(h_ready, 1)
            dve.wait_ge(loaded, 7 * 16)
            dve.tensor_copy(before_b[:], before[:])
            chain(dve.memset(ones_b[:], 1.0))

            dve.wait_ge(routed, 1)
            dve.tensor_copy(logits[:], rest[:, 1536:1536 + NT * (E + 1)].rearrange("p (n e) -> p n e", n=NT)).then_inc(logits_ready, 1)
            dve.wait_ge(logits_ready, 1)
            for n in range(NT):
                ins = dve.max(top[:, n], logits[:, n, 0:E])
            chain(ins)
            for n in range(NT):
                ins = dve.max_index(top_at[:, n], top[:, n], logits[:, n, 0:E])
            chain(ins)
            dve.tensor_copy(top_atf[:], top_at[:, :, 0:4]).then_inc(chain_done, 1)
            dve.tensor_tensor(wtop[:], top[:, :, 0:4], top[:, :, 0:1].broadcast_to([128, NT, 4]), ALU.subtract).then_inc(top_ready, 1)
            step[0] += 1
            dve.wait_ge(chain_done, step[0])
            chain(dve.tensor_tensor(onehot[:], sh.iota[:].unsqueeze(1).unsqueeze(1).broadcast_to([128, NT, 4, E]),
                                    top_atf[:].unsqueeze(3).broadcast_to([128, NT, 4, E]), ALU.is_equal))
            chain(dve.tensor_reduce(sel[:], onehot[:].rearrange("p n k e -> p n e k"), AX.X, ALU.add))
            dve.tensor_copy(sel_b[:], sel[:]).then_inc(sel_ready, 1)
            dve.wait_ge(exp_done, 1)
            chain(dve.tensor_reduce(wsum[:], wtop[:], AX.X, ALU.add))
            chain(dve.reciprocal(tmp[:], wsum[:]))
            chain(dve.tensor_tensor(wtop[:], wtop[:], tmp[:].unsqueeze(2).broadcast_to([128, NT, 4]), ALU.mult))
            chain(dve.tensor_tensor(onehot[:], onehot[:], wtop[:].unsqueeze(3).broadcast_to([128, NT, 4, E]), ALU.mult))
            chain(dve.tensor_reduce(w_tok[:], onehot[:].rearrange("p n k e -> p n e k"), AX.X, ALU.add))
            chain(dve.tensor_copy(sh.w_hi[:], w_tok[:]))
            dve.tensor_tensor(sh.w_lo[:], w_tok[:], sh.w_hi[:], ALU.subtract)
            dve.wait_ge(exp_done, 2)
            chain(dve.tensor_scalar(wsum[:], sig[:], 1.0, None, ALU.add))
            chain(dve.reciprocal(sig[:], wsum[:]))
            dve.wait_ge(counted, 1)
            dve.scalar_tensor_tensor(out=sh.place[:], in0=wide[:, 0:NT * E].rearrange("p (n e) -> p n e", e=E), scalar=1.0,
                                     in1=sel[:], op0=ALU.add, op1=ALU.mult).then_inc(place_ready, 1)

            def silu_up(s):
                tg, f = STEPS[s]
                r, w = rows_of(f), (GROUPS[tg][1] - GROUPS[tg][0]) * 128
                g_ps = rest[0:r, 1024 * (s % 2):1024 * (s % 2) + w]
                u_ps = rest[0:r, 1024 * (s % 2) + 512:1024 * (s % 2) + 512 + w]
                e, t = en[s % 2][0:r, 0:w], act_g[s % 2][0:r, 0:w]
                dve.wait_ge(en_done, s + 1)
                chain(dve.tensor_scalar(e, e, 1.0, None, ALU.add))
                chain(dve.reciprocal(t, e))
                chain(dve.tensor_tensor(t, g_ps, t, ALU.mult))
                if f == 0 and tg >= 2:
                    dve.wait_ge(down_done, GROUPS[tg - 2][1])
                dve.tensor_tensor(gu[tg % 2][0:r, f, 0:w], u_ps, t, ALU.mult).then_inc(gu_done, 1)

            def add_shared(tg):
                for n in range(*GROUPS[tg]):
                    dve.wait_ge(down_done, n + 1)
                    dve.scalar_tensor_tensor(out=x[:, n], in0=wide[:, (n % 4) * 512:(n % 4) * 512 + D], scalar=sig[:, n:n + 1],
                                             in1=x[:, n], op0=ALU.mult, op1=ALU.add).then_inc(added, 1)

            for tg in range(len(GROUPS)):
                for f in range(FC):
                    silu_up(FC * tg + f)
                if tg:
                    add_shared(tg - 1)
            add_shared(len(GROUPS) - 1)


def routed_experts(env, sh):
    nc, a = env.nc, env.a
    QN = E // 4
    with ExitStack() as ctx:
        def sb(name, shape, dt=F32):
            return ctx.enter_context(nc.sbuf_tensor("r_" + name, shape, dt))

        def sem(name):
            return ctx.enter_context(nc.semaphore("r_" + name))

        x, ident = env.x, env.ident
        slots = sb("slots", [128, NT, E * CAP], BF16)
        ident_b = sb("ident_b", [128, 128], BF16)
        iota1 = sb("iota1", [128, CAP])
        own = sb("own", [128, QN, E])
        w_all = sb("w_all", [128, QN, 2 * E])
        w_mine = sb("w_mine", [128, QN, 2, E])
        w_slot = sb("w_slot", [128, QN])
        xeT = sb("xeT", [128, 2, E * CAP])
        xg = [sb(f"xg{i}", [128, 2, 128]) for i in range(2)]
        en = sb("en", [128, F])
        t_g = sb("t_g", [128, F])
        gu = sb("gu", [128, F])
        guT = [sb(f"guT{i}", [FH, 2, 128]) for i in range(2)]
        ye = sb("ye", [128, D])
        ye_hi = sb("ye_hi", [128, QN, D], BF16)
        ye_lo = sb("ye_lo", [128, QN, D], BF16)
        slotsT = [sb(f"slotsT{i}", [128, QN, 128], BF16) for i in range(2)]
        gather = ctx.enter_context(nc.psum_tensor("gather", [128, 2, E * CAP], F32))
        up_ps = ctx.enter_context(nc.psum_tensor("up_ps", [128, 512], F32))
        turn_ps = ctx.enter_context(nc.psum_tensor("turn_ps", [128, 512], F32))
        down_ps = ctx.enter_context(nc.psum_tensor("down_ps", [128, 512], F32))
        w_ps_flat = ctx.enter_context(nc.psum_tensor("w_ps", [128, QN * 2 * E], F32))
        w_ps = w_ps_flat[:].rearrange("p (q k) -> p q k", q=QN)

        loaded = sem("loaded")
        chain_done = sem("chain_done")
        slots_ready = sem("slots_ready")
        gathered = sem("gathered")
        xeT_ready = sem("xeT_ready")
        w_slot_ready = sem("w_slot_ready")
        xg_ready = sem("xg_ready")
        up_done = sem("up_done")
        en_done = sem("en_done")
        gu_chain = sem("gu_chain")
        gu_ready = sem("gu_ready")
        turned = sem("turned")
        guT_ready = sem("guT_ready")
        down_done = sem("down_done")
        ye_chain = sem("ye_chain")
        ye_ready = sem("ye_ready")
        st_turned = sem("st_turned")
        st_ready = sem("st_ready")
        combined = sem("combined")
        out_ready = sem("out_ready")
        stored = sem("stored")

        block = ctx.enter_context(nc.Block())
        x_out = env.out.rearrange("b s d -> (b s) d").rearrange("(n p) d -> p n d", p=128)

        @block.sync
        def _(sp):
            sp.dma_start(own[:].rearrange("p q e -> p (q e)"), a["own"]).then_inc(loaded, 16)
            with sp.Fori(0, QN // 2 - 1) as i:
                for par in range(2):
                    sp.wait_ge(down_done, 2 * i + par + 1)
                    sh.load(sp, a, 2 * i + par + 2, par)
            for n in range(NT):
                sp.wait_ge(out_ready, n + 1)
                sp.dma_start(x_out[:, n], x[:, n]).then_inc(stored, 16)
            sp.wait_ge(stored, 16 * NT)

        @block.gpsimd
        def _(pool):
            pool.wait_ge(xeT_ready, 4)

            def fetch(q, par):
                src = xeT[:, :, q * 128:(q + 1) * 128] if isinstance(q, int) else xeT[:, :, bass.ds(q * 128, 128)]
                pool.tensor_copy(xg[par][:], src).then_inc(xg_ready, 1)

            fetch(0, 0)
            fetch(1, 1)
            with pool.Fori(0, QN // 2 - 1) as i:
                for par in range(2):
                    pool.wait_ge(up_done, 2 * i + par + 1)
                    fetch(2 * i + par + 2, par)

        @block.tensor
        def _(pe):
            for n in range(NT):
                pe.wait_ge(slots_ready, n + 1)
                for c in range(2):
                    for part, hp in enumerate((sh.h_hi, sh.h_lo)):
                        for k in range(2):
                            m = pe.matmul(gather[:, c, k * 512:(k + 1) * 512], hp[:, n, c * 128:(c + 1) * 128],
                                          slots[:, n, k * 512:(k + 1) * 512], start=(n == 0 and part == 0),
                                          stop=(n == NT - 1 and part == 1))
                for q in range(QN):
                    for part, wp in enumerate((sh.w_hi, sh.w_lo)):
                        m = pe.matmul(w_ps[:, q, part * E:(part + 1) * E], slots[:, n, q * 128:(q + 1) * 128], wp[:, n],
                                      start=(n == 0 and q == 0 and part == 0), stop=(n == NT - 1), skip_group_check=True)
            m.then_inc(gathered, 1)

            def group(q, par, n_loads):
                pe.wait_ge(xg_ready, q + 1)
                pe.wait_ge(sh.loaded[par], n_loads)
                if not isinstance(q, int) or q > 0:
                    pe.wait_ge(gu_ready, q)
                for e in range(4):
                    for c in range(2):
                        m = pe.matmul(up_ps[32 * e:32 * e + 32, 0:2 * F], xg[par][:, c, 32 * e:32 * e + 32],
                                      sh.w_up[par][:, c, e], start=(c == 0), stop=(c == 1))
                m.then_inc(up_done, 1)
                pe.wait_ge(gu_ready, q + 1)
                for k in range(2):
                    m = pe.transpose(turn_ps[0:FH, k * 128:(k + 1) * 128], gu[:, k * FH:(k + 1) * FH], ident[:])
                m.then_inc(turned, 1)
                pe.wait_ge(guT_ready, q + 1)
                if not isinstance(q, int) or q > 0:
                    pe.wait_ge(ye_chain, 2 * q)
                for e in range(4):
                    for k in range(2):
                        m = pe.matmul(down_ps[32 * e:32 * e + 32, 0:D], guT[par][:, k, 32 * e:32 * e + 32],
                                      sh.w_down[par][:, k, e], start=(k == 0), stop=(k == 1))
                m.then_inc(down_done, 1)

            group(0, 0, LOADS)
            with pe.Fori(0, QN // 2 - 1) as i:
                group(2 * i + 1, 1, LOADS * i + LOADS)
                group(2 * i + 2, 0, LOADS * i + 2 * LOADS)
            group(QN - 1, 1, QN // 2 * LOADS)

            st = [turn_ps[:].bitcast(BF16), up_ps[:].bitcast(BF16)]
            out_ps = [down_ps, w_ps_flat]
            pe.wait_ge(ye_ready, QN)
            for n in range(NT + 1):
                if n < NT:
                    if n >= 2:
                        pe.wait_ge(st_ready, n - 1)
                    for q in range(QN):
                        m = pe.transpose(st[n % 2][:, q * 128:(q + 1) * 128], slots[:, n, q * 128:(q + 1) * 128], ident_b[:])
                    m.then_inc(st_turned, 1)
                if n >= 1:
                    k = n - 1
                    pe.wait_ge(st_ready, k + 1)
                    if k >= 2:
                        pe.wait_ge(out_ready, k - 1)
                    for q in range(QN):
                        for part, yp in enumerate((ye_hi, ye_lo)):
                            m = pe.matmul(out_ps[k % 2][:, 0:D], slotsT[k % 2][:, q], yp[:, q],
                                          start=(q == 0 and part == 0), stop=(q == QN - 1 and part == 1))
                    m.then_inc(combined, 1)

        @block.scalar
        def _(act):
            act.preload_act_table_set("natural_log_exp_and_others")
            act.wait_ge(gathered, 1)
            for c in range(2):
                for k in range(2):
                    act.activation(xeT[:, c, k * 512:(k + 1) * 512], gather[:, c, k * 512:(k + 1) * 512], ACT.Copy).then_inc(xeT_ready, 1)

            def group(q, par):
                act.wait_ge(up_done, q + 1)
                act.activation(en[:], up_ps[:, 0:F], ACT.Exp, scale=-1.0).then_inc(en_done, 1)
                act.wait_ge(turned, q + 1)
                act.activation(guT[par][:].rearrange("p k t -> p (k t)"), turn_ps[0:FH, 0:256], ACT.Copy).then_inc(guT_ready, 1)

            with act.Fori(0, QN // 2) as i:
                group(2 * i, 0)
                group(2 * i + 1, 1)
            st = [turn_ps[:].bitcast(BF16), up_ps[:].bitcast(BF16)]
            for n in range(NT):
                act.wait_ge(st_turned, n + 1)
                if n >= 2:
                    act.wait_ge(combined, n - 1)
                act.activation(slotsT[n % 2][:].rearrange("p q t -> p (q t)"), st[n % 2], ACT.Copy).then_inc(st_ready, 1)

        @block.vector
        def _(dve):
            step = [0]

            def chain(ins):
                step[0] += 1
                ins.then_inc(chain_done, 1)
                dve.wait_ge(chain_done, step[0])

            dve.tensor_copy(ident_b[:], ident[:])
            chain(dve.tensor_scalar(iota1[:], sh.iota[:, 0:CAP], 1.0, None, ALU.add))
            for n in range(NT):
                dve.tensor_tensor(slots[:, n].rearrange("p (e c) -> p e c", c=CAP),
                                  iota1[:].unsqueeze(1).broadcast_to([128, E, CAP]),
                                  sh.place[:, n].unsqueeze(2).broadcast_to([128, E, CAP]), ALU.is_equal).then_inc(slots_ready, 1)
            dve.wait_ge(gathered, 1)
            dve.wait_ge(loaded, 16)
            chain(dve.tensor_tensor(w_mine[:], w_ps.rearrange("p q (k e) -> p q k e", k=2),
                                    own[:].unsqueeze(2).broadcast_to([128, QN, 2, E]), ALU.mult))
            chain(dve.tensor_reduce(w_slot[:], w_mine[:].rearrange("p q k e -> p q (k e)"), AX.X, ALU.add))

            def group(q):
                dve.wait_ge(en_done, q + 1)
                dve.tensor_scalar(en[:], en[:], 1.0, None, ALU.add).then_inc(gu_chain, 1)
                dve.wait_ge(gu_chain, 3 * q + 1)
                dve.reciprocal(t_g[:], en[:]).then_inc(gu_chain, 1)
                dve.wait_ge(gu_chain, 3 * q + 2)
                dve.tensor_tensor(t_g[:], up_ps[:, 0:F], t_g[:], ALU.mult).then_inc(gu_chain, 1)
                dve.wait_ge(gu_chain, 3 * q + 3)
                dve.tensor_tensor(gu[:], up_ps[:, F:2 * F], t_g[:], ALU.mult).then_inc(gu_ready, 1)
                dve.wait_ge(down_done, q + 1)
                w = w_slot[:, q:q + 1] if isinstance(q, int) else w_slot[:, bass.ds(q, 1)]
                dve.tensor_tensor(ye[:], down_ps[:, 0:D], w.broadcast_to([128, D]), ALU.mult).then_inc(ye_chain, 1)
                dve.wait_ge(ye_chain, 2 * q + 1)

                def at(t):
                    return t[:, q] if isinstance(q, int) else t[:, bass.ds(q, 1)].rearrange("p o d -> p (o d)")
                dve.tensor_copy(at(ye_hi), ye[:]).then_inc(ye_chain, 1)
                dve.wait_ge(ye_chain, 2 * q + 2)
                dve.tensor_tensor(at(ye_lo), ye[:], at(ye_hi), ALU.subtract).then_inc(ye_ready, 1)

            with dve.Fori(0, QN // 2) as i:
                group(2 * i)
                group(2 * i + 1)
            out_ps = [down_ps, w_ps_flat]
            for n in range(NT):
                dve.wait_ge(combined, n + 1)
                dve.tensor_tensor(x[:, n], x[:, n], out_ps[n % 2][:, 0:D], ALU.add).then_inc(out_ready, 1)


def kernel(**inputs):
    import concourse.bacc as bacc
    from concourse.bass_utils import run_bass_kernel_spmd

    pre = "L0_xattn_"
    f = {k: np.ascontiguousarray(v) for k, v in inputs.items()}

    def rows(*names):
        return np.ascontiguousarray(np.broadcast_to(np.concatenate([f[pre + n] for n in names])[None], (128, sum(f[pre + n].size for n in names))))

    kv_bias = np.concatenate([f[pre + "bk"], f[pre + "bv"]]).reshape(H, 2, HD)
    dca_bias = f[pre + "bkv_dca"].reshape(2, D)
    arrays = {
        "x": f["x"], "ctx": f["ctx_1024"],
        "Wq": f[pre + "Wq"], "Wk": f[pre + "Wk"], "Wv": f[pre + "Wv"], "Wkv_dca": f[pre + "Wkv_dca"], "Wo": f[pre + "Wo"],
        "bq_rows": rows("bq"), "bo_rows": rows("bo"),
        "bk_rows": np.tile(kv_bias[:, 0].reshape(1, D), (128, 1)), "bk_dca_rows": np.tile(dca_bias[0:1], (128, 1)),
        "bv_cols": np.ascontiguousarray(np.stack([kv_bias[:, 1].reshape(G, 128), dca_bias[1].reshape(G, 128)]).transpose(2, 1, 0)),
        "ln_cols": np.ascontiguousarray(np.tile(np.stack([f[pre + n] for n in (
            "qn_w", "qn_b", "kn_w", "kn_b", "kn_dca_w", "kn_dca_b")], 1), (128 // HD, 1))),
        "ident": np.eye(128, dtype=np.float32),
        "fold": np.tile(np.eye(S1, dtype=np.float32), (2, 1)),
    }
    p = np.arange(128)
    arrays["before"] = (p[:, None] < p[None, :]).astype(np.float32)
    arrays["iota"] = np.tile(np.arange(E, dtype=np.float32), (128, 1))
    arrays["own"] = (4 * np.arange(E // 4)[None, :, None] + p[:, None, None] // CAP == np.arange(E)).astype(
        np.float32).reshape(128, -1)
    arrays["pair_masks"] = np.stack([p // HD % 2 == 0, p // HD % 2 == 1, p < S1, (p >= S1) & (p < PR)], 1).astype(np.float32)
    sel, jj = np.zeros((128, 4, 2, 128), np.float32), np.arange(4)
    for r in (0, 32):
        sel[r + jj, jj, 0, :] = 1
        sel[r + jj, jj, 1, 0:REST] = 1
        sel[r + 4 + jj, jj, 1, DROW:DROW + DCA] = 1
    arrays["sel"] = sel
    arrays["Wroute"] = np.concatenate([f["L0_ffn_Wr"], f["L0_ffn_Wse"]], 1)
    for n in ("Wg", "Wu", "Wd", "Wsg", "Wsu", "Wsd"):
        arrays[n] = f["L0_ffn_" + n]

    nc = bacc.Bacc("TRN2", target_bir_lowering=False, num_devices=1)
    aps, feed = {}, {}
    for name, arr in arrays.items():
        feed[f"in_{name}_dram"] = arr
        aps[name] = nc.dram_tensor(f"in_{name}_dram", arr.shape, mybir.dt.from_np(arr.dtype), kind="ExternalInput").ap()
    out = nc.dram_tensor("out_0_dram", (B, S1, D), F32, kind="ExternalOutput").ap()
    program(nc, aps, out)
    r = run_bass_kernel_spmd(nc, [feed], core_ids=[0])
    return r.results[0]["out_0_dram"]
```
